# Optimizing a Trainium2 kernel written in Bass

```python
import numpy as np
import jax
import jax.numpy as jnp

def _softmax(x, axis=-1):
    return jax.nn.softmax(x, axis=axis)

def _gelu(x):
    return jax.nn.gelu(x, approximate=True)

def _silu(x):
    return jax.nn.silu(x)

def _sigmoid(x):
    return jax.nn.sigmoid(x)

def _layernorm(x, axis=-1, eps=1e-05):
    m = jnp.mean(x, axis=axis, keepdims=True)
    v = jnp.var(x, axis=axis, keepdims=True)
    return (x - m) / jnp.sqrt(v + eps)

def _scatter_add(tgt, idx, src, axis=0):
    return tgt.at[idx].add(src)

def _segment_sum(src, seg, n):
    return jax.ops.segment_sum(src, seg, n)
kernel_name = 'mk_conv_preact_d2_conv_nchw384_r2_e15f68'

def setup_inputs(seed: int=0):
    np.random.seed(seed)
    _w = jnp.asarray

    def _rec_inputs():
        import jax
        import jax.numpy as jnp
        _gk = jax.random.key(seed)
        x = -0.0001538 + 1 * jax.random.normal(jax.random.fold_in(_gk, 1), (16, 192, 32, 32), jnp.float32)
        return x
    x = _rec_inputs()

    def _L0_conv_setup():
        import jax, jax.numpy as jnp
        import numpy as np
        D_MODEL = 192
        D_STATE = 32
        D_CONV = 3
        EXPAND = 2
        HEADDIM = 32
        NGROUPS = 1
        CHUNK = 128
        D_INNER = EXPAND * D_MODEL
        NHEADS = D_INNER // HEADDIM
        CONV_DIM = D_INNER + 2 * NGROUPS * D_STATE
        D_IN_PROJ = 2 * D_INNER + 2 * NGROUPS * D_STATE + NHEADS
        EPS = 1e-05

        def _chunk_scan(x, dt, A, Bm, Cm):
            b, l, h, p = x.shape
            nc = l // CHUNK
            xc = x.reshape(b, nc, CHUNK, h, p)
            dtc = dt.reshape(b, nc, CHUNK, h)
            hpg = h // NGROUPS
            Bh = jnp.repeat(Bm.reshape(b, nc, CHUNK, NGROUPS, D_STATE), hpg, axis=3)
            Ch = jnp.repeat(Cm.reshape(b, nc, CHUNK, NGROUPS, D_STATE), hpg, axis=3)
            dA = dtc * A
            dA_cs = jnp.cumsum(dA, axis=2)
            Lmat = jnp.exp(dA_cs[:, :, :, None, :] - dA_cs[:, :, None, :, :])
            causal = jnp.tril(jnp.ones((CHUNK, CHUNK), bool))
            att = jnp.einsum('bcihn,bcjhn->bcijh', Ch, Bh) * Lmat * dtc[:, :, None, :, :]
            att = jnp.where(causal[None, None, :, :, None], att, 0.0)
            y_intra = jnp.einsum('bcijh,bcjhp->bcihp', att, xc)
            decay_to_end = jnp.exp(dA_cs[:, :, -1:, :] - dA_cs)
            states = jnp.einsum('bcjhn,bcjh,bcjhp->bchpn', Bh, decay_to_end * dtc, xc)
            chunk_decay = jnp.exp(dA_cs[:, :, -1, :])

            def step(carry, inp):
                st, dec = inp
                new = carry * dec[:, :, None, None] + st
                return (new, carry)
            init = jnp.zeros((b, h, p, D_STATE), x.dtype)
            _, prevs = jax.lax.scan(step, init, (jnp.moveaxis(states, 1, 0), jnp.moveaxis(chunk_decay, 1, 0)))
            prev_states = jnp.moveaxis(prevs, 0, 1)
            y_inter = jnp.einsum('bcihn,bcih,bchpn->bcihp', Ch, jnp.exp(dA_cs), prev_states)
            return (y_intra + y_inter).reshape(b, l, h, p)
        key = jax.random.key(seed)
        ks = jax.random.split(key, 8)
        B, H, W = (16, 32, 32)
        u = jax.random.normal(ks[0], (B, D_MODEL, H, W), jnp.float32)
        in_proj_w = jax.random.normal(ks[1], (D_IN_PROJ, D_MODEL), jnp.float32) / np.sqrt(D_MODEL)
        conv_w = jax.random.normal(ks[2], (CONV_DIM, 1, D_CONV, D_CONV), jnp.float32) / np.sqrt(D_CONV * D_CONV)
        conv_b = jax.random.normal(ks[3], (CONV_DIM,), jnp.float32) * 0.01
        dt = jnp.exp(jax.random.uniform(ks[4], (NHEADS,)) * (np.log(0.1) - np.log(0.001)) + np.log(0.001))
        dt = jnp.clip(dt, 0.0001, None)
        dt_bias = dt + jnp.log(-jnp.expm1(-dt))
        A_log = jnp.log(jax.random.uniform(ks[5], (NHEADS,), minval=1.0, maxval=16.0))
        D = jnp.ones((NHEADS,), jnp.float32)
        norm_w = jnp.ones((D_INNER,), jnp.float32)
        norm_b = jnp.zeros((D_INNER,), jnp.float32)
        out_proj_w = jax.random.normal(ks[6], (D_MODEL, D_INNER), jnp.float32) / np.sqrt(D_INNER)
        return {'u': u, 'in_proj_w': in_proj_w, 'conv_w': conv_w, 'conv_b': conv_b, 'dt_bias': dt_bias, 'A_log': A_log, 'D': D, 'norm_w': norm_w, 'norm_b': norm_b, 'out_proj_w': out_proj_w}
    _L0_conv_all = _L0_conv_setup()
    _L0_conv_in = {k: v for k, v in _L0_conv_all.items() if k in ('in_proj_w', 'conv_w', 'conv_b', 'dt_bias', 'A_log', 'D', 'norm_w', 'norm_b', 'out_proj_w')}
    del _L0_conv_all

    def _L1_conv_setup():
        import jax, jax.numpy as jnp
        import numpy as np
        DIM = 192
        D_STATE = 16

        def _selective_scan(x_in, delta, A, Bm, Cm, D):
            Bsz, L, dim = x_in.shape
            n = A.shape[1]

            def step(h, inp):
                d_t, x_t, b_t, c_t = inp
                h = jnp.exp(d_t[..., None] * A) * h + (d_t * x_t)[..., None] * b_t[:, None, :]
                y_t = jnp.einsum('bdn,bn->bd', h, c_t)
                return (h, y_t)
            h0 = jnp.zeros((Bsz, dim, n), dtype=x_in.dtype)
            xs = (jnp.swapaxes(delta, 0, 1), jnp.swapaxes(x_in, 0, 1), jnp.swapaxes(Bm, 0, 1), jnp.swapaxes(Cm, 0, 1))
            _, ys = jax.lax.scan(step, h0, xs)
            y = jnp.swapaxes(ys, 0, 1)
            return y + x_in * D
        key = jax.random.key(seed)
        ks = jax.random.split(key, 8)
        B, C, H, W = (4, DIM, 32, 32)
        x = jax.random.normal(ks[0], (B, C, H, W), dtype=jnp.float32)
        P = 2 * DIM + 2 * D_STATE
        W_proj = jax.random.normal(ks[1], (P, DIM), dtype=jnp.float32) * 0.02
        b_proj = jnp.zeros((P,), dtype=jnp.float32)
        A_log = jnp.log(jax.random.uniform(ks[2], (DIM, D_STATE), dtype=jnp.float32) + 0.0001)
        D = jnp.ones((DIM,), dtype=jnp.float32)
        dt_bias = jnp.zeros((DIM,), dtype=jnp.float32)
        W_out = jax.random.normal(ks[3], (DIM, DIM), dtype=jnp.float32) * 0.02
        b_out = jnp.zeros((DIM,), dtype=jnp.float32)
        return {'x': x, 'W_proj': W_proj, 'b_proj': b_proj, 'A_log': A_log, 'D': D, 'dt_bias': dt_bias, 'W_out': W_out, 'b_out': b_out}
    _L1_conv_all = _L1_conv_setup()
    _L1_conv_in = {k: v for k, v in _L1_conv_all.items() if k in ('W_proj', 'b_proj', 'A_log', 'D', 'dt_bias', 'W_out', 'b_out')}
    del _L1_conv_all
    return {'x': x, 'L0_conv_in_proj_w': _L0_conv_in['in_proj_w'], 'L0_conv_conv_w': _L0_conv_in['conv_w'], 'L0_conv_conv_b': _L0_conv_in['conv_b'], 'L0_conv_dt_bias': _L0_conv_in['dt_bias'], 'L0_conv_A_log': _L0_conv_in['A_log'], 'L0_conv_D': _L0_conv_in['D'], 'L0_conv_norm_w': _L0_conv_in['norm_w'], 'L0_conv_norm_b': _L0_conv_in['norm_b'], 'L0_conv_out_proj_w': _L0_conv_in['out_proj_w'], 'L1_conv_W_proj': _L1_conv_in['W_proj'], 'L1_conv_b_proj': _L1_conv_in['b_proj'], 'L1_conv_A_log': _L1_conv_in['A_log'], 'L1_conv_D': _L1_conv_in['D'], 'L1_conv_dt_bias': _L1_conv_in['dt_bias'], 'L1_conv_W_out': _L1_conv_in['W_out'], 'L1_conv_b_out': _L1_conv_in['b_out']}

def reference(x, L0_conv_in_proj_w, L0_conv_conv_w, L0_conv_conv_b, L0_conv_dt_bias, L0_conv_A_log, L0_conv_D, L0_conv_norm_w, L0_conv_norm_b, L0_conv_out_proj_w, L1_conv_W_proj, L1_conv_b_proj, L1_conv_A_log, L1_conv_D, L1_conv_dt_bias, L1_conv_W_out, L1_conv_b_out):
    import jax
    import jax.numpy as jnp

    def _L0_conv_ref(u, in_proj_w, conv_w, conv_b, dt_bias, A_log, D, norm_w, norm_b, out_proj_w):
        import jax, jax.numpy as jnp
        import numpy as np
        D_MODEL = 192
        D_STATE = 32
        D_CONV = 3
        EXPAND = 2
        HEADDIM = 32
        NGROUPS = 1
        CHUNK = 128
        D_INNER = EXPAND * D_MODEL
        NHEADS = D_INNER // HEADDIM
        CONV_DIM = D_INNER + 2 * NGROUPS * D_STATE
        D_IN_PROJ = 2 * D_INNER + 2 * NGROUPS * D_STATE + NHEADS
        EPS = 1e-05

        def _chunk_scan(x, dt, A, Bm, Cm):
            b, l, h, p = x.shape
            nc = l // CHUNK
            xc = x.reshape(b, nc, CHUNK, h, p)
            dtc = dt.reshape(b, nc, CHUNK, h)
            hpg = h // NGROUPS
            Bh = jnp.repeat(Bm.reshape(b, nc, CHUNK, NGROUPS, D_STATE), hpg, axis=3)
            Ch = jnp.repeat(Cm.reshape(b, nc, CHUNK, NGROUPS, D_STATE), hpg, axis=3)
            dA = dtc * A
            dA_cs = jnp.cumsum(dA, axis=2)
            Lmat = jnp.exp(dA_cs[:, :, :, None, :] - dA_cs[:, :, None, :, :])
            causal = jnp.tril(jnp.ones((CHUNK, CHUNK), bool))
            att = jnp.einsum('bcihn,bcjhn->bcijh', Ch, Bh) * Lmat * dtc[:, :, None, :, :]
            att = jnp.where(causal[None, None, :, :, None], att, 0.0)
            y_intra = jnp.einsum('bcijh,bcjhp->bcihp', att, xc)
            decay_to_end = jnp.exp(dA_cs[:, :, -1:, :] - dA_cs)
            states = jnp.einsum('bcjhn,bcjh,bcjhp->bchpn', Bh, decay_to_end * dtc, xc)
            chunk_decay = jnp.exp(dA_cs[:, :, -1, :])

            def step(carry, inp):
                st, dec = inp
                new = carry * dec[:, :, None, None] + st
                return (new, carry)
            init = jnp.zeros((b, h, p, D_STATE), x.dtype)
            _, prevs = jax.lax.scan(step, init, (jnp.moveaxis(states, 1, 0), jnp.moveaxis(chunk_decay, 1, 0)))
            prev_states = jnp.moveaxis(prevs, 0, 1)
            y_inter = jnp.einsum('bcihn,bcih,bchpn->bcihp', Ch, jnp.exp(dA_cs), prev_states)
            return (y_intra + y_inter).reshape(b, l, h, p)
        B, C, H, W = u.shape
        L = H * W
        useq = u.reshape(B, C, L).transpose(0, 2, 1)
        zxbcdt = useq @ in_proj_w.T
        z = zxbcdt[..., :D_INNER]
        xBC = zxbcdt[..., D_INNER:D_INNER + CONV_DIM]
        dt = jax.nn.softplus(zxbcdt[..., D_INNER + CONV_DIM:] + dt_bias)
        xBC = xBC.reshape(B, H, W, CONV_DIM)
        kern = jnp.transpose(conv_w, (2, 3, 1, 0))
        xBC = jax.lax.conv_general_dilated(xBC, kern, (1, 1), 'SAME', dimension_numbers=('NHWC', 'HWIO', 'NHWC'), feature_group_count=CONV_DIM) + conv_b
        xBC = jax.nn.silu(xBC).reshape(B, L, CONV_DIM)
        x = xBC[..., :D_INNER].reshape(B, L, NHEADS, HEADDIM)
        Bm = xBC[..., D_INNER:D_INNER + NGROUPS * D_STATE].reshape(B, L, NGROUPS, D_STATE)
        Cm = xBC[..., D_INNER + NGROUPS * D_STATE:].reshape(B, L, NGROUPS, D_STATE)
        A = -jnp.exp(A_log)
        y = _chunk_scan(x, dt, A, Bm, Cm) + D[None, None, :, None] * x
        y = y.reshape(B, L, D_INNER)
        mu = jnp.mean(y, axis=-1, keepdims=True)
        var = jnp.var(y, axis=-1, keepdims=True)
        y = (y - mu) / jnp.sqrt(var + EPS) * norm_w + norm_b
        y = y * z
        out = y @ out_proj_w.T
        return out.reshape(B, H, W, C).transpose(0, 3, 1, 2)

    def _L1_conv_ref(x, W_proj, b_proj, A_log, D, dt_bias, W_out, b_out):
        import jax, jax.numpy as jnp
        import numpy as np
        DIM = 192
        D_STATE = 16

        def _selective_scan(x_in, delta, A, Bm, Cm, D):
            Bsz, L, dim = x_in.shape
            n = A.shape[1]

            def step(h, inp):
                d_t, x_t, b_t, c_t = inp
                h = jnp.exp(d_t[..., None] * A) * h + (d_t * x_t)[..., None] * b_t[:, None, :]
                y_t = jnp.einsum('bdn,bn->bd', h, c_t)
                return (h, y_t)
            h0 = jnp.zeros((Bsz, dim, n), dtype=x_in.dtype)
            xs = (jnp.swapaxes(delta, 0, 1), jnp.swapaxes(x_in, 0, 1), jnp.swapaxes(Bm, 0, 1), jnp.swapaxes(Cm, 0, 1))
            _, ys = jax.lax.scan(step, h0, xs)
            y = jnp.swapaxes(ys, 0, 1)
            return y + x_in * D
        B, C, H, W = x.shape
        L = H * W
        seq = x.reshape(B, C, L).transpose(0, 2, 1)
        proj = seq @ W_proj.T + b_proj
        x_in = proj[..., :DIM]
        delta = proj[..., DIM:2 * DIM]
        Bm = proj[..., 2 * DIM:2 * DIM + D_STATE]
        Cm = proj[..., 2 * DIM + D_STATE:]
        A = -jnp.exp(A_log)
        delta = jax.nn.softplus(delta + dt_bias)
        y = _selective_scan(x_in, delta, A, Bm, Cm, D)
        out = y @ W_out.T + b_out
        return out.transpose(0, 2, 1).reshape(B, C, H, W)

    def _gn(v, G=32, eps=1e-05):
        B_, C_, H_, W_ = v.shape
        g = v.reshape(B_, G, C_ // G, H_, W_)
        m = jnp.mean(g, axis=(2, 3, 4), keepdims=True)
        s = jnp.var(g, axis=(2, 3, 4), keepdims=True)
        return ((g - m) / jnp.sqrt(s + eps)).reshape(v.shape)

    def _ln_c(v, eps=1e-06):
        m = jnp.mean(v, axis=1, keepdims=True)
        s = jnp.var(v, axis=1, keepdims=True)
        return (v - m) / jnp.sqrt(s + eps)

    def _ln_t(v, eps=1e-05):
        m = jnp.mean(v, axis=-1, keepdims=True)
        s = jnp.var(v, axis=-1, keepdims=True)
        return (v - m) / jnp.sqrt(s + eps)

    def _to_tokens(v):
        B_, C_, H_, W_ = v.shape
        return v.reshape(B_, C_, H_ * W_).transpose(0, 2, 1)

    def _from_tokens(t, like):
        B_, C_, H_, W_ = like.shape
        return t.transpose(0, 2, 1).reshape(B_, C_, H_, W_)
    x = x + _L0_conv_ref(_gn(x), L0_conv_in_proj_w, L0_conv_conv_w, L0_conv_conv_b, L0_conv_dt_bias, L0_conv_A_log, L0_conv_D, L0_conv_norm_w, L0_conv_norm_b, L0_conv_out_proj_w)
    x = x + _L1_conv_ref(_gn(x), L1_conv_W_proj, L1_conv_b_proj, L1_conv_A_log, L1_conv_D, L1_conv_dt_bias, L1_conv_W_out, L1_conv_b_out)
    return x

_drawn_inputs = setup_inputs


def setup_inputs(seed=0):
    import zlib

    import numpy as np

    out = dict(_drawn_inputs(seed))
    spreads = {'L0_conv_D': (1.0, 0.2),
     'L0_conv_norm_w': (1.0, 0.2),
     'L0_conv_norm_b': (0.0, 0.1),
     'L1_conv_b_proj': (0.0, 0.1),
     'L1_conv_D': (1.0, 0.6),
     'L1_conv_dt_bias': (0.0, 2.0),
     'L1_conv_b_out': (0.0, 0.1)}
    factors = {'L0_conv_conv_b': 6.929}
    for name, (base, spread) in spreads.items():
        noise = np.random.default_rng([zlib.crc32(name.encode()), seed]).standard_normal(out[name].shape)
        drawn = base * np.exp(spread * noise) if base else spread * noise
        out[name] = jnp.asarray(drawn.astype(out[name].dtype))
    for name, factor in factors.items():
        out[name] = (out[name] * factor).astype(out[name].dtype)
    return out
```

```python
from contextlib import ExitStack

import concourse.bass as bass
from concourse import mybir

ALU = mybir.AluOpType
ACT = mybir.ActivationFunctionType
F32 = mybir.dt.float32
BF16 = mybir.dt.bfloat16
AX_X = mybir.AxisListType.X

P = 128
B, C, H, W = 16, 192, 32, 32
L = H * W
Q = 128
NCH = L // Q
CB_ = C - P
GROUP = 6
NG = C // GROUP
GEPS = 1e-5
LEPS = 1e-5
DI = 384
NS = 32
NH = 12
HD = 32
XM = DI // P
CONVD = DI + 2 * NS
PROJ0 = 2 * DI + 2 * NS + NH
ZD = DI + NH
HPB = 4
NRB = NH // HPB
MASKED = -1e30
S1 = 16
PROJ1 = 2 * C + 2 * S1
DG = P // S1
NDG = C // DG
HALF = L // 2
CPH = HALF // Q
UNITS = 2 * NDG


class Signal:

    def __init__(self, sem, per_batch):
        self.sem, self.per_batch = sem, per_batch

    def at(self, b, k):
        return b * self.per_batch + k


def build(nc, x_d, inw_d, cw_d, cb_d, dtb_d, alog0_d, d0_d, nw_d, nb_d, outw_d,
          wp_d, bp_d, alog1_d, d1_d, dtb1_d, wo_d, bo_d, out_d):
    with ExitStack() as ctx:
        def sb(name, shape, dt=F32):
            return ctx.enter_context(nc.sbuf_tensor(name, shape, dt))

        def sem(name):
            return ctx.enter_context(nc.semaphore(name))

        def sig(name, per_batch):
            return Signal(sem(name), per_batch)

        bank = [ctx.enter_context(nc.psum_tensor(f"bank{i}", [P, 512], F32)) for i in range(8)]

        ident = sb("ident", [P, P])
        identb = sb("identb", [P, P], BF16)
        upper = sb("upper", [P, P])
        ones = sb("ones", [P, P])
        maskneg = sb("maskneg", [P, P], BF16)
        sel = sb("sel", [P, DG])
        ga = sb("ga", [P, 43 * GROUP])
        gb = sb("gb", [CB_, 43 * GROUP])
        neghalf = sb("neghalf", [P, 2])
        wt0a = sb("wt0a", [P, PROJ0])
        wt0b = sb("wt0b", [CB_, PROJ0])
        wo0 = sb("wo0", [P, XM, C])
        wt1a = sb("wt1a", [P, PROJ1])
        wt1b = sb("wt1b", [CB_ + 2, PROJ1])
        wo1a = sb("wo1a", [P, C])
        wo1b = sb("wo1b", [CB_, C])
        cw = sb("cw", [P, XM + 1, 9])
        cb = sb("cb", [P, XM + 1])
        dtb = sb("dtb", [P, NH])
        aneg0 = sb("aneg0", [P, NH])
        dcol = sb("dcol", [P, XM])
        diagd = sb("diagd", [P, XM, P])
        nwb = sb("nwb", [P, DI])
        nbb = sb("nbb", [P, DI])
        aneg1 = sb("aneg1", [P, NDG])
        d1b = sb("d1b", [P, C])
        boc = sb("boc", [P, 2])

        xa = sb("xa", [P, L])
        xb = sb("xb", [CB_, L])
        x1a = sb("x1a", [P, L])
        x1b = sb("x1b", [CB_, L])
        xna = sb("xna", [P, L])
        xnb = sb("xnb", [CB_ + 2, L])
        st = sb("st", [P, 2, 2, 6])
        mv = sb("mv", [P, 2, 2])
        spare = sb("spare", [P, 1])
        spare1 = sb("spare1", [P, 1])
        gm = sb("gm", [P, 2])
        gd = sb("gd", [P, 2])
        gq = sb("gq", [P, 2])
        gv = sb("gv", [P, 2])
        gr = sb("gr", [P, 2])
        cpad = [sb(f"cpad{m}", [P, H + 2, W + 2]) for m in range(XM)]
        bcpad = sb("bcpad", [P, H // 2 + 2, W + 2])
        xs = [sb(f"xs{m}", [P, L]) for m in range(XM)]
        bcacc = sb("bcacc", [P, HALF])
        bs = sb("bs", [NS, L])
        cs_ = sb("cs_", [NS, L])
        ztd = sb("ztd", [P, NCH, ZD])
        dtx = sb("dtx", [P, NCH, NH])
        dte = sb("dte", [P, NCH, NH])
        dtl = sb("dtl", [P, NCH, NH])
        dtu = sb("dtu", [P, NCH, NH])
        dt0 = sb("dt0", [P, NCH, NH])
        da0 = sb("da0", [P, NCH, NH])
        csum = sb("csum", [P, 2, NCH, NH])
        cexp = sb("cexp", [P, 2, NCH, NH])
        wend = sb("wend", [P, NCH, NH])
        xtok = sb("xtok", [P, 2, DI + NS])
        cbt = sb("cbt", [P, 2, Q])
        diff = sb("diff", [P, NH, Q])
        att = sb("att", [P, NH, Q])
        xdt = sb("xdt", [P, 2, DI])
        xw = sb("xw", [P, 2, DI])
        state = sb("state", [NS, DI])
        yint = sb("yint", [P, DI])
        y0 = sb("y0", [P, 2, DI])
        lst = sb("lst", [P, 2, 6])
        lmv = sb("lmv", [P, 2, 2])
        lve = sb("lve", [P, 2])
        lrs = sb("lrs", [P, 2])
        yw = sb("yw", [P, 2, DI])
        yz = sb("yz", [P, 2, DI])
        yzt = sb("yzt", [P, XM, L])
        p1 = sb("p1", [P, NCH, PROJ1])
        sp_e = diff[:, :, :].rearrange("p h q -> p (h q)").rearrange("p (c d) -> p c d", d=C)
        sp_l = att[:, :, :].rearrange("p h q -> p (h q)").rearrange("p (c d) -> p c d", d=C)
        sp_u = yzt[:, 0:2, :].rearrange("p m l -> p (m l)")[:, 0:NCH * C].rearrange("p (c d) -> p c d", d=C)
        delta = sb("delta", [P, NCH, C])
        u1 = sb("u1", [P, NCH, C])
        crep = sb("crep", [P, L])
        ctok = sb("ctok", [P, NCH, S1, DG])
        dtok = sb("dtok", [P, 2, CPH, S1, DG])
        wtok = sb("wtok", [P, 2, CPH, S1, DG])
        decay = sb("decay", [P, 2, HALF])
        hst = sb("hst", [P, 3, HALF])
        carry = sb("carry", [P, NDG])
        hc = sb("hc", [P, 2, HALF])
        y1 = sp_l
        y1ta = yzt[:, 2, :]
        y1tb = yzt[0:CB_, 1, :]

        s_const = sem("constants_made")
        s_pool = sem("pool_constants")
        s_wload = sem("weights_loaded")
        s_wps = sem("weight_transposed")
        s_wev = sem("weight_copied")
        s_prep = sem("weights_prepared")
        x_loaded = sig("x_loaded", 32)
        x1_ready = sig("x1_ready", 4)
        out_ready = sig("out_ready", 4)
        x1_free = sig("x1_free", 32)
        stats_ready = sig("stats_ready", 4)
        gmean_ps = sig("gmean_ps", 2)
        gdev_ready = sig("gdev_ready", 2)
        gvar_ps = sig("gvar_ps", 2)
        gve_ready = sig("gve_ready", 2)
        grstd_ready = sig("grstd_ready", 2)
        xn_ready = sig("xn_ready", 4)
        conv_ps = sig("conv_ps", 8)
        conv_in = sig("conv_in", 9)
        z_ps = sig("z_ps", NCH)
        z_copied = sig("z_copied", NCH)
        conv_done = sig("conv_done", XM + 1)
        silu_done = sig("silu_done", XM + 4)
        dtx_ready = sig("dtx_ready", 1)
        dte_ready = sig("dte_ready", 1)
        dtl_ready = sig("dtl_ready", 1)
        da_ready = sig("da_ready", 1)
        cs_ps = sig("cs_ps", 1)
        csum_ready = sig("csum_ready", 1)
        wdiff_ready = sig("wdiff_ready", 1)
        cexp_ready = sig("cexp_ready", 1)
        wexp_ready = sig("wexp_ready", 1)
        wend_ready = sig("wend_ready", 1)
        xt_ps = sig("xt_ps", NCH)
        xt_copied = sig("xt_copied", NCH)
        cbt_ps = sig("cbt_ps", NCH + 2)
        cbt_copied = sig("cbt_copied", NCH)
        yzt_copied = sig("yzt_copied", NCH)
        row_ps = sig("row_ps", NCH * NRB)
        diff_ready = sig("diff_ready", NCH * NRB)
        lexp_ready = sig("lexp_ready", NCH)
        att_ready = sig("att_ready", NCH)
        xdt_ready = sig("xdt_ready", NCH)
        xw_ready = sig("xw_ready", NCH)
        state_ps = sig("state_ps", NCH - 1)
        inter_ps = sig("inter_ps", NCH - 1)
        state_ready = sig("state_ready", NCH - 1)
        yint_ready = sig("yint_ready", NCH - 1)
        y_ps = sig("y_ps", NCH)
        y0_ready = sig("y0_ready", NCH)
        lve_ready = sig("lve_ready", NCH)
        lrs_ready = sig("lrs_ready", NCH)
        ynorm_ready = sig("ynorm_ready", NCH)
        yaff_ready = sig("yaff_ready", NCH)
        yz_ready = sig("yz_ready", NCH)
        o0_ps = sig("o0_ps", 4)
        p1_ps = sig("p1_ps", NCH)
        p1_copied = sig("p1_copied", NCH)
        spe_ready = sig("spe_ready", 1)
        spl_ready = sig("spl_ready", 1)
        delta_ready = sig("delta_ready", 1)
        u1_ready = sig("u1_ready", 1)
        crep_ps = sig("crep_ps", 2)
        crep_copied = sig("crep_copied", 2)
        ctok_made = sig("ctok_made", 1)
        d_made = sig("d_made", UNITS)
        w_made = sig("w_made", UNITS)
        drep_ps = sig("drep_ps", UNITS)
        wrep_ps = sig("wrep_ps", UNITS)
        decay_ready = sig("decay_ready", UNITS)
        scanned = sig("scanned", UNITS)
        carried = sig("carried", NDG)
        hc_ready = sig("hc_ready", UNITS)
        y_sum_ps = sig("y_sum_ps", UNITS)
        y1_copied = sig("y1_copied", 2)
        y1_ready = sig("y1_ready", 1)
        y1t_ps = sig("y1t_ps", NCH)
        y1t_copied = sig("y1t_copied", NCH)
        o1_ps = sig("o1_ps", 4)

        dve_chain = sig("dve_chain", DVE_STEPS)
        act_chain = sig("act_chain", ACT_STEPS)
        pool_chain = sig("pool_chain", POOL_STEPS)

        block = ctx.enter_context(nc.Block())

        def bc(ap, shape):
            return ap.to_broadcast(shape)

        nat0 = p1[:, 0:7, 0:C]
        nato = ztd[:, 0:2, 0:DI]
        natp = yzt[:, 0, 0:4 * C].rearrange("p (r c) -> p r c", c=C)
        natw = yzt[:, 1, 0:2 * C].rearrange("p (r c) -> p r c", c=C)
        jobs = []
        for r in range(7):
            n = min(P, PROJ0 - r * P)
            parts = [(0, n, r * P if r < 3 else ZD + (r - 3) * P)]
            if r == 6:
                parts = [(0, 2 * NS, ZD + DI), (2 * NS, NH, DI)]
            for k, (c0, kn, dst) in enumerate(((0, P, wt0a), (P, CB_, wt0b))):
                jobs.append((nat0[0:n, r, c0:c0 + kn], n, kn,
                             [(dst[0:kn, d:d + w], s, w) for s, w, d in parts]))
        for r in range(2):
            n = P if r == 0 else CB_
            for m in range(XM):
                jobs.append((nato[0:n, r, m * P:(m + 1) * P], n, P, [(wo0[:, m, r * P:r * P + n], 0, n)]))
        for r in range(4):
            n = min(P, PROJ1 - r * P)
            for c0, kn, dst in ((0, P, wt1a), (P, CB_, wt1b)):
                jobs.append((natp[0:n, r, c0:c0 + kn], n, kn, [(dst[0:kn, r * P:r * P + n], 0, n)]))
        for r in range(2):
            n = P if r == 0 else CB_
            for c0, kn, dst in ((0, P, wo1a), (P, CB_, wo1b)):
                jobs.append((natw[0:n, r, c0:c0 + kn], n, kn, [(dst[0:kn, r * P:r * P + n], 0, n)]))
        copies = []
        total = 0
        for j in jobs:
            total += len(j[3])
            copies.append(total)

        @block.sync
        def _(sp):
            n = [0]

            def load(dst, src):
                sp.dma_start(dst, src, allow_slow_non_contiguous=True).then_inc(s_wload, 16)
                n[0] += 1

            sp.dma_start(xa[:, :], x_d[0, 0:P, :]).then_inc(x_loaded.sem, 16)
            sp.dma_start(xb[:, :], x_d[0, P:C, :]).then_inc(x_loaded.sem, 16)
            load(nat0[:, 0:6, :], inw_d[0:6 * P, :].rearrange("(r p) c -> p r c", p=P))
            load(nat0[0:PROJ0 - 6 * P, 6, :], inw_d[6 * P:PROJ0, :])
            load(nato[:, 0, :], outw_d[0:P, :])
            load(nato[0:CB_, 1, :], outw_d[P:C, :])
            load(natp[:, 0:3, :], wp_d[0:3 * P, :].rearrange("(r p) c -> p r c", p=P))
            load(natp[0:PROJ1 - 3 * P, 3, :], wp_d[3 * P:PROJ1, :])
            load(natw[:, 0, :], wo_d[0:P, :])
            load(natw[0:CB_, 1, :], wo_d[P:C, :])
            load(cw[:, 0:XM, :], cw_d[0:DI, :].rearrange("(m p) t -> p m t", p=P))
            load(cb[:, 0:XM], cb_d[0:DI].rearrange("(m p) -> p m", p=P))
            for h in range(2):
                load(cw[h * 2 * NS:(h + 1) * 2 * NS, XM, :], cw_d[DI:CONVD, :])
                load(cb[h * 2 * NS:(h + 1) * 2 * NS, XM:XM + 1], cb_d[DI:CONVD].rearrange("(p a) -> p a", a=1))
            load(dtb[:, :], dtb_d.partition_broadcast(P))
            load(aneg0[:, :], alog0_d.partition_broadcast(P))
            for h in range(NH):
                load(dcol[(h % 4) * HD:(h % 4 + 1) * HD, h // 4:h // 4 + 1], d0_d[h:h + 1].partition_broadcast(HD))
            load(nwb[:, :], nw_d.partition_broadcast(P))
            load(nbb[:, :], nb_d.partition_broadcast(P))
            for s in range(S1):
                load(aneg1[s * DG:(s + 1) * DG, :], alog1_d.rearrange("(g d) n -> n d g", d=DG)[s, :, :])
            load(d1b[:, :], d1_d.partition_broadcast(P))
            sp.wait_ge(s_const, 1)
            load(boc[:, 0:1], bo_d[0:P].rearrange("(p a) -> p a", a=1))
            load(boc[0:CB_, 1:2], bo_d[P:C].rearrange("(p a) -> p a", a=1))
            load(wt1b[CB_:CB_ + 1, :], bp_d.rearrange("(a n) -> a n", a=1))
            load(wt1b[CB_ + 1:CB_ + 2, C:2 * C], dtb1_d.rearrange("(a n) -> a n", a=1))
            assert n[0] == NLOADS
            sp.dma_start(spare1[:, :], bo_d[0:P].rearrange("(p a) -> p a", a=1),
                         allow_slow_non_contiguous=True).then_inc(x1_free.sem, 16)

            with sp.Fori(0, B - 1) as b:
                sp.wait_ge(x1_ready.sem, x1_ready.at(b, 4))
                sp.dma_start(xa[:, :], x_d[b + 1, 0:P, :]).then_inc(x_loaded.sem, 16)
                sp.dma_start(xb[:, :], x_d[b + 1, P:C, :]).then_inc(x_loaded.sem, 16)
                sp.wait_ge(out_ready.sem, out_ready.at(b, 4))
                sp.dma_start(out_d[b, 0:P, :], x1a[:, :]).then_inc(x1_free.sem, 16)
                sp.dma_start(out_d[b, P:C, :], x1b[:, :]).then_inc(x1_free.sem, 16)
            sp.wait_ge(out_ready.sem, B * 4)
            sp.dma_start(out_d[B - 1, 0:P, :], x1a[:, :]).then_inc(x1_free.sem, 16)
            sp.dma_start(out_d[B - 1, P:C, :], x1b[:, :]).then_inc(x1_free.sem, 16)
            sp.wait_ge(x1_free.sem, B * 32 + 16)

        @block.gpsimd
        def _(pool):
            done = [0]

            def made_before(ins):
                done[0] += 1
                ins.then_inc(s_pool, 1)
                pool.wait_ge(s_pool, done[0])

            made_before(nc.gpsimd.memset(wt1b[CB_:CB_ + 2, :], 0.0))
            nc.gpsimd.memset(boc[:, :], 0.0).then_inc(s_const, 1)
            pool.wait_ge(s_const, 1)
            made_before(nc.gpsimd.memset(xnb[CB_:CB_ + 2, :], 1.0))
            for t in (ident, identb, maskneg):
                made_before(nc.gpsimd.memset(t[:, :], 0.0))
            for t in (upper, ones, ga, gb):
                made_before(nc.gpsimd.memset(t[:, :], 1.0))
            made_before(nc.gpsimd.memset(neghalf[:, :], -0.5))
            made_before(nc.gpsimd.memset(mv[:, :, :], 0.0))
            for t in cpad + [bcpad]:
                made_before(nc.gpsimd.memset(t[:, :, :], 0.0))
            for t in (ident, identb):
                made_before(nc.gpsimd.affine_select(out=t[:, :], in_=t[:, :], compare_op=ALU.not_equal, fill=1.0,
                                                    base=0, pattern=[[-1, P]], channel_multiplier=1))
            made_before(nc.gpsimd.affine_select(out=upper[:, :], in_=upper[:, :], compare_op=ALU.is_ge, fill=0.0,
                                                base=0, pattern=[[1, P]], channel_multiplier=-1))
            made_before(nc.gpsimd.affine_select(out=maskneg[:, :], in_=maskneg[:, :], compare_op=ALU.is_ge,
                                                fill=MASKED, base=0, pattern=[[1, P]], channel_multiplier=-1))
            for t, off in ((ga, 0), (gb, P)):
                v = t[:, :].rearrange("p (q r) -> p q r", r=GROUP)
                made_before(nc.gpsimd.affine_select(out=v, in_=v, compare_op=ALU.is_ge, fill=0.0, base=off,
                                                    pattern=[[-GROUP, 43], [0, GROUP]], channel_multiplier=1))
                made_before(nc.gpsimd.affine_select(out=v, in_=v, compare_op=ALU.is_ge, fill=0.0,
                                                    base=GROUP - 1 - off,
                                                    pattern=[[GROUP, 43], [0, GROUP]], channel_multiplier=-1))
            nc.gpsimd.memset(carry[:, :], 0.0).then_inc(s_const, 1)
            pool.wait_ge(s_const, 2)
            pool.wait_ge(s_prep, PREPS)

            with pool.Fori(0, B) as b:
                made = [0]

                def step(ins):
                    made[0] += 1
                    ins.then_inc(pool_chain.sem, 1)
                    pool.wait_ge(pool_chain.sem, pool_chain.at(b, made[0]))

                def group_rstd(n):
                    pool.wait_ge(gve_ready.sem, gve_ready.at(b, n + 1))
                    nc.gpsimd.tensor_tensor(gr[:, :], gv[:, :], neghalf[:, :], ALU.pow).then_inc(grstd_ready.sem, 1)

                def scaled_x(c):
                    pool.wait_ge(xt_copied.sem, xt_copied.at(b, c + 1))
                    if c == 0:
                        pool.wait_ge(wend_ready.sem, wend_ready.at(b, 1))
                    if c >= 2:
                        pool.wait_ge(y_ps.sem, y_ps.at(b, c - 1))
                        pool.wait_ge(state_ps.sem, state_ps.at(b, c - 1))
                    xv = xtok[:, c % 2, 0:DI].rearrange("p (h d) -> p h d", d=HD)
                    nc.gpsimd.tensor_tensor(xdt[:, c % 2, :].rearrange("p (h d) -> p h d", d=HD), xv,
                                            bc(dt0[:, c, :].unsqueeze(2), [P, NH, HD]), ALU.mult).then_inc(xdt_ready.sem, 1)
                    nc.gpsimd.tensor_tensor(xw[:, c % 2, :].rearrange("p (h d) -> p h d", d=HD), xv,
                                            bc(wend[:, c, :].unsqueeze(2), [P, NH, HD]), ALU.mult).then_inc(xw_ready.sem, 1)

                def attention(c):
                    pool.wait_ge(lexp_ready.sem, lexp_ready.at(b, c + 1))
                    pool.wait_ge(cbt_copied.sem, cbt_copied.at(b, c + 1))
                    if c >= 1:
                        pool.wait_ge(y_ps.sem, y_ps.at(b, c))
                    nc.gpsimd.tensor_tensor(att[:, :, :], diff[:, :, :],
                                            bc(cbt[:, c % 2, :].unsqueeze(1), [P, NH, Q]),
                                            ALU.mult).then_inc(att_ready.sem, 1)

                def layer_rstd(c):
                    pool.wait_ge(lve_ready.sem, lve_ready.at(b, c + 1))
                    nc.gpsimd.tensor_tensor(lrs[:, c % 2:c % 2 + 1], lve[:, c % 2:c % 2 + 1], neghalf[:, 0:1],
                                            ALU.pow).then_inc(lrs_ready.sem, 1)

                def layer_affine(c):
                    pool.wait_ge(ynorm_ready.sem, ynorm_ready.at(b, c + 1))
                    step(nc.gpsimd.tensor_tensor(yw[:, c % 2, :], yw[:, c % 2, :], nwb[:, :], ALU.mult))
                    nc.gpsimd.tensor_tensor(yw[:, c % 2, :], yw[:, c % 2, :], nbb[:, :], ALU.add).then_inc(yaff_ready.sem, 1)

                group_rstd(0)
                for c in range(NCH + 2):
                    if c >= 2:
                        layer_affine(c - 2)
                    if c < NCH:
                        scaled_x(c)
                        attention(c)
                    if 1 <= c <= NCH:
                        layer_rstd(c - 1)
                group_rstd(1)
                for i in range(UNITS):
                    hf = i // NDG
                    pool.wait_ge(scanned.sem, scanned.at(b, i + 1))
                    if i == 0:
                        pool.wait_ge(crep_copied.sem, crep_copied.at(b, 2))
                    if i >= 2:
                        pool.wait_ge(y_sum_ps.sem, y_sum_ps.at(b, i - 1))
                    nc.gpsimd.tensor_tensor(hc[:, i % 2, :], hst[:, i % 3, :], crep[:, hf * HALF:(hf + 1) * HALF],
                                            ALU.mult).then_inc(hc_ready.sem, 1)
                assert made[0] == POOL_STEPS, made

        @block.scalar
        def _(act):
            for j, (_, n, kn, outs) in enumerate(jobs):
                act.wait_ge(s_wps, j + 1)
                for dst, s, w in outs:
                    nc.scalar.copy(dst, bank[j % 8][0:kn, s:s + w]).then_inc(s_wev, 1)
            act.wait_ge(s_wload, 16 * NLOADS)
            nc.scalar.activation(aneg0[:, :], aneg0[:, :], ACT.Exp).then_inc(s_wev, 1)
            nc.scalar.activation(aneg1[:, :], aneg1[:, :], ACT.Exp).then_inc(s_wev, 1)
            act.wait_ge(s_prep, PREPS)

            with act.Fori(0, B) as b:
                made = [0]

                def step(ins):
                    made[0] += 1
                    ins.then_inc(act_chain.sem, 1)
                    act.wait_ge(act_chain.sem, act_chain.at(b, made[0]))

                for m in range(XM):
                    for h in range(2):
                        act.wait_ge(conv_ps.sem, conv_ps.at(b, 2 * m + h + 1))
                        nc.scalar.copy(cpad[m][:, 1 + 16 * h:17 + 16 * h, 1:W + 1],
                                       bank[2 * m + h][:, :].rearrange("p (r w) -> p r w", w=W)).then_inc(conv_in.sem, 1)
                act.wait_ge(conv_ps.sem, conv_ps.at(b, 7))
                nc.scalar.copy(bcpad[:, 1:17, 1:W + 1],
                               bank[6][:, :].rearrange("p (r w) -> p r w", w=W)).then_inc(conv_in.sem, 1)
                act.wait_ge(conv_ps.sem, conv_ps.at(b, 8))
                nc.scalar.copy(bcpad[0:64, 17, 1:W + 1], bank[7][0:64, 0:W]).then_inc(conv_in.sem, 1)
                nc.scalar.copy(bcpad[64:P, 0, 1:W + 1], bank[7][64:P, 0:W]).then_inc(conv_in.sem, 1)
                for c in range(NCH):
                    act.wait_ge(z_ps.sem, z_ps.at(b, c + 1))
                    nc.scalar.copy(ztd[:, c, :], bank[c][:, 0:ZD]).then_inc(z_copied.sem, 1)

                act.wait_ge(dtx_ready.sem, dtx_ready.at(b, 1))
                step(nc.scalar.activation(dte[:, :, :], dtx[:, :, :], ACT.Abs))
                nc.scalar.activation(dte[:, :, :], dte[:, :, :], ACT.Exp, scale=-1.0).then_inc(dte_ready.sem, 1)
                act.wait_ge(dte_ready.sem, dte_ready.at(b, 1))
                nc.scalar.activation(dtl[:, :, :], dte[:, :, :], ACT.Ln, bias=1.0).then_inc(dtl_ready.sem, 1)
                act.wait_ge(csum_ready.sem, csum_ready.at(b, 1))
                nc.scalar.activation(cexp[:, :, :, :], csum[:, :, :, :], ACT.Exp).then_inc(cexp_ready.sem, 1)
                act.wait_ge(wdiff_ready.sem, wdiff_ready.at(b, 1))
                nc.scalar.activation(wend[:, :, :], wend[:, :, :], ACT.Exp).then_inc(wexp_ready.sem, 1)

                for m in range(XM):
                    act.wait_ge(conv_done.sem, conv_done.at(b, m + 1))
                    nc.scalar.activation(xs[m][:, :], xs[m][:, :], ACT.Silu, bias=cb[:, m:m + 1]).then_inc(silu_done.sem, 1)
                act.wait_ge(conv_done.sem, conv_done.at(b, XM + 1))
                for h in range(2):
                    for k, dst in enumerate((bs, cs_)):
                        r = 64 * h + NS * k
                        nc.scalar.activation(dst[:, h * HALF:(h + 1) * HALF], bcacc[r:r + NS, :], ACT.Silu,
                                             bias=cb[r:r + NS, XM:XM + 1]).then_inc(silu_done.sem, 1)

                def chunk_in(c):
                    act.wait_ge(xt_ps.sem, xt_ps.at(b, c + 1))
                    if c >= 2:
                        act.wait_ge(xw_ready.sem, xw_ready.at(b, c - 1))
                        act.wait_ge(state_ps.sem, state_ps.at(b, c - 1))
                    nc.scalar.copy(xtok[:, c % 2, :], bank[1][:, 0:DI + NS]).then_inc(xt_copied.sem, 1)

                def cbt_and_yzt(c):
                    act.wait_ge(cbt_ps.sem, cbt_ps.at(b, c + 1))
                    if c < NCH:
                        if c >= 2:
                            act.wait_ge(att_ready.sem, att_ready.at(b, c - 1))
                        nc.scalar.copy(cbt[:, c % 2, :], bank[5][:, 0:Q]).then_inc(cbt_copied.sem, 1)
                    if c >= 2:
                        nc.scalar.copy(yzt[:, :, (c - 2) * Q:(c - 1) * Q],
                                       bank[5][:, Q:4 * Q].rearrange("p (m q) -> p m q", q=Q)).then_inc(yzt_copied.sem, 1)

                def decays(c):
                    act.wait_ge(diff_ready.sem, diff_ready.at(b, NRB * (c + 1)))
                    nc.scalar.activation(diff[:, :, :], diff[:, :, :], ACT.Exp).then_inc(lexp_ready.sem, 1)

                for c in range(NCH + 2):
                    if c < NCH:
                        chunk_in(c)
                    cbt_and_yzt(c)
                    if c < NCH:
                        decays(c)

                for c in range(NCH):
                    act.wait_ge(p1_ps.sem, p1_ps.at(b, c + 1))
                    nc.scalar.copy(p1[:, c, :], bank[c][:, 0:PROJ1]).then_inc(p1_copied.sem, 1)
                act.wait_ge(p1_copied.sem, p1_copied.at(b, NCH))
                nc.scalar.copy(ctok[:, :, :, :], bc(p1[:, :, 2 * C + S1:2 * C + 2 * S1].unsqueeze(3),
                                                    [P, NCH, S1, DG])).then_inc(ctok_made.sem, 1)
                step(nc.scalar.activation(sp_e, p1[:, :, C:2 * C], ACT.Abs))
                nc.scalar.activation(sp_e, sp_e, ACT.Exp, scale=-1.0).then_inc(spe_ready.sem, 1)
                act.wait_ge(spe_ready.sem, spe_ready.at(b, 1))
                nc.scalar.activation(sp_l, sp_e, ACT.Ln, bias=1.0).then_inc(spl_ready.sem, 1)
                for h in range(2):
                    act.wait_ge(crep_ps.sem, crep_ps.at(b, h + 1))
                    nc.scalar.copy(crep[:, h * HALF:(h + 1) * HALF], bank[6 + h][:, :]).then_inc(crep_copied.sem, 1)

                def carry_out(i):
                    act.wait_ge(scanned.sem, scanned.at(b, i + 1))
                    nc.scalar.copy(carry[:, i:i + 1], hst[:, i % 3, HALF - 1:HALF]).then_inc(carried.sem, 1)

                def copy_y(hf):
                    act.wait_ge(y_sum_ps.sem, y_sum_ps.at(b, NDG * (hf + 1)))
                    for k in range(2):
                        ins = nc.scalar.copy(y1[:, CPH * hf + 2 * k:CPH * hf + 2 * k + 2, :],
                                             bank[4 + k][:, 0:2 * C].rearrange("p (c d) -> p c d", d=C))
                    ins.then_inc(y1_copied.sem, 1)

                def repeat_delta(i):
                    hf, g = i // NDG, i % NDG
                    if i >= 2:
                        act.wait_ge(drep_ps.sem, drep_ps.at(b, i - 1))
                    for c in range(CPH):
                        ins = nc.scalar.copy(dtok[:, i % 2, c, :, :],
                                             bc(delta[:, CPH * hf + c, g * DG:(g + 1) * DG].unsqueeze(1), [P, S1, DG]))
                    ins.then_inc(d_made.sem, 1)

                act.wait_ge(delta_ready.sem, delta_ready.at(b, 1))
                repeat_delta(0)
                for i in range(UNITS):
                    if i + 1 < UNITS:
                        repeat_delta(i + 1)
                    act.wait_ge(drep_ps.sem, drep_ps.at(b, i + 1))
                    if i >= 2:
                        act.wait_ge(scanned.sem, scanned.at(b, i - 1))
                    g = i % NDG
                    nc.scalar.activation(decay[:, i % 2, :], bank[i % 2][:, :], ACT.Exp,
                                         scale=aneg1[:, g:g + 1]).then_inc(decay_ready.sem, 1)
                    if 2 <= i < NDG + 2:
                        carry_out(i - 2)
                    if i == NDG + 3:
                        copy_y(0)
                copy_y(1)
                for c in range(NCH):
                    act.wait_ge(y1t_ps.sem, y1t_ps.at(b, c + 1))
                    nc.scalar.copy(y1ta[:, c * Q:(c + 1) * Q], bank[6 + c % 2][:, 0:Q])
                    nc.scalar.copy(y1tb[:, c * Q:(c + 1) * Q], bank[6 + c % 2][0:CB_, Q:2 * Q]).then_inc(y1t_copied.sem, 1)
                assert made[0] == ACT_STEPS, made

        @block.vector
        def _(dve):
            dve.wait_ge(s_const, 2)
            nc.vector.tensor_reduce(sel[:, :], ident[:, :].rearrange("p (n d) -> p d n", d=DG), AX_X, ALU.add).then_inc(s_prep, 1)
            dve.wait_ge(s_wload, 16 * NLOADS)
            for m in range(XM):
                nc.vector.tensor_scalar(diagd[:, m, :], ident[:, :], dcol[:, m:m + 1], None, ALU.mult).then_inc(s_prep, 1)
            dve.wait_ge(s_wev, copies[-1] + 2)
            nc.vector.tensor_scalar(aneg0[:, :], aneg0[:, :], -1.0, None, ALU.mult).then_inc(s_prep, 1)
            nc.vector.tensor_scalar(aneg1[:, :], aneg1[:, :], -1.0, None, ALU.mult).then_inc(s_prep, 1)
            dve.wait_ge(s_prep, PREPS)

            with dve.Fori(0, B) as b:
                made = [0]

                def step(ins):
                    made[0] += 1
                    ins.then_inc(dve_chain.sem, 1)
                    dve.wait_ge(dve_chain.sem, dve_chain.at(b, made[0]))

                def group_norm(n, ta, tb):
                    for h in range(2):
                        nc.vector.bn_stats(st[:, 0, h, :], ta[:, h * HALF:(h + 1) * HALF])
                        ins = nc.vector.bn_stats(st[0:CB_, 1, h, :], tb[:, h * HALF:(h + 1) * HALF])
                    step(ins)
                    nc.vector.memset(spare[:, :], 0.0)
                    nc.vector.bn_aggr(mv[:, 0, :], st[:, 0, :, :].rearrange("p a s -> p (a s)")).then_inc(stats_ready.sem, 1)
                    nc.vector.bn_aggr(mv[0:CB_, 1, :], st[0:CB_, 1, :, :].rearrange("p a s -> p (a s)")).then_inc(stats_ready.sem, 1)
                    dve.wait_ge(gmean_ps.sem, gmean_ps.at(b, n + 1))
                    step(nc.vector.tensor_scalar(gm[:, :], bank[0][:, 0:2], 1.0 / GROUP, None, ALU.mult))
                    step(nc.vector.tensor_tensor(gd[:, :], mv[:, :, 0], gm[:, :], ALU.subtract))
                    step(nc.vector.tensor_tensor(gd[:, :], gd[:, :], gd[:, :], ALU.mult))
                    nc.vector.tensor_tensor(gq[:, :], gd[:, :], mv[:, :, 1], ALU.add).then_inc(gdev_ready.sem, 1)
                    dve.wait_ge(gvar_ps.sem, gvar_ps.at(b, n + 1))
                    nc.vector.tensor_scalar(gv[:, :], bank[1][:, 0:2], 1.0 / GROUP, GEPS, ALU.mult, ALU.add).then_inc(gve_ready.sem, 1)
                    dve.wait_ge(grstd_ready.sem, grstd_ready.at(b, n + 1))
                    nc.vector.tensor_scalar(xna[:, :], ta[:, :], gm[:, 0:1], gr[:, 0:1], ALU.subtract, ALU.mult).then_inc(xn_ready.sem, 1)
                    nc.vector.tensor_scalar(xnb[0:CB_, :], tb[:, :], gm[0:CB_, 1:2], gr[0:CB_, 1:2],
                                            ALU.subtract, ALU.mult).then_inc(xn_ready.sem, 1)

                def conv(m, image, acc, rows):
                    accv = acc.rearrange("p (r w) -> p r w", w=W)
                    for t in range(9):
                        win = image[:, t // 3:t // 3 + rows, t % 3:t % 3 + W]
                        if t == 0:
                            ins = nc.vector.tensor_scalar(accv, win, cw[:, m, 0:1], None, ALU.mult)
                        else:
                            ins = nc.vector.scalar_tensor_tensor(accv, win, cw[:, m, t:t + 1], accv, ALU.mult, ALU.add)
                        if t < 8:
                            step(ins)
                    ins.then_inc(conv_done.sem, 1)

                def softplus(v, e, l, u, out):
                    step(nc.vector.tensor_scalar(u, e, 1.0, None, ALU.add))
                    step(nc.vector.scalar_tensor_tensor(u, u, -1.0, e, ALU.add, ALU.subtract))
                    step(nc.vector.tensor_tensor(u, l, u, ALU.subtract))
                    return nc.vector.scalar_tensor_tensor(out, v, 0.0, u, ALU.max, ALU.add)

                dve.wait_ge(x_loaded.sem, x_loaded.at(b, 32))
                group_norm(0, xa, xb)

                dve.wait_ge(z_copied.sem, z_copied.at(b, NCH))
                nc.vector.tensor_tensor(dtx[:, :, :], ztd[:, :, DI:ZD], bc(dtb[:, :].unsqueeze(1), [P, NCH, NH]),
                                        ALU.add).then_inc(dtx_ready.sem, 1)
                conv(0, cpad[0], xs[0][:, :], H)
                dve.wait_ge(dtl_ready.sem, dtl_ready.at(b, 1))
                step(softplus(dtx[:, :, :], dte[:, :, :], dtl[:, :, :], dtu[:, :, :], dt0[:, :, :]))
                nc.vector.tensor_tensor(da0[:, :, :], dt0[:, :, :], bc(aneg0[:, :].unsqueeze(1), [P, NCH, NH]),
                                        ALU.mult).then_inc(da_ready.sem, 1)
                dve.wait_ge(cs_ps.sem, cs_ps.at(b, 1))
                nc.vector.tensor_copy(csum[:, :, :, :].rearrange("p a c h -> p (a c h)"),
                                      bank[0][:, 0:2 * NCH * NH]).then_inc(csum_ready.sem, 1)
                dve.wait_ge(csum_ready.sem, csum_ready.at(b, 1))
                nc.vector.tensor_tensor(wend[:, :, :], csum[:, 1, :, :], csum[:, 0, :, :], ALU.subtract).then_inc(wdiff_ready.sem, 1)
                dve.wait_ge(wexp_ready.sem, wexp_ready.at(b, 1))
                nc.vector.tensor_tensor(wend[:, :, :], wend[:, :, :], dt0[:, :, :], ALU.mult).then_inc(wend_ready.sem, 1)
                conv(1, cpad[1], xs[1][:, :], H)
                conv(2, cpad[2], xs[2][:, :], H)
                conv(XM, bcpad, bcacc[:, :], H // 2)

                def differences(c):
                    if c >= 1:
                        dve.wait_ge(att_ready.sem, att_ready.at(b, c))
                    for r in range(NRB):
                        dve.wait_ge(row_ps.sem, row_ps.at(b, NRB * c + r + 1))
                        nc.vector.tensor_tensor(diff[:, HPB * r:HPB * (r + 1), :],
                                                bank[2 + r][:, :].rearrange("p (h q) -> p h q", q=Q),
                                                bc(csum[:, 0, c, HPB * r:HPB * (r + 1)].unsqueeze(2), [P, HPB, Q]),
                                                ALU.subtract).then_inc(diff_ready.sem, 1)

                def carry_state(c):
                    sv = state[:, :].rearrange("p (h d) -> p h d", d=HD)
                    dve.wait_ge(state_ps.sem, state_ps.at(b, c + 1))
                    if c == 0:
                        nc.vector.tensor_copy(state[:, :], bank[0][0:NS, 0:DI]).then_inc(state_ready.sem, 1)
                        return
                    dve.wait_ge(inter_ps.sem, inter_ps.at(b, c))
                    step(nc.vector.tensor_tensor(sv, sv, bc(cexp[0:NS, 1, c, :].unsqueeze(2), [NS, NH, HD]), ALU.mult))
                    nc.vector.tensor_tensor(state[:, :], state[:, :], bank[0][0:NS, 0:DI], ALU.add).then_inc(state_ready.sem, 1)

                def outputs(c):
                    if c >= 1:
                        dve.wait_ge(inter_ps.sem, inter_ps.at(b, c))
                        nc.vector.tensor_tensor(yint[:, :].rearrange("p (h d) -> p h d", d=HD),
                                                bank[6][:, 0:DI].rearrange("p (h d) -> p h d", d=HD),
                                                bc(cexp[:, 0, c, :].unsqueeze(2), [P, NH, HD]),
                                                ALU.mult).then_inc(yint_ready.sem, 1)
                        dve.wait_ge(yint_ready.sem, yint_ready.at(b, c))
                        dve.wait_ge(y_ps.sem, y_ps.at(b, c + 1))
                        ins = nc.vector.tensor_tensor(y0[:, c % 2, :], yint[:, :], bank[7][:, 0:DI], ALU.add)
                    else:
                        dve.wait_ge(y_ps.sem, y_ps.at(b, 1))
                        ins = nc.vector.tensor_copy(y0[:, 0, :], bank[7][:, 0:DI])
                    ins.then_inc(y0_ready.sem, 1)
                    dve.wait_ge(y0_ready.sem, y0_ready.at(b, c + 1))
                    step(nc.vector.bn_stats(lst[:, c % 2, :], y0[:, c % 2, :]))
                    nc.vector.memset(spare[:, :], 0.0)
                    step(nc.vector.bn_aggr(lmv[:, c % 2, :], lst[:, c % 2, :]))
                    nc.vector.tensor_scalar(lve[:, c % 2:c % 2 + 1], lmv[:, c % 2, 1:2], LEPS, None, ALU.add).then_inc(lve_ready.sem, 1)

                def normalise(c):
                    dve.wait_ge(lrs_ready.sem, lrs_ready.at(b, c + 1))
                    nc.vector.tensor_scalar(yw[:, c % 2, :], y0[:, c % 2, :], lmv[:, c % 2, 0:1], lrs[:, c % 2:c % 2 + 1],
                                            ALU.subtract, ALU.mult).then_inc(ynorm_ready.sem, 1)

                def gate(c):
                    dve.wait_ge(yaff_ready.sem, yaff_ready.at(b, c + 1))
                    if c >= 2:
                        dve.wait_ge(cbt_ps.sem, cbt_ps.at(b, c + 1))
                    nc.vector.tensor_tensor(yz[:, c % 2, :], yw[:, c % 2, :], ztd[:, c, 0:DI], ALU.mult).then_inc(yz_ready.sem, 1)

                dve.wait_ge(cexp_ready.sem, cexp_ready.at(b, 1))
                for c in range(NCH + 2):
                    if c < NCH:
                        differences(c)
                    if 1 <= c < NCH:
                        carry_state(c - 1)
                    if 1 <= c <= NCH:
                        outputs(c - 1)
                    if c >= 2:
                        gate(c - 2)
                    if 1 <= c <= NCH:
                        normalise(c - 1)

                dve.wait_ge(x1_free.sem, x1_free.at(b, 16))
                for m, (dst, src, n) in enumerate(((x1a, xa, P), (x1b, xb, CB_))):
                    for h in range(2):
                        k = 2 * m + h
                        dve.wait_ge(o0_ps.sem, o0_ps.at(b, k + 1))
                        nc.vector.tensor_tensor(dst[:, h * HALF:(h + 1) * HALF], bank[1 + k][0:n, :],
                                                src[:, h * HALF:(h + 1) * HALF], ALU.add).then_inc(x1_ready.sem, 1)
                dve.wait_ge(x1_ready.sem, x1_ready.at(b, 4))
                group_norm(1, x1a, x1b)

                dve.wait_ge(spl_ready.sem, spl_ready.at(b, 1))
                softplus(p1[:, :, C:2 * C], sp_e, sp_l, sp_u, delta[:, :, :]).then_inc(delta_ready.sem, 1)
                dve.wait_ge(delta_ready.sem, delta_ready.at(b, 1))
                nc.vector.tensor_tensor(u1[:, :, :], delta[:, :, :], p1[:, :, 0:C], ALU.mult).then_inc(u1_ready.sem, 1)
                dve.wait_ge(u1_ready.sem, u1_ready.at(b, 1))

                def inputs(i):
                    hf, g = i // NDG, i % NDG
                    if i >= 2:
                        dve.wait_ge(wrep_ps.sem, wrep_ps.at(b, i - 1))
                    for c in range(CPH):
                        cc = CPH * hf + c
                        ins = nc.vector.tensor_tensor(
                            wtok[:, i % 2, c, :, :],
                            bc(u1[:, cc, g * DG:(g + 1) * DG].unsqueeze(1), [P, S1, DG]),
                            bc(p1[:, cc, 2 * C:2 * C + S1].unsqueeze(2), [P, S1, DG]), ALU.mult)
                    ins.then_inc(w_made.sem, 1)

                def scan(i):
                    hf, g = i // NDG, i % NDG
                    dve.wait_ge(decay_ready.sem, decay_ready.at(b, i + 1))
                    dve.wait_ge(wrep_ps.sem, wrep_ps.at(b, i + 1))
                    if i >= 3:
                        dve.wait_ge(hc_ready.sem, hc_ready.at(b, i - 2))
                        if i < NDG + 3:
                            dve.wait_ge(carried.sem, carried.at(b, i - 2))
                    if hf:
                        dve.wait_ge(carried.sem, carried.at(b, g + 1))
                    nc.vector.tensor_tensor_scan(hst[:, i % 3, :], decay[:, i % 2, :], bank[2 + i % 2][:, :],
                                                 carry[:, g:g + 1] if hf else 0.0, ALU.mult, ALU.add).then_inc(scanned.sem, 1)

                for i in range(UNITS + 1):
                    if i < UNITS:
                        inputs(i)
                    if i >= 1:
                        scan(i - 1)

                step(nc.vector.tensor_tensor(p1[:, :, 0:C], p1[:, :, 0:C], bc(d1b[:, :].unsqueeze(1), [P, NCH, C]), ALU.mult))
                dve.wait_ge(y1_copied.sem, y1_copied.at(b, 2))
                nc.vector.tensor_tensor(y1[:, :, :], y1[:, :, :], p1[:, :, 0:C], ALU.add).then_inc(y1_ready.sem, 1)

                for m, (dst, n) in enumerate(((x1a, P), (x1b, CB_))):
                    for h in range(2):
                        k = 2 * m + h
                        dve.wait_ge(o1_ps.sem, o1_ps.at(b, k + 1))
                        nc.vector.scalar_tensor_tensor(dst[:, h * HALF:(h + 1) * HALF], bank[k][0:n, :], boc[0:n, m:m + 1],
                                                       dst[:, h * HALF:(h + 1) * HALF], ALU.add, ALU.add).then_inc(out_ready.sem, 1)
                assert made[0] == DVE_STEPS, (made, DVE_STEPS)

        @block.tensor
        def _(pe):
            pe.wait_ge(s_const, 2)
            pe.wait_ge(s_wload, 16 * NLOADS)
            for j, (src, n, kn, outs) in enumerate(jobs):
                if j >= 8:
                    pe.wait_ge(s_wev, copies[j - 8])
                nc.tensor.transpose(bank[j % 8][0:kn, 0:n], src, ident[0:n, 0:n]).then_inc(s_wps, 1)
            pe.wait_ge(s_prep, PREPS)
            pe.wait_ge(s_wev, copies[-1])

            def mm(out, lhsT, rhs, start, stop):
                return nc.tensor.matmul(out, lhsT, rhs, start=start, stop=stop, skip_group_check=True)

            with pe.Fori(0, B) as b:
                def group_sums(n):
                    pe.wait_ge(stats_ready.sem, stats_ready.at(b, 2 * n + 2))
                    for m in range(2):
                        mm(bank[0][:, m:m + 1], ga[:, m * P:(m + 1) * P], mv[:, 0, 0:1], True, False)
                        ins = mm(bank[0][:, m:m + 1], gb[:, m * P:(m + 1) * P], mv[0:CB_, 1, 0:1], False, True)
                    ins.then_inc(gmean_ps.sem, 1)
                    pe.wait_ge(gdev_ready.sem, gdev_ready.at(b, n + 1))
                    for m in range(2):
                        mm(bank[1][:, m:m + 1], ga[:, m * P:(m + 1) * P], gq[:, 0:1], True, False)
                        ins = mm(bank[1][:, m:m + 1], gb[:, m * P:(m + 1) * P], gq[0:CB_, 1:2], False, True)
                    ins.then_inc(gvar_ps.sem, 1)

                group_sums(0)
                pe.wait_ge(xn_ready.sem, xn_ready.at(b, 2))
                for m in range(XM):
                    w0 = ZD + m * P
                    for h in range(2):
                        t = slice(h * HALF, (h + 1) * HALF)
                        mm(bank[2 * m + h][:, :], wt0a[:, w0:w0 + P], xna[:, t], True, False)
                        mm(bank[2 * m + h][:, :], wt0b[:, w0:w0 + P], xnb[0:CB_, t], False, True).then_inc(conv_ps.sem, 1)
                w0 = ZD + DI
                for bk, spans in ((6, ((0, HALF), (HALF, HALF))), (7, ((HALF, W), (HALF - W, W)))):
                    for h, (t0, n) in enumerate(spans):
                        o = bank[bk][64 * h:64 * (h + 1), 0:n]
                        mm(o, wt0a[:, w0:w0 + 2 * NS], xna[:, t0:t0 + n], True, False)
                        ins = mm(o, wt0b[:, w0:w0 + 2 * NS], xnb[0:CB_, t0:t0 + n], False, True)
                    ins.then_inc(conv_ps.sem, 1)
                for c in range(NCH):
                    t = slice(c * Q, (c + 1) * Q)
                    pe.wait_ge(conv_in.sem, conv_in.at(b, c + 1 if c < 7 else 9))
                    mm(bank[c][:, 0:ZD], xna[:, t], wt0a[:, 0:ZD], True, False)
                    mm(bank[c][:, 0:ZD], xnb[0:CB_, t], wt0b[:, 0:ZD], False, True).then_inc(z_ps.sem, 1)

                pe.wait_ge(da_ready.sem, da_ready.at(b, 1))
                n = NCH * NH
                mm(bank[0][:, 0:n], upper[:, :], da0[:, :, :].rearrange("p c h -> p (c h)"), True, True)
                mm(bank[0][:, n:2 * n], ones[:, :], da0[:, :, :].rearrange("p c h -> p (c h)"), True, True).then_inc(cs_ps.sem, 1)

                pe.wait_ge(csum_ready.sem, csum_ready.at(b, 1))
                pe.wait_ge(z_copied.sem, z_copied.at(b, NCH))

                def rows(c):
                    for r in range(NRB):
                        if c >= 1:
                            pe.wait_ge(diff_ready.sem, diff_ready.at(b, NRB * (c - 1) + r + 1))
                        for k in range(HPB):
                            h = HPB * r + k
                            nc.tensor.matmul(bank[2 + r][:, k * Q:(k + 1) * Q], bc(csum[:, 0, c, h:h + 1], [P, P]), ident[:, :],
                                             start=(k == 0), stop=False, is_transpose=True, skip_group_check=True)
                        mm(bank[2 + r][:, :].rearrange("p (h q) -> p h q", q=Q), identb[:, :],
                           bc(maskneg[:, :].unsqueeze(1), [P, HPB, Q]), False, True).then_inc(row_ps.sem, 1)

                def chunk_in(c):
                    t = slice(c * Q, (c + 1) * Q)
                    if c == 0:
                        pe.wait_ge(silu_done.sem, silu_done.at(b, XM + 4))
                    else:
                        pe.wait_ge(xt_copied.sem, xt_copied.at(b, c))
                    for m in range(XM):
                        nc.tensor.transpose(bank[1][:, m * P:(m + 1) * P], xs[m][:, t], ident[:, :])
                    nc.tensor.transpose(bank[1][:, DI:DI + NS], bs[:, t], ident[0:NS, 0:NS]).then_inc(xt_ps.sem, 1)

                def cbt_and_yzt(c):
                    if c >= 1:
                        pe.wait_ge(cbt_copied.sem, cbt_copied.at(b, min(c, NCH)))
                    if c >= 3:
                        pe.wait_ge(yzt_copied.sem, yzt_copied.at(b, c - 2))
                    if c < NCH:
                        t = slice(c * Q, (c + 1) * Q)
                        ins = mm(bank[5][:, 0:Q], bs[:, t], cs_[:, t], True, True)
                    if c >= 2:
                        pe.wait_ge(yz_ready.sem, yz_ready.at(b, c - 1))
                        for m in range(XM):
                            ins = nc.tensor.transpose(bank[5][:, (m + 1) * Q:(m + 2) * Q], yz[:, c % 2, m * P:(m + 1) * P],
                                                      ident[:, :])
                    ins.then_inc(cbt_ps.sem, 1)

                def new_state(c):
                    pe.wait_ge(xw_ready.sem, xw_ready.at(b, c + 1))
                    if c >= 1:
                        pe.wait_ge(state_ready.sem, state_ready.at(b, c))
                    mm(bank[0][0:NS, 0:DI], xtok[:, c % 2, DI:DI + NS], xw[:, c % 2, :], True, True).then_inc(state_ps.sem, 1)

                def from_state(c):
                    pe.wait_ge(state_ready.sem, state_ready.at(b, c))
                    if c >= 2:
                        pe.wait_ge(yint_ready.sem, yint_ready.at(b, c - 1))
                    mm(bank[6][:, 0:DI], cs_[:, c * Q:(c + 1) * Q], state[:, :], True, True).then_inc(inter_ps.sem, 1)

                def within(c):
                    t = slice(c * Q, (c + 1) * Q)
                    if c >= 1:
                        pe.wait_ge(y0_ready.sem, y0_ready.at(b, c))
                    for m in range(XM):
                        mm(bank[7][:, m * P:(m + 1) * P], xs[m][:, t], diagd[:, m, :], m == 0, False)
                    pe.wait_ge(xdt_ready.sem, xdt_ready.at(b, c + 1))
                    pe.wait_ge(att_ready.sem, att_ready.at(b, c + 1))
                    for h in range(NH):
                        ins = mm(bank[7][:, h * HD:(h + 1) * HD], att[:, h, :], xdt[:, c % 2, h * HD:(h + 1) * HD],
                                 False, h == NH - 1)
                    ins.then_inc(y_ps.sem, 1)

                rows(0)
                for c in range(NCH + 2):
                    if c < NCH:
                        chunk_in(c)
                    cbt_and_yzt(c)
                    if c < NCH:
                        if c + 1 < NCH:
                            rows(c + 1)
                            new_state(c)
                        if c >= 1:
                            from_state(c)
                        within(c)

                pe.wait_ge(yzt_copied.sem, yzt_copied.at(b, NCH))
                for m, n in enumerate((P, CB_)):
                    for h in range(2):
                        k = 2 * m + h
                        for j in range(XM):
                            ins = mm(bank[1 + k][0:n, :], wo0[:, j, m * P:m * P + n], yzt[:, j, h * HALF:(h + 1) * HALF],
                                     j == 0, j == XM - 1)
                        ins.then_inc(o0_ps.sem, 1)

                group_sums(1)
                pe.wait_ge(xn_ready.sem, xn_ready.at(b, 4))
                for c in range(NCH):
                    t = slice(c * Q, (c + 1) * Q)
                    mm(bank[c][:, 0:PROJ1], xna[:, t], wt1a[:, :], True, False)
                    mm(bank[c][:, 0:PROJ1], xnb[:, t], wt1b[:, :], False, True).then_inc(p1_ps.sem, 1)
                pe.wait_ge(ctok_made.sem, ctok_made.at(b, 1))
                for c in range(NCH):
                    ins = nc.tensor.transpose(bank[6 + c // CPH][:, (c % CPH) * Q:(c % CPH + 1) * Q],
                                              ctok[:, c, :, :].rearrange("p n d -> p (n d)"), ident[:, :])
                    if c % CPH == CPH - 1:
                        ins.then_inc(crep_ps.sem, 1)

                def spread(i):
                    hf, g = i // NDG, i % NDG
                    pe.wait_ge(d_made.sem, d_made.at(b, i + 1))
                    if i >= 2:
                        pe.wait_ge(decay_ready.sem, decay_ready.at(b, i - 1))
                    for c in range(CPH):
                        ins = nc.tensor.transpose(bank[i % 2][:, c * Q:(c + 1) * Q],
                                                  dtok[:, i % 2, c, :, :].rearrange("p n d -> p (n d)"), ident[:, :])
                    ins.then_inc(drep_ps.sem, 1)
                    if i >= 2:
                        pe.wait_ge(scanned.sem, scanned.at(b, i - 1))
                    pe.wait_ge(w_made.sem, w_made.at(b, i + 1))
                    for c in range(CPH):
                        ins = nc.tensor.transpose(bank[2 + i % 2][:, c * Q:(c + 1) * Q],
                                                  wtok[:, i % 2, c, :, :].rearrange("p n d -> p (n d)"), ident[:, :])
                    ins.then_inc(wrep_ps.sem, 1)

                def sum_states(i):
                    hf, g = i // NDG, i % NDG
                    if i == NDG:
                        pe.wait_ge(y1_copied.sem, y1_copied.at(b, 1))
                    pe.wait_ge(hc_ready.sem, hc_ready.at(b, i + 1))
                    for c in range(CPH):
                        o = (c % 2) * C + g * DG
                        ins = mm(bank[4 + c // 2][:, o:o + DG], hc[:, i % 2, c * Q:(c + 1) * Q], sel[:, :], True, True)
                    ins.then_inc(y_sum_ps.sem, 1)

                for i in range(UNITS + 3):
                    if i < UNITS:
                        spread(i)
                    if i >= 3:
                        sum_states(i - 3)
                pe.wait_ge(y1_ready.sem, y1_ready.at(b, 1))
                for c in range(NCH):
                    if c >= 2:
                        pe.wait_ge(y1t_copied.sem, y1t_copied.at(b, c - 1))
                    nc.tensor.transpose(bank[6 + c % 2][:, 0:P], y1[:, c, 0:P], ident[:, :])
                    nc.tensor.transpose(bank[6 + c % 2][0:CB_, Q:2 * Q], y1[:, c, P:C], ident[:, :]).then_inc(y1t_ps.sem, 1)
                pe.wait_ge(y1t_copied.sem, y1t_copied.at(b, NCH))
                for m, n in enumerate((P, CB_)):
                    for h in range(2):
                        t = slice(h * HALF, (h + 1) * HALF)
                        k = 2 * m + h
                        mm(bank[k][0:n, :], wo1a[:, m * P:m * P + n], y1ta[:, t], True, False)
                        mm(bank[k][0:n, :], wo1b[:, m * P:m * P + n], y1tb[:, t], False, True).then_inc(o1_ps.sem, 1)


NLOADS = 51
PREPS = 6
DVE_STEPS = 70
ACT_STEPS = 2
POOL_STEPS = NCH

_INS = [("x", (B, C, L)), ("L0_conv_in_proj_w", (PROJ0, C)), ("L0_conv_conv_w", (CONVD, 9)),
        ("L0_conv_conv_b", (CONVD,)), ("L0_conv_dt_bias", (NH,)), ("L0_conv_A_log", (NH,)),
        ("L0_conv_D", (NH,)), ("L0_conv_norm_w", (DI,)), ("L0_conv_norm_b", (DI,)),
        ("L0_conv_out_proj_w", (C, DI)), ("L1_conv_W_proj", (PROJ1, C)), ("L1_conv_b_proj", (PROJ1,)),
        ("L1_conv_A_log", (C, S1)), ("L1_conv_D", (C,)), ("L1_conv_dt_bias", (C,)),
        ("L1_conv_W_out", (C, C)), ("L1_conv_b_out", (C,))]


def kernel(**inputs):
    import numpy as _np
    import concourse.bacc as _bacc
    from concourse import mybir as _mybir
    from concourse.bass_utils import run_bass_kernel_spmd as _run

    nc = _bacc.Bacc("TRN2", target_bir_lowering=False, num_devices=1)
    arrays, args = {}, []
    for name, shape in _INS:
        a = _np.ascontiguousarray(inputs[name]).reshape(shape)
        arrays[f"in_{name}_dram"] = a
        args.append(nc.dram_tensor(f"in_{name}_dram", shape, _mybir.dt.from_np(a.dtype), kind="ExternalInput").ap())
    args.append(nc.dram_tensor("out_0_dram", (B, C, L), _mybir.dt.float32, kind="ExternalOutput").ap())
    build(nc, *args)
    r = _run(nc, [arrays], core_ids=[0])
    return r.results[0]["out_0_dram"].reshape(B, C, H, W)
```

```python
from contextlib import ExitStack

import concourse.bass as bass
from concourse import mybir

ALU = mybir.AluOpType
ACT = mybir.ActivationFunctionType
F32 = mybir.dt.float32
BF16 = mybir.dt.bfloat16
AX_X = mybir.AxisListType.X

P = 128
B, C, H, W = 16, 192, 32, 32
L = H * W
Q = 128
NCH = L // Q
CB_ = C - P
GROUP = 6
NG = C // GROUP
GEPS = 1e-5
LEPS = 1e-5
DI = 384
NS = 32
NH = 12
HD = 32
XM = DI // P
CONVD = DI + 2 * NS
PROJ0 = 2 * DI + 2 * NS + NH
ZD = DI + NH
HPB = 4
NRB = NH // HPB
MASKED = -1e30
S1 = 16
PROJ1 = 2 * C + 2 * S1
DG = P // S1
NDG = C // DG
HALF = L // 2
CPH = HALF // Q
UNITS = 2 * NDG


SLOTS = UNITS
FILLS = 9
FILL_AT = (4, 4, 5, 5, 6, 6, 7, 9, 9)
CONV_AT = 6
TAPS = 4
SSD_AT = 16
SSD_LAST = 9
PRE_AT = SSD_AT + 2 * (NCH - 1) + SSD_LAST
P1_AT = (4, 4, 5, 5, 6, 6)
TAIL_AT = 6
COL_D, COL_B, COL_C = C, 2 * C, 2 * C + P
WCOLS = 2 * C + 2 * P
PIECE = (0, 2)
MID = 1
P1_TILES = (("dA", 0), ("dB", 0), ("xA", 0), ("xB", 0), ("B", 0), ("C", 0), ("dA", 1), ("xA", 1), ("B", 1), ("C", 1))
EARLY = 6
RING = 4
MID_STORE_AT = 8
YQ = 2
YG = NDG // YQ


class Signal:

    def __init__(self, sem, per_image):
        self.sem, self.per_image = sem, per_image

    def at(self, n, k):
        return n * self.per_image + k


class Steps:

    def __init__(self, eng, raised, n):
        self.eng, self.raised, self.n, self.done = eng, raised, n, 0

    def __call__(self, ins):
        self.done += 1
        ins.then_inc(self.raised.sem, 1)
        self.eng.wait_ge(self.raised.sem, self.raised.at(self.n, self.done))


def build(nc, scratch, x_d, inw_d, cw_d, cb_d, dtb_d, alog0_d, d0_d, nw_d, nb_d, outw_d,
          wp_d, bp_d, alog1_d, d1_d, dtb1_d, wo_d, bo_d, out_d):
    with ExitStack() as ctx:
        def sb(name, shape, dt=F32):
            return ctx.enter_context(nc.sbuf_tensor(name, shape, dt))

        def sem(name):
            return ctx.enter_context(nc.semaphore(name))

        def sig(name, per_image):
            return Signal(sem(name), per_image)

        bank = [ctx.enter_context(nc.psum_tensor(f"bank{i}", [P, 512], F32)) for i in range(8)]
        B_GATE, B_OUT, B_YSUM = 0, 1, 2
        B_XY, B_CBT, B_STATE = 3, 4, 5
        B_YT = 0
        FILL_BANKS = (3, 4, 5)
        B_CSUM = 3
        ROW_BANKS = (6, 6, 7)
        P1_BANKS = (3, 4, 5, 6, 7, 0, 5, 6, 7, 5)

        ident = sb("ident", [P, P])
        identb = sb("identb", [P, P], BF16)
        upper = sb("upper", [P, P])
        ones = sb("ones", [P, P])
        maskneg = sb("maskneg", [P, P], BF16)
        sel = sb("sel", [P, DG])
        ga = sb("ga", [P, 43 * GROUP])
        gb = sb("gb", [CB_, 43 * GROUP])
        neghalf = sb("neghalf", [P, 2])
        wt0a = sb("wt0a", [P, PROJ0])
        wt0b = sb("wt0b", [CB_, PROJ0])
        wo0 = sb("wo0", [P, XM, C])
        wt1a = sb("wt1a", [P, WCOLS])
        wt1b = sb("wt1b", [CB_ + 2, WCOLS])
        bbc = sb("bbc", [CB_ + 1, 2 * S1])
        wo1a = sb("wo1a", [P, C])
        wo1b = sb("wo1b", [P, C])
        cw = sb("cw", [P, XM + 1, 9])
        cb = sb("cb", [P, XM + 1])
        dtb = sb("dtb", [P, NH])
        aneg0 = sb("aneg0", [P, NH])
        dcol = sb("dcol", [P, XM])
        diagd = sb("diagd", [P, XM, P])
        nwc = sb("nwc", [P, XM])
        nbc = sb("nbc", [P, XM])
        aneg1 = sb("aneg1", [P, NDG])
        d1c = sb("d1c", [P, 2])
        boc = sb("boc", [P, 2])

        xa = sb("xa", [P, L])
        xb = sb("xb", [CB_, L])
        xna = sb("xna", [P, L])
        xnb = sb("xnb", [CB_ + 2, L])
        st = sb("st", [P, 2, 2, 6])
        mv = sb("mv", [P, 2, 2])
        spare = sb("spare", [P, 1])
        gm = sb("gm", [P, 2])
        gd = sb("gd", [P, 2])
        gq = sb("gq", [P, 2])
        gv = sb("gv", [P, 2])
        gr = sb("gr", [P, 2])
        cpad = [sb(f"cpad{m}", [P, H + 2, W + 2]) for m in range(2)]
        bcpad = sb("bcpad", [P, H // 2 + 2, W + 2])
        xs = [sb(f"xs{m}", [P, L]) for m in range(XM)]
        bcacc = sb("bcacc", [P, HALF])
        bs = sb("bs", [NS, L])
        cs_ = sb("cs_", [NS, L])
        dtx = sb("dtx", [P, NCH, NH])
        dte = sb("dte", [P, NCH, NH])
        dtl = sb("dtl", [P, NCH, NH])
        dtu = sb("dtu", [P, NCH, NH])
        dt0 = sb("dt0", [P, NCH, NH])
        da0 = sb("da0", [P, NCH, NH])
        csum = sb("csum", [P, 2, NCH, NH])
        lndt = sb("lndt", [P, NCH, NH])
        ncs = sb("ncs", [P, NCH, NH])
        cexp = sb("cexp", [P, 2, NCH, NH])
        wend = sb("wend", [P, NCH, NH])
        xtok = sb("xtok", [P, 2, DI + NS])
        cbt = sb("cbt", [P, 2, Q])
        att = sb("att", [P, 2, NH, Q])
        xw = sb("xw", [P, 2, DI])
        state = sb("state", [NS, DI])
        yint = sb("yint", [P, 2, DI])
        y0 = sb("y0", [P, 2, DI])
        lst = sb("lst", [P, 2, 6])
        lmv = sb("lmv", [P, 2, 2])
        lve = sb("lve", [P, 2])
        lrs = sb("lrs", [P, 2])
        yzt = sb("yzt", [P, 2, XM, Q])
        x1a = [sb(f"x1a{p}", [P, L]) for p in range(2)]
        x1b = [sb(f"x1b{p}", [CB_, L]) for p in range(2)]
        xcm = [sb(f"xcm{p}", [P, 3, HALF]) for p in range(2)]
        brep = [sb(f"brep{p}", [P, L]) for p in range(2)]
        crep = [sb(f"crep{p}", [P, L]) for p in range(2)]
        delta = sb("delta", [P, 3, HALF])
        u1 = sb("u1", [P, 3, HALF])
        drep = sb("drep", [P, RING, HALF])
        urep = sb("urep", [P, RING, HALF])
        decay = sb("decay", [P, 2, HALF])
        hst = sb("hst", [P, 3, HALF])
        carry = sb("carry", [P, NDG])
        hc = sb("hc", [P, 2, HALF])
        y1 = sb("y1", [P, NCH, C])
        y1ta = sb("y1ta", [P, 2, Q])
        y1tb = sb("y1tb", [P, 2, Q])
        attv = att[:, :, :, :].rearrange("p a h q -> p (a h q)")
        sp_e = attv[:, 0:3 * HALF].rearrange("p (c d) -> p c d", d=HALF)
        sp_l = attv[:, 3 * HALF:6 * HALF].rearrange("p (c d) -> p c d", d=HALF)

        s_const = sem("constants_made")
        s_pool = sem("pool_constants")
        s_wload = sem("weights_loaded")
        s_wps = sem("weight_transposed")
        s_wev = sem("weight_copied")
        s_prep = sem("weights_prepared")
        x_loaded = sig("x_loaded", 32)
        stats_ready = sig("stats_ready", 4)
        gmean_ps = sig("gmean_ps", 2)
        gdev_ready = sig("gdev_ready", 2)
        gvar_ps = sig("gvar_ps", 2)
        gve_ready = sig("gve_ready", 2)
        grstd_ready = sig("grstd_ready", 2)
        xn_ready = sig("xn_ready", 4)
        fill_ps = sig("fill_ps", FILLS)
        fill_copied = sig("fill_copied", FILLS)
        conv_done = sig("conv_done", XM + 1)
        silu_done = sig("silu_done", XM + 4)
        dtx_ready = sig("dtx_ready", 1)
        dte_ready = sig("dte_ready", 1)
        dtl_ready = sig("dtl_ready", 1)
        da_ready = sig("da_ready", 1)
        cs_ps = sig("cs_ps", 1)
        csum_ready = sig("csum_ready", 1)
        wdiff_ready = sig("wdiff_ready", 1)
        lndt_ready = sig("lndt_ready", 1)
        ncs_ready = sig("ncs_ready", 1)
        cexp_ready = sig("cexp_ready", 1)
        wexp_ready = sig("wexp_ready", 1)
        wend_ready = sig("wend_ready", 1)
        xt_ps = sig("xt_ps", NCH)
        xt_copied = sig("xt_copied", NCH)
        cb_ps = sig("cb_ps", NCH)
        cbt_copied = sig("cbt_copied", NCH)
        row_ps = sig("row_ps", NCH * NRB)
        row_exp = sig("row_exp", NCH * NRB)
        att_ready = sig("att_ready", 2 * NCH)
        xw_ready = sig("xw_ready", NCH - 1)
        state_ps = sig("state_ps", NCH - 1)
        inter_ps = sig("inter_ps", NCH - 1)
        state_ready = sig("state_ready", NCH - 1)
        yint_ready = sig("yint_ready", NCH - 1)
        y_ps = sig("y_ps", NCH)
        y0_ready = sig("y0_ready", NCH)
        lve_ready = sig("lve_ready", NCH)
        lrs_ready = sig("lrs_ready", NCH)
        ynorm_ready = sig("ynorm_ready", NCH)
        yt_ps = sig("yt_ps", NCH)
        yt_made = sig("yt_made", NCH)
        z_ps = sig("z_ps", NCH)
        gated = sig("gated", NCH)
        o0_ps = sig("o0_ps", NCH)
        x1_ready = sig("x1_ready", 2 * NCH)
        p1_ps = sig("p1_ps", 10)
        p1_copied = sig("p1_copied", 10)
        spe_ready = sig("spe_ready", 2)
        spl_ready = sig("spl_ready", 2)
        delta_ready = sig("delta_ready", 2)
        u1_first = sig("u1_first", 1)
        u1_second = sig("u1_second", 1)
        kept_first = sig("kept_first", 16 * 6)
        kept_second = sig("kept_second", 16 * 2)
        delta_read = [sig(f"delta_read{k}", 16 * UNITS // RING) for k in range(RING)]
        u_read = [sig(f"u_read{k}", 16 * UNITS // RING) for k in range(RING)]
        w_made = sig("w_made", UNITS)
        decay_ready = sig("decay_ready", UNITS)
        scanned = sig("scanned", UNITS)
        carried = sig("carried", NDG)
        hc_ready = sig("hc_ready", UNITS)
        y_sum_ps = sig("y_sum_ps", UNITS)
        y1_copied = sig("y1_copied", 2 * YQ)
        y1t_ps = sig("y1t_ps", NCH)
        y1t_made = sig("y1t_made", NCH)
        o1_ps = sig("o1_ps", NCH)
        out_ready = sig("out_ready", 2 * NCH)
        stored = sig("stored", 32)

        dve_steps = sig("dve_steps", DVE_STEPS)
        act_steps = sig("act_steps", ACT_STEPS)
        dve_mid_steps = sig("dve_mid_steps", DVE_MID_STEPS)
        act_mid_steps = sig("act_mid_steps", ACT_MID_STEPS)

        block = ctx.enter_context(nc.Block())

        def bc(ap, shape):
            return ap.to_broadcast(shape)

        def chunk_at(s, stage):
            c, odd = divmod(s - SSD_AT - stage, 2)
            return c if not odd and 0 <= c < NCH else -1

        def passes(eng, run):
            run(-1, 1, False, False, True)
            run(0, 0, True, False, True)
            with eng.Fori(0, (B - 2) // 2) as i:
                run(2 * i + 1, 1, True, True, True)
                run(2 * i + 2, 0, True, True, True)
            run(B - 1, 1, True, True, False)
            run(B, 0, False, True, False)

        nat0 = attv[:, 0:7 * C].rearrange("p (r c) -> p r c", c=C)
        nato = attv[:, 7 * C:11 * C].rearrange("p (r c) -> p r c", c=DI)
        natp = attv[:, 11 * C:15 * C].rearrange("p (r c) -> p r c", c=C)
        natw = y0[:, 0, :].rearrange("p (r c) -> p r c", c=C)
        jobs = []
        for r in range(7):
            n = min(P, PROJ0 - r * P)
            parts = [(0, n, r * P if r < 3 else ZD + (r - 3) * P)]
            if r == 6:
                parts = [(0, 2 * NS, ZD + DI), (2 * NS, NH, DI)]
            for c0, kn, dst in ((0, P, wt0a), (P, CB_, wt0b)):
                jobs.append((nat0[0:n, r, c0:c0 + kn], n, kn, [(dst[0:kn, d:d + w], s, w) for s, w, d in parts]))
        for r in range(2):
            n = P if r == 0 else CB_
            for m in range(XM):
                jobs.append((nato[0:n, r, m * P:(m + 1) * P], n, P, [(wo0[:, m, r * P:r * P + n], 0, n)]))
        for r in range(4):
            n = min(P, PROJ1 - r * P)
            for c0, kn, dst in ((0, P, wt1a), (P, CB_, wt1b)):
                outs = [(dst[0:kn, r * P:r * P + n], 0, n)]
                if r == 3:
                    outs = [(dst[0:kn, d:d + P].rearrange("p (n d) -> p n d", d=DG), s0, S1) for s0, d in ((0, COL_B), (S1, COL_C))]
                jobs.append((natp[0:n, r, c0:c0 + kn], n, kn, outs))
        for r in range(2):
            n = P if r == 0 else CB_
            for c0, kn, dst in ((0, P, wo1a), (P, CB_, wo1b)):
                outs = [(dst[k0:k0 + kn, r * P:r * P + n], 0, n) for k0 in ((0,) if kn == P else (0, CB_))]
                jobs.append((natw[0:n, r, c0:c0 + kn], n, kn, outs))
        copies = []
        total = 0
        for j in jobs:
            total += len(j[3])
            copies.append(total)

        @block.sync
        def _(sp):
            n = [0]

            def load(dst, src):
                sp.dma_start(dst, src, allow_slow_non_contiguous=True).then_inc(s_wload, 16)
                n[0] += 1

            def load_x(k):
                sp.dma_start(xa[:, :], x_d[k, 0:P, :]).then_inc(x_loaded.sem, 16)
                sp.dma_start(xb[:, :], x_d[k, P:C, :]).then_inc(x_loaded.sem, 16)

            load_x(0)
            load(nat0[:, 0:6, :], inw_d[0:6 * P, :].rearrange("(r p) c -> p r c", p=P))
            load(nat0[0:PROJ0 - 6 * P, 6, :], inw_d[6 * P:PROJ0, :])
            load(nato[:, 0, :], outw_d[0:P, :])
            load(nato[0:CB_, 1, :], outw_d[P:C, :])
            load(natp[:, 0:3, :], wp_d[0:3 * P, :].rearrange("(r p) c -> p r c", p=P))
            load(natp[0:PROJ1 - 3 * P, 3, :], wp_d[3 * P:PROJ1, :])
            load(natw[:, 0, :], wo_d[0:P, :])
            load(natw[0:CB_, 1, :], wo_d[P:C, :])
            load(cw[:, 0:XM, :], cw_d[0:DI, :].rearrange("(m p) t -> p m t", p=P))
            load(cb[:, 0:XM], cb_d[0:DI].rearrange("(m p) -> p m", p=P))
            for h in range(2):
                load(cw[h * 2 * NS:(h + 1) * 2 * NS, XM, :], cw_d[DI:CONVD, :])
                load(cb[h * 2 * NS:(h + 1) * 2 * NS, XM:XM + 1], cb_d[DI:CONVD].rearrange("(p a) -> p a", a=1))
            load(dtb[:, :], dtb_d.partition_broadcast(P))
            load(aneg0[:, :], alog0_d.partition_broadcast(P))
            for h in range(NH):
                load(dcol[(h % 4) * HD:(h % 4 + 1) * HD, h // 4:h // 4 + 1], d0_d[h:h + 1].partition_broadcast(HD))
            load(nwc[:, :], nw_d.rearrange("(m p) -> p m", p=P))
            load(nbc[:, :], nb_d.rearrange("(m p) -> p m", p=P))
            for s in range(S1):
                load(aneg1[s * DG:(s + 1) * DG, :], alog1_d.rearrange("(g d) n -> n d g", d=DG)[s, :, :])
            load(d1c[:, 0:1], d1_d[0:P].rearrange("(p a) -> p a", a=1))
            for h in range(2):
                load(d1c[h * CB_:(h + 1) * CB_, 1:2], d1_d[P:C].rearrange("(p a) -> p a", a=1))
            sp.wait_ge(s_const, 1)
            load(boc[:, 0:1], bo_d[0:P].rearrange("(p a) -> p a", a=1))
            load(boc[0:CB_, 1:2], bo_d[P:C].rearrange("(p a) -> p a", a=1))
            bp = bp_d.rearrange("(a n) -> a n", a=1)
            load(wt1b[CB_:CB_ + 1, 0:2 * C], bp[:, 0:2 * C])
            load(bbc[CB_:CB_ + 1, :], bp[:, 2 * C:2 * C + 2 * S1])
            load(wt1b[CB_ + 1:CB_ + 2, COL_D:COL_D + C], dtb1_d.rearrange("(a n) -> a n", a=1))
            assert n[0] == NLOADS, n

            def keep(par, which, src, piece, done):
                if piece == MID:
                    for h in range(2):
                        sp.dma_start(scratch[par, which, P:C, h * HALF:(h + 1) * HALF],
                                     src[h * CB_:(h + 1) * CB_, MID, :]).then_inc(done.sem, 16)
                else:
                    h = piece // 2
                    sp.dma_start(scratch[par, which, 0:P, h * HALF:(h + 1) * HALF], src[:, piece, :]).then_inc(done.sem, 16)

            def read_repeated(b, i, par, prev):
                hf, g = i // NDG, i % NDG
                if i == 0:
                    sp.wait_ge(kept_first.sem, kept_first.at(b, 16 * 6))
                elif i >= RING or prev:
                    sp.wait_ge(scanned.sem, scanned.at(b, i - RING + 1))
                for which, (dst, read) in enumerate(((drep, delta_read), (urep, u_read))):
                    if which == 1 and i == NDG - 1:
                        sp.wait_ge(kept_second.sem, kept_second.at(b, 16 * 2))
                    src = scratch[par, which, g * DG:(g + 1) * DG, hf * HALF:(hf + 1) * HALF]
                    sp.dma_start(dst[:, i % RING, :], bc(src.unsqueeze(0), [S1, DG, HALF])).then_inc(read[i % RING].sem, 16)

            def traffic(b, par, scan, end, first, load_next):
                for s in range(SLOTS):
                    if end and s == TAIL_AT + NCH + RING:
                        sp.wait_ge(out_ready.sem, out_ready.at(b - 1, 2 * NCH))
                        sp.dma_start(out_d[b - 1, 0:P, :], x1a[1 - par][:, :]).then_inc(stored.sem, 16)
                        sp.dma_start(out_d[b - 1, P:C, :], x1b[1 - par][:, :]).then_inc(stored.sem, 16)
                    if scan:
                        if s == MID_STORE_AT:
                            sp.wait_ge(delta_ready.sem, delta_ready.at(b, 2))
                            keep(par, 0, delta, 2, kept_second)
                            sp.wait_ge(u1_second.sem, u1_second.at(b, 1))
                            keep(par, 1, u1, 2, kept_second)
                        read_repeated(b, s, par, end)
                    if load_next and s == PRE_AT + RING:
                        sp.wait_ge(x1_ready.sem, x1_ready.at(b + 1, 2 * NCH))
                        load_x(b + 2)
                if first:
                    sp.wait_ge(delta_ready.sem, delta_ready.at(b + 1, 1))
                    for piece in (0, MID):
                        keep(1 - par, 0, delta, piece, kept_first)
                    sp.wait_ge(u1_first.sem, u1_first.at(b + 1, 1))
                    for piece in (0, MID):
                        keep(1 - par, 1, u1, piece, kept_first)

            traffic(-1, 1, False, False, True, True)
            traffic(0, 0, True, False, True, True)
            with sp.Fori(0, (B - 4) // 2) as i:
                traffic(2 * i + 1, 1, True, True, True, True)
                traffic(2 * i + 2, 0, True, True, True, True)
            traffic(B - 3, 1, True, True, True, True)
            traffic(B - 2, 0, True, True, True, False)
            traffic(B - 1, 1, True, True, False, False)
            traffic(B, 0, False, True, False, False)
            sp.wait_ge(stored.sem, B * 32)

        @block.gpsimd
        def _(pool):
            done = [0]

            def made_before(ins):
                done[0] += 1
                ins.then_inc(s_pool, 1)
                pool.wait_ge(s_pool, done[0])

            made_before(nc.gpsimd.memset(wt1b[CB_:CB_ + 2, :], 0.0))
            nc.gpsimd.memset(boc[:, :], 0.0).then_inc(s_const, 1)
            pool.wait_ge(s_const, 1)
            made_before(nc.gpsimd.memset(xnb[CB_:CB_ + 2, :], 1.0))
            for t in (ident, identb, maskneg):
                made_before(nc.gpsimd.memset(t[:, :], 0.0))
            for t in (upper, ones, ga, gb):
                made_before(nc.gpsimd.memset(t[:, :], 1.0))
            made_before(nc.gpsimd.memset(neghalf[:, :], -0.5))
            made_before(nc.gpsimd.memset(mv[:, :, :], 0.0))
            for t in cpad + [bcpad]:
                made_before(nc.gpsimd.memset(t[:, :, :], 0.0))
            for t in (ident, identb):
                made_before(nc.gpsimd.affine_select(out=t[:, :], in_=t[:, :], compare_op=ALU.not_equal, fill=1.0,
                                                    base=0, pattern=[[-1, P]], channel_multiplier=1))
            made_before(nc.gpsimd.affine_select(out=upper[:, :], in_=upper[:, :], compare_op=ALU.is_ge, fill=0.0,
                                                base=0, pattern=[[1, P]], channel_multiplier=-1))
            made_before(nc.gpsimd.affine_select(out=maskneg[:, :], in_=maskneg[:, :], compare_op=ALU.is_ge,
                                                fill=MASKED, base=0, pattern=[[1, P]], channel_multiplier=-1))
            for t, off in ((ga, 0), (gb, P)):
                v = t[:, :].rearrange("p (q r) -> p q r", r=GROUP)
                made_before(nc.gpsimd.affine_select(out=v, in_=v, compare_op=ALU.is_ge, fill=0.0, base=off,
                                                    pattern=[[-GROUP, 43], [0, GROUP]], channel_multiplier=1))
                made_before(nc.gpsimd.affine_select(out=v, in_=v, compare_op=ALU.is_ge, fill=0.0,
                                                    base=GROUP - 1 - off,
                                                    pattern=[[GROUP, 43], [0, GROUP]], channel_multiplier=-1))
            nc.gpsimd.memset(carry[:, :], 0.0).then_inc(s_const, 1)
            pool.wait_ge(s_const, 2)
            pool.wait_ge(s_prep, PREPS)

            def group_rstd(n, g):
                pool.wait_ge(gve_ready.sem, gve_ready.at(n, g + 1))
                nc.gpsimd.tensor_tensor(gr[:, :], gv[:, :], neghalf[:, :], ALU.pow).then_inc(grstd_ready.sem, 1)

            def scaled_x(n, c):
                pool.wait_ge(xt_copied.sem, xt_copied.at(n, c + 1))
                if c == 0:
                    pool.wait_ge(wend_ready.sem, wend_ready.at(n, 1))
                if c >= 2:
                    pool.wait_ge(state_ps.sem, state_ps.at(n, c - 1))
                nc.gpsimd.tensor_tensor(xw[:, c % 2, :].rearrange("p (h d) -> p h d", d=HD),
                                        xtok[:, c % 2, 0:DI].rearrange("p (h d) -> p h d", d=HD),
                                        bc(wend[:, c, :].unsqueeze(2), [P, NH, HD]), ALU.mult).then_inc(xw_ready.sem, 1)

            def attention(n, c, h0, h1):
                pool.wait_ge(row_exp.sem, row_exp.at(n, NRB * c + h1 // HPB))
                pool.wait_ge(cbt_copied.sem, cbt_copied.at(n, c + 1))
                a = att[:, c % 2, h0:h1, :]
                nc.gpsimd.tensor_tensor(a, a, bc(cbt[:, c % 2, :].unsqueeze(1), [P, h1 - h0, Q]),
                                        ALU.mult).then_inc(att_ready.sem, 1)

            def layer_rstd(n, c):
                pool.wait_ge(lve_ready.sem, lve_ready.at(n, c + 1))
                nc.gpsimd.tensor_tensor(lrs[:, c % 2:c % 2 + 1], lve[:, c % 2:c % 2 + 1], neghalf[:, 0:1],
                                        ALU.pow).then_inc(lrs_ready.sem, 1)

            def first_block(n, s):
                if s == 3:
                    group_rstd(n, 0)
                c = chunk_at(s, 1)
                if c >= 0:
                    if c < NCH - 1:
                        scaled_x(n, c)
                    attention(n, c, 0, HPB)
                c = chunk_at(s, 2)
                if c >= 0:
                    attention(n, c, HPB, NH)
                c = chunk_at(s, 4)
                if c >= 0:
                    layer_rstd(n, c)
                if s == PRE_AT + 3:
                    group_rstd(n, 1)

            def second_half(n, s, par):
                if s == 4:
                    pool.wait_ge(delta_ready.sem, delta_ready.at(n, 2))
                    nc.gpsimd.tensor_tensor(u1[:, 2, :], delta[:, 2, :], xcm[par][:, 2, :], ALU.mult).then_inc(u1_second.sem, 1)

            def states_by_c(n, i, par, prev):
                hf = i // NDG
                pool.wait_ge(scanned.sem, scanned.at(n, i + 1))
                if i == 0:
                    pool.wait_ge(p1_copied.sem, p1_copied.at(n, EARLY))
                if i == NDG:
                    pool.wait_ge(p1_copied.sem, p1_copied.at(n, 10))
                if i >= 2 or prev:
                    pool.wait_ge(y_sum_ps.sem, y_sum_ps.at(n, i - 1))
                nc.gpsimd.tensor_tensor(hc[:, i % 2, :], hst[:, i % 3, :], crep[par][:, hf * HALF:(hf + 1) * HALF],
                                        ALU.mult).then_inc(hc_ready.sem, 1)

            def run(b, par, scan, end, first):
                for s in range(SLOTS if scan or first else 2):
                    if s < 2:
                        if end:
                            states_by_c(b - 1, UNITS - 2 + s, 1 - par, False)
                    elif scan:
                        states_by_c(b, s - 2, par, end)
                    if scan:
                        second_half(b, s, par)
                    if first:
                        first_block(b + 1, s)

            passes(pool, run)

        @block.scalar
        def _(act):
            nc.scalar.preload_act_table_set(EXP_LN)
            for j, (_, n, kn, outs) in enumerate(jobs):
                act.wait_ge(s_wps, j + 1)
                for dst, s, w in outs:
                    src = bank[j % 8][0:kn, s:s + w]
                    if len(dst.shape) == 3:
                        src = bc(src.unsqueeze(2), [kn, w, DG])
                    nc.scalar.copy(dst, src).then_inc(s_wev, 1)
            act.wait_ge(s_wload, 16 * NLOADS)
            for s0, d in ((0, COL_B), (S1, COL_C)):
                nc.scalar.copy(wt1b[CB_:CB_ + 1, d:d + P].rearrange("p (n d) -> p n d", d=DG),
                               bc(bbc[CB_:CB_ + 1, s0:s0 + S1].unsqueeze(2), [1, S1, DG])).then_inc(s_wev, 1)
            nc.scalar.activation(aneg0[:, :], aneg0[:, :], ACT.Exp).then_inc(s_wev, 1)
            nc.scalar.activation(aneg1[:, :], aneg1[:, :], ACT.Exp).then_inc(s_wev, 1)
            act.wait_ge(s_prep, PREPS)

            def copy_fill(n, k):
                ps = bank[FILL_BANKS[k % 3]]
                act.wait_ge(fill_ps.sem, fill_ps.at(n, k + 1))
                if k == 6:
                    ins = nc.scalar.copy(dtx[:, :, :].rearrange("p c h -> p (c h)"), ps[:, 0:NCH * NH])
                elif k == 4:
                    ins = nc.scalar.copy(bcpad[:, 1:17, 1:W + 1], ps[:, :].rearrange("p (r w) -> p r w", w=W))
                elif k == 5:
                    nc.scalar.copy(bcpad[0:64, 17, 1:W + 1], ps[0:64, 0:W])
                    ins = nc.scalar.copy(bcpad[64:P, 0, 1:W + 1], ps[64:P, 0:W])
                else:
                    m, h = FILL_TILES[k]
                    if m == 2:
                        act.wait_ge(conv_done.sem, conv_done.at(n, 1))
                    ins = nc.scalar.copy(cpad[m % 2][:, 1 + 16 * h:17 + 16 * h, 1:W + 1],
                                         ps[:, :].rearrange("p (r w) -> p r w", w=W))
                ins.then_inc(fill_copied.sem, 1)

            def exp_rows(n, c, r):
                act.wait_ge(row_ps.sem, row_ps.at(n, NRB * c + r + 1))
                if r == 0 and c == 0:
                    act.wait_ge(ncs_ready.sem, ncs_ready.at(n, 1))
                if r == 0 and c >= 2:
                    act.wait_ge(y_ps.sem, y_ps.at(n, c - 1))
                for k in range(HPB):
                    h = HPB * r + k
                    ins = nc.scalar.activation(att[:, c % 2, h, :], bank[ROW_BANKS[r]][:, k * Q:(k + 1) * Q], ACT.Exp,
                                               bias=ncs[:, c, h:h + 1])
                ins.then_inc(row_exp.sem, 1)

            def first_block(n, s, step, par, last, again):
                for k, at in enumerate(FILL_AT):
                    if s == at + 1:
                        copy_fill(n, k)
                if s == 10:
                    act.wait_ge(dtx_ready.sem, dtx_ready.at(n, 1))
                    step(nc.scalar.activation(dte[:, :, :], dtx[:, :, :], ACT.Abs))
                    nc.scalar.activation(dte[:, :, :], dte[:, :, :], ACT.Exp, scale=-1.0).then_inc(dte_ready.sem, 1)
                    act.wait_ge(dte_ready.sem, dte_ready.at(n, 1))
                    nc.scalar.activation(dtl[:, :, :], dte[:, :, :], ACT.Ln, bias=1.0).then_inc(dtl_ready.sem, 1)
                if s == 12:
                    act.wait_ge(csum_ready.sem, csum_ready.at(n, 1))
                    nc.scalar.activation(lndt[:, :, :], lndt[:, :, :], ACT.Ln).then_inc(lndt_ready.sem, 1)
                    nc.scalar.activation(cexp[:, :, :, :], csum[:, :, :, :], ACT.Exp).then_inc(cexp_ready.sem, 1)
                    nc.scalar.activation(wend[:, :, :], wend[:, :, :], ACT.Exp).then_inc(wexp_ready.sem, 1)
                if s == SILU_AT[0]:
                    act.wait_ge(conv_done.sem, conv_done.at(n, 3))
                    for m in range(2):
                        nc.scalar.activation(xs[m][:, :], xs[m][:, :], ACT.Silu, bias=cb[:, m:m + 1]).then_inc(silu_done.sem, 1)
                    for h in range(2):
                        for k, dst in enumerate((bs, cs_)):
                            r = 64 * h + NS * k
                            nc.scalar.activation(dst[:, h * HALF:(h + 1) * HALF], bcacc[r:r + NS, :], ACT.Silu,
                                                 bias=cb[r:r + NS, XM:XM + 1]).then_inc(silu_done.sem, 1)
                    nc.scalar.preload_act_table_set(EXP_LN)
                if s == SILU_AT[1]:
                    act.wait_ge(conv_done.sem, conv_done.at(n, 4))
                    nc.scalar.activation(xs[2][:, :], xs[2][:, :], ACT.Silu, bias=cb[:, 2:3]).then_inc(silu_done.sem, 1)
                    nc.scalar.preload_act_table_set(EXP_LN)
                c = chunk_at(s, 6)
                if c >= 0:
                    act.wait_ge(yt_ps.sem, yt_ps.at(n, c + 1))
                    if c >= 2:
                        act.wait_ge(o0_ps.sem, o0_ps.at(n, c - 1))
                    for m in range(XM):
                        ins = nc.scalar.activation(yzt[:, c % 2, m, :], bank[B_CBT][:, (m + 1) * Q:(m + 2) * Q],
                                                   ACT.Identity, bias=nbc[:, m:m + 1], scale=nwc[:, m:m + 1])
                    ins.then_inc(yt_made.sem, 1)
                c = chunk_at(s, 2)
                if c >= 0:
                    exp_rows(n, c, 1)
                    exp_rows(n, c, 2)
                c = chunk_at(s, 1)
                if c >= 0:
                    exp_rows(n, c, 0)
                    act.wait_ge(xt_ps.sem, xt_ps.at(n, c + 1))
                    if c >= 2:
                        act.wait_ge(xw_ready.sem, xw_ready.at(n, c - 1))
                        act.wait_ge(state_ps.sem, state_ps.at(n, c - 1))
                    nc.scalar.copy(xtok[:, c % 2, :], bank[B_XY][:, 0:DI + NS]).then_inc(xt_copied.sem, 1)
                    act.wait_ge(cb_ps.sem, cb_ps.at(n, c + 1))
                    if c >= 2:
                        act.wait_ge(att_ready.sem, att_ready.at(n, 2 * (c - 1)))
                    nc.scalar.copy(cbt[:, c % 2, :], bank[B_CBT][:, 0:Q]).then_inc(cbt_copied.sem, 1)
                for k in range(EARLY):
                    if s == PRE_AT + P1_AT[k] + 1:
                        copy_projected(n, k, par, last, again)
                if s == PRE_AT + 5:
                    softplus_parts(n, 0, step)

            def copy_projected(n, k, par, last, again):
                act.wait_ge(p1_ps.sem, p1_ps.at(n, k + 1))
                if k == 0 and last:
                    act.wait_ge(kept_second.sem, kept_second.at(n - 1, 16 * 2))
                if k == 0 and again:
                    act.wait_ge(y1t_made.sem, y1t_made.at(n - 2, NCH))
                    act.wait_ge(hc_ready.sem, hc_ready.at(n - 2, UNITS))
                what, h = P1_TILES[k]
                dst = {"dA": delta[:, PIECE[h], :], "dB": delta[:, MID, :], "xA": xcm[par][:, PIECE[h], :],
                       "xB": xcm[par][:, MID, :], "B": brep[par][:, h * HALF:(h + 1) * HALF],
                       "C": crep[par][:, h * HALF:(h + 1) * HALF]}[what]
                nc.scalar.copy(dst, bank[P1_BANKS[k]][:, :]).then_inc(p1_copied.sem, 1)

            def softplus_parts(n, h, step):
                cc = slice(0, 2) if h == 0 else slice(2, 3)
                act.wait_ge(p1_copied.sem, p1_copied.at(n, 2 if h == 0 else EARLY + 1))
                act.wait_ge(y_ps.sem, y_ps.at(n, NCH))
                step(nc.scalar.activation(sp_e[:, cc, :], delta[:, cc, :], ACT.Abs))
                nc.scalar.activation(sp_e[:, cc, :], sp_e[:, cc, :], ACT.Exp, scale=-1.0).then_inc(spe_ready.sem, 1)
                act.wait_ge(spe_ready.sem, spe_ready.at(n, h + 1))
                nc.scalar.activation(sp_l[:, cc, :], sp_e[:, cc, :], ACT.Ln, bias=1.0).then_inc(spl_ready.sem, 1)

            def second_half(n, s, par, step):
                for k in (EARLY, EARLY + 1):
                    if s == 1:
                        copy_projected(n, k, par, False, False)
                if s == 1:
                    softplus_parts(n, 1, step)
                for k in (EARLY + 2, EARLY + 3):
                    if s == 2 + k - EARLY - 2:
                        copy_projected(n, k, par, False, False)

            def copy_y(n, q, prev):
                hf, k = q // YQ, q % YQ
                act.wait_ge(y_sum_ps.sem, y_sum_ps.at(n, YG * (q + 1)))
                if q == 0 and prev:
                    act.wait_ge(y1t_ps.sem, y1t_ps.at(n - 1, NCH))
                nc.scalar.copy(y1[:, CPH * hf:CPH * (hf + 1), k * YG * DG:(k + 1) * YG * DG],
                               bank[B_YSUM][:, 0:CPH * YG * DG].rearrange("p (c d) -> p c d", d=YG * DG)).then_inc(y1_copied.sem, 1)

            def run(b, par, scan, end, first):
                step = Steps(act, act_steps, b + 1)
                mid_step = Steps(act, act_mid_steps, b)
                for s in range(SLOTS if scan or first else TAIL_AT + NCH + 1):
                    if scan:
                        second_half(b, s, par, mid_step)
                    if first:
                        first_block(b + 1, s, step, 1 - par, scan, end)
                    if scan:
                        read = delta_read[s % RING]
                        act.wait_ge(read.sem, read.at(b, 16 * (s // RING + 1)))
                        if s >= 2 or end:
                            act.wait_ge(scanned.sem, scanned.at(b, s - 1))
                        g = s % NDG
                        nc.scalar.activation(decay[:, s % 2, :], drep[:, s % RING, :], ACT.Exp,
                                             scale=aneg1[:, g:g + 1]).then_inc(decay_ready.sem, 1)
                        if 2 <= s < NDG + 2:
                            act.wait_ge(scanned.sem, scanned.at(b, s - 1))
                            nc.scalar.copy(carry[:, s - 2:s - 1], hst[:, (s - 2) % 3, HALF - 1:HALF]).then_inc(carried.sem, 1)
                        for q in range(2 * YQ - 1):
                            if s == YG * (q + 1) + 2:
                                copy_y(b, q, end)
                    if end:
                        if s == 2:
                            copy_y(b - 1, 2 * YQ - 1, False)
                assert not first or step.done == ACT_STEPS, step.done

            passes(act, run)

        @block.vector
        def _(dve):
            dve.wait_ge(s_const, 2)
            nc.vector.tensor_reduce(sel[:, :], ident[:, :].rearrange("p (n d) -> p d n", d=DG), AX_X, ALU.add).then_inc(s_prep, 1)
            dve.wait_ge(s_wload, 16 * NLOADS)
            for m in range(XM):
                nc.vector.tensor_scalar(diagd[:, m, :], ident[:, :], dcol[:, m:m + 1], None, ALU.mult).then_inc(s_prep, 1)
            dve.wait_ge(s_wev, copies[-1] + 4)
            nc.vector.tensor_scalar(aneg0[:, :], aneg0[:, :], -1.0, None, ALU.mult).then_inc(s_prep, 1)
            nc.vector.tensor_scalar(aneg1[:, :], aneg1[:, :], -1.0, None, ALU.mult).then_inc(s_prep, 1)
            dve.wait_ge(s_prep, PREPS)

            def channel_stats(t, k, n, h):
                return nc.vector.bn_stats(st[0:n, k, h, :], t[:, h * HALF:(h + 1) * HALF])

            def channel_moments():
                nc.vector.memset(spare[:, :], 0.0)
                nc.vector.bn_aggr(mv[:, 0, :], st[:, 0, :, :].rearrange("p a s -> p (a s)")).then_inc(stats_ready.sem, 1)
                nc.vector.bn_aggr(mv[0:CB_, 1, :], st[0:CB_, 1, :, :].rearrange("p a s -> p (a s)")).then_inc(stats_ready.sem, 1)

            def group_deviation(n, g, step):
                dve.wait_ge(gmean_ps.sem, gmean_ps.at(n, g + 1))
                step(nc.vector.tensor_scalar(gm[:, :], bank[3][:, 0:2], 1.0 / GROUP, None, ALU.mult))
                step(nc.vector.tensor_tensor(gd[:, :], mv[:, :, 0], gm[:, :], ALU.subtract))
                step(nc.vector.tensor_tensor(gd[:, :], gd[:, :], gd[:, :], ALU.mult))
                nc.vector.tensor_tensor(gq[:, :], gd[:, :], mv[:, :, 1], ALU.add).then_inc(gdev_ready.sem, 1)

            def group_variance(n, g):
                dve.wait_ge(gvar_ps.sem, gvar_ps.at(n, g + 1))
                nc.vector.tensor_scalar(gv[:, :], bank[4][:, 0:2], 1.0 / GROUP, GEPS, ALU.mult, ALU.add).then_inc(gve_ready.sem, 1)

            def normalise_groups(n, g, ta, tb):
                dve.wait_ge(grstd_ready.sem, grstd_ready.at(n, g + 1))
                nc.vector.tensor_scalar(xna[:, :], ta, gm[:, 0:1], gr[:, 0:1], ALU.subtract, ALU.mult).then_inc(xn_ready.sem, 1)
                nc.vector.tensor_scalar(xnb[0:CB_, :], tb, gm[0:CB_, 1:2], gr[0:CB_, 1:2],
                                        ALU.subtract, ALU.mult).then_inc(xn_ready.sem, 1)

            def conv_tap(n, k, step):
                o, t = k // 9, k % 9
                m = (0, 1, XM, 2)[o]
                image, acc, rows = ((cpad[m % 2], xs[m], H) if m < XM else (bcpad, bcacc, H // 2))
                if t == 0:
                    dve.wait_ge(fill_copied.sem, fill_copied.at(n, (2, 4, 6, 9)[o]))
                accv = acc[:, :].rearrange("p (r w) -> p r w", w=W)
                win = image[:, t // 3:t // 3 + rows, t % 3:t % 3 + W]
                if t == 0:
                    ins = nc.vector.tensor_scalar(accv, win, cw[:, m, 0:1], None, ALU.mult)
                else:
                    ins = nc.vector.scalar_tensor_tensor(accv, win, cw[:, m, t:t + 1], accv, ALU.mult, ALU.add)
                if t < 8:
                    step(ins)
                else:
                    ins.then_inc(conv_done.sem, 1)

            def softplus(v, e, l, u, out, step):
                step(nc.vector.tensor_scalar(u, e, 1.0, None, ALU.add))
                step(nc.vector.scalar_tensor_tensor(u, u, -1.0, e, ALU.add, ALU.subtract))
                step(nc.vector.tensor_tensor(u, l, u, ALU.subtract))
                return nc.vector.scalar_tensor_tensor(out, v, 0.0, u, ALU.max, ALU.add)

            def carry_state(n, c, step):
                sv = state[:, :].rearrange("p (h d) -> p h d", d=HD)
                dve.wait_ge(state_ps.sem, state_ps.at(n, c + 1))
                if c == 0:
                    nc.vector.tensor_copy(state[:, :], bank[B_STATE][0:NS, 0:DI]).then_inc(state_ready.sem, 1)
                    return
                step(nc.vector.tensor_tensor(sv, sv, bc(cexp[0:NS, 1, c, :].unsqueeze(2), [NS, NH, HD]), ALU.mult))
                nc.vector.tensor_tensor(state[:, :], state[:, :], bank[B_STATE][0:NS, 0:DI], ALU.add).then_inc(state_ready.sem, 1)

            def from_state(n, c):
                dve.wait_ge(inter_ps.sem, inter_ps.at(n, c))
                nc.vector.tensor_tensor(yint[:, c % 2, :].rearrange("p (h d) -> p h d", d=HD),
                                        bank[B_STATE][:, 0:DI].rearrange("p (h d) -> p h d", d=HD),
                                        bc(cexp[:, 0, c, :].unsqueeze(2), [P, NH, HD]), ALU.mult).then_inc(yint_ready.sem, 1)

            def chunk_output(n, c, step):
                dve.wait_ge(y_ps.sem, y_ps.at(n, c + 1))
                if c >= 2:
                    dve.wait_ge(yt_ps.sem, yt_ps.at(n, c - 1))
                if c == 0:
                    ins = nc.vector.tensor_copy(y0[:, 0, :], bank[B_XY][:, 0:DI])
                else:
                    dve.wait_ge(yint_ready.sem, yint_ready.at(n, c))
                    ins = nc.vector.tensor_tensor(y0[:, c % 2, :], yint[:, c % 2, :], bank[B_XY][:, 0:DI], ALU.add)
                ins.then_inc(y0_ready.sem, 1)
                dve.wait_ge(y0_ready.sem, y0_ready.at(n, c + 1))
                step(nc.vector.bn_stats(lst[:, c % 2, :], y0[:, c % 2, :]))
                nc.vector.memset(spare[:, :], 0.0)
                step(nc.vector.bn_aggr(lmv[:, c % 2, :], lst[:, c % 2, :]))
                nc.vector.tensor_scalar(lve[:, c % 2:c % 2 + 1], lmv[:, c % 2, 1:2], LEPS, None, ALU.add).then_inc(lve_ready.sem, 1)

            def normalise(n, c):
                dve.wait_ge(lrs_ready.sem, lrs_ready.at(n, c + 1))
                nc.vector.tensor_scalar(y0[:, c % 2, :], y0[:, c % 2, :], lmv[:, c % 2, 0:1], lrs[:, c % 2:c % 2 + 1],
                                        ALU.subtract, ALU.mult).then_inc(ynorm_ready.sem, 1)

            def gate(n, c):
                dve.wait_ge(yt_made.sem, yt_made.at(n, c + 1))
                dve.wait_ge(z_ps.sem, z_ps.at(n, c + 1))
                yz = yzt[:, c % 2, :, :].rearrange("p m q -> p (m q)")
                nc.vector.tensor_tensor(yz, yz, bank[B_GATE][:, 0:DI], ALU.mult).then_inc(gated.sem, 1)

            def residual(n, c, par):
                dve.wait_ge(o0_ps.sem, o0_ps.at(n, c + 1))
                t = slice(c * Q, (c + 1) * Q)
                nc.vector.tensor_tensor(x1a[par][:, t], bank[B_OUT][:, 0:Q], xa[:, t], ALU.add).then_inc(x1_ready.sem, 1)
                nc.vector.tensor_tensor(x1b[par][:, t], bank[B_OUT][0:CB_, Q:2 * Q], xb[:, t], ALU.add).then_inc(x1_ready.sem, 1)

            def first_block_soon(n, s, step, par, last, again):
                if s == 2:
                    group_deviation(n, 0, step)
                if s == 3:
                    group_variance(n, 0)
                if s == 4:
                    if last:
                        dve.wait_ge(p1_ps.sem, p1_ps.at(n - 1, 10))
                    normalise_groups(n, 0, xa[:, :], xb[:, :])
                if s == 9:
                    dve.wait_ge(fill_copied.sem, fill_copied.at(n, 7))
                    nc.vector.tensor_tensor(dtx[:, :, :], dtx[:, :, :], bc(dtb[:, :].unsqueeze(1), [P, NCH, NH]),
                                            ALU.add).then_inc(dtx_ready.sem, 1)
                if s == 11:
                    dve.wait_ge(dtl_ready.sem, dtl_ready.at(n, 1))
                    step(softplus(dtx[:, :, :], dte[:, :, :], dtl[:, :, :], dtu[:, :, :], dt0[:, :, :], step))
                    nc.vector.tensor_tensor(da0[:, :, :], dt0[:, :, :], bc(aneg0[:, :].unsqueeze(1), [P, NCH, NH]),
                                            ALU.mult).then_inc(da_ready.sem, 1)
                if s == 12:
                    step(nc.vector.tensor_scalar(lndt[:, :, :], dt0[:, :, :], TINY, None, ALU.max))
                    dve.wait_ge(cs_ps.sem, cs_ps.at(n, 1))
                    step(nc.vector.tensor_copy(csum[:, :, :, :].rearrange("p a c h -> p (a c h)"),
                                               bank[B_CSUM][:, 0:2 * NCH * NH]))
                    nc.vector.tensor_tensor(wend[:, :, :], csum[:, 1, :, :], csum[:, 0, :, :], ALU.subtract).then_inc(csum_ready.sem, 1)
                if s == 13:
                    dve.wait_ge(lndt_ready.sem, lndt_ready.at(n, 1))
                    nc.vector.tensor_tensor(ncs[:, :, :], lndt[:, :, :], csum[:, 0, :, :], ALU.subtract).then_inc(ncs_ready.sem, 1)
                    dve.wait_ge(wexp_ready.sem, wexp_ready.at(n, 1))
                    nc.vector.tensor_tensor(wend[:, :, :], wend[:, :, :], dt0[:, :, :], ALU.mult).then_inc(wend_ready.sem, 1)
                c = chunk_at(s, 9)
                if c >= 0:
                    if c == 0 and again:
                        dve.wait_ge(stored.sem, stored.at(n - 2, 32))
                    residual(n, c, par)
                c = chunk_at(s, 3)
                if 0 <= c < NCH - 1:
                    carry_state(n, c, step)
                c = chunk_at(s, 5)
                if c >= 0:
                    normalise(n, c)
                c = chunk_at(s, 7)
                if c >= 0:
                    gate(n, c)
                c = chunk_at(s, 2)
                if c >= 1:
                    from_state(n, c)
                c = chunk_at(s, 4)
                if c >= 0:
                    chunk_output(n, c, step)
                if s == PRE_AT + 2:
                    group_deviation(n, 1, step)
                if s == PRE_AT + 3:
                    group_variance(n, 1)
                if s == PRE_AT + 4:
                    normalise_groups(n, 1, x1a[par][:, :], x1b[par][:, :])

            def first_block_later(n, s, step, par, again):
                if s == 0:
                    dve.wait_ge(x_loaded.sem, x_loaded.at(n, 32))
                    for h in range(2):
                        channel_stats(xa, 0, P, h)
                        ins = channel_stats(xb, 1, CB_, h)
                    step(ins)
                    channel_moments()
                for k in range(TAPS * (s - CONV_AT), TAPS * (s - CONV_AT + 1)):
                    if 0 <= k < 9 * (XM + 1):
                        conv_tap(n, k, step)
                c = chunk_at(s, SSD_LAST)
                if c in (CPH - 1, NCH - 1):
                    h = c // CPH
                    dve.wait_ge(x1_ready.sem, x1_ready.at(n, 2 * (c + 1)))
                    channel_stats(x1a[par], 0, P, h)
                    ins = channel_stats(x1b[par], 1, CB_, h)
                    if h:
                        step(ins)
                        channel_moments()
                if s == PRE_AT + 6:
                    softplus_piece(n, 0, step)
                if s == PRE_AT + 7:
                    dve.wait_ge(delta_ready.sem, delta_ready.at(n, 1))
                    dve.wait_ge(p1_copied.sem, p1_copied.at(n, 4))
                    nc.vector.tensor_tensor(u1[:, 0:2, :], delta[:, 0:2, :], xcm[par][:, 0:2, :], ALU.mult).then_inc(u1_first.sem, 1)

            def softplus_piece(n, h, step):
                cc = slice(0, 2) if h == 0 else slice(2, 3)
                dve.wait_ge(spl_ready.sem, spl_ready.at(n, h + 1))
                d = delta[:, cc, :]
                softplus(d, sp_e[:, cc, :], sp_l[:, cc, :], u1[:, cc, :], d, step).then_inc(delta_ready.sem, 1)

            def inputs(b, i, par):
                hf = i // NDG
                if i == 0:
                    dve.wait_ge(p1_copied.sem, p1_copied.at(b, EARLY))
                if i == NDG:
                    dve.wait_ge(p1_copied.sem, p1_copied.at(b, 10))
                read = u_read[i % RING]
                dve.wait_ge(read.sem, read.at(b, 16 * (i // RING + 1)))
                w = urep[:, i % RING, :]
                nc.vector.tensor_tensor(w, w, brep[par][:, hf * HALF:(hf + 1) * HALF], ALU.mult).then_inc(w_made.sem, 1)

            def scan_unit(n, i, prev):
                hf, g = i // NDG, i % NDG
                dve.wait_ge(decay_ready.sem, decay_ready.at(n, i + 1))
                dve.wait_ge(w_made.sem, w_made.at(n, i + 1))
                if i >= 3 or prev:
                    dve.wait_ge(hc_ready.sem, hc_ready.at(n, i - 2))
                    if 3 <= i < NDG + 3:
                        dve.wait_ge(carried.sem, carried.at(n, i - 2))
                if hf:
                    dve.wait_ge(carried.sem, carried.at(n, g + 1))
                nc.vector.tensor_tensor_scan(hst[:, i % 3, :], decay[:, i % 2, :], urep[:, i % RING, :],
                                             carry[:, g:g + 1] if hf else 0.0, ALU.mult, ALU.add).then_inc(scanned.sem, 1)

            def with_skip(n, k, par):
                h = k // CPH
                t = slice((k % CPH) * Q, (k % CPH + 1) * Q)
                r = slice(h * CB_, (h + 1) * CB_)
                dve.wait_ge(y1t_ps.sem, y1t_ps.at(n, k + 1))
                if k >= 2:
                    dve.wait_ge(o1_ps.sem, o1_ps.at(n, k - 1))
                nc.vector.scalar_tensor_tensor(y1ta[:, k % 2, :], xcm[par][:, PIECE[h], t], d1c[:, 0:1],
                                               bank[B_YT][:, 0:Q], ALU.mult, ALU.add)
                nc.vector.scalar_tensor_tensor(y1tb[r, k % 2, :], xcm[par][r, MID, t], d1c[r, 1:2],
                                               bank[B_YT][r, Q:2 * Q], ALU.mult, ALU.add).then_inc(y1t_made.sem, 1)

            def finish(n, k, par):
                dve.wait_ge(o1_ps.sem, o1_ps.at(n, k + 1))
                t = slice(k * Q, (k + 1) * Q)
                nc.vector.scalar_tensor_tensor(x1a[par][:, t], bank[B_OUT][:, 0:Q], boc[:, 0:1], x1a[par][:, t],
                                               ALU.add, ALU.add).then_inc(out_ready.sem, 1)
                nc.vector.scalar_tensor_tensor(x1b[par][:, t], bank[B_OUT][0:CB_, Q:2 * Q], boc[0:CB_, 1:2], x1b[par][:, t],
                                               ALU.add, ALU.add).then_inc(out_ready.sem, 1)

            def run(b, par, scan, end, first):
                step = Steps(dve, dve_steps, b + 1)
                mid_step = Steps(dve, dve_mid_steps, b)
                for s in range(SLOTS if scan or first else TAIL_AT + NCH + 1):
                    if first:
                        first_block_soon(b + 1, s, step, 1 - par, scan, end)
                    if s == 0:
                        if end:
                            scan_unit(b - 1, UNITS - 1, False)
                    elif scan:
                        scan_unit(b, s - 1, end)
                    if scan:
                        inputs(b, s, par)
                        if s == 3:
                            softplus_piece(b, 1, mid_step)
                    if end and 0 <= s - TAIL_AT < NCH:
                        with_skip(b - 1, s - TAIL_AT, 1 - par)
                    if end and 0 <= s - TAIL_AT - 1 < NCH:
                        finish(b - 1, s - TAIL_AT - 1, 1 - par)
                    if first:
                        first_block_later(b + 1, s, step, 1 - par, end)
                assert not first or step.done == DVE_STEPS, step.done

            passes(dve, run)

        @block.tensor
        def _(pe):
            pe.wait_ge(s_const, 2)
            pe.wait_ge(s_wload, 16 * NLOADS)
            for j, (src, n, kn, outs) in enumerate(jobs):
                if j >= 8:
                    pe.wait_ge(s_wev, copies[j - 8])
                nc.tensor.transpose(bank[j % 8][0:kn, 0:n], src, ident[0:n, 0:n]).then_inc(s_wps, 1)
            pe.wait_ge(s_prep, PREPS)
            pe.wait_ge(s_wev, copies[-1] + 2)

            def mm(out, lhsT, rhs, start, stop):
                return nc.tensor.matmul(out, lhsT, rhs, start=start, stop=stop, skip_group_check=True)

            def group_sum(out, stats):
                for m in range(2):
                    mm(out[:, m:m + 1], ga[:, m * P:(m + 1) * P], stats[0], True, False)
                    ins = mm(out[:, m:m + 1], gb[:, m * P:(m + 1) * P], stats[1], False, True)
                return ins

            def group_means(n, g):
                pe.wait_ge(stats_ready.sem, stats_ready.at(n, 2 * g + 2))
                group_sum(bank[3], (mv[:, 0, 0:1], mv[0:CB_, 1, 0:1])).then_inc(gmean_ps.sem, 1)

            def group_variances(n, g):
                pe.wait_ge(gdev_ready.sem, gdev_ready.at(n, g + 1))
                group_sum(bank[4], (gq[:, 0:1], gq[0:CB_, 1:2])).then_inc(gvar_ps.sem, 1)

            def fill(n, k):
                ps = bank[FILL_BANKS[k % 3]]
                if k == 0:
                    pe.wait_ge(xn_ready.sem, xn_ready.at(n, 2))
                if k >= 3:
                    pe.wait_ge(fill_copied.sem, fill_copied.at(n, k - 2))
                if k == 6:
                    for c in range(NCH):
                        t = slice(c * Q, (c + 1) * Q)
                        o = ps[:, c * NH:(c + 1) * NH]
                        mm(o, xna[:, t], wt0a[:, DI:ZD], True, False)
                        ins = mm(o, xnb[0:CB_, t], wt0b[:, DI:ZD], False, True)
                elif k in (4, 5):
                    w0 = ZD + DI
                    for h, (t0, w) in enumerate(((0, HALF), (HALF, HALF)) if k == 4 else ((HALF, W), (HALF - W, W))):
                        o = ps[64 * h:64 * (h + 1), 0:w]
                        mm(o, wt0a[:, w0:w0 + 2 * NS], xna[:, t0:t0 + w], True, False)
                        ins = mm(o, wt0b[:, w0:w0 + 2 * NS], xnb[0:CB_, t0:t0 + w], False, True)
                else:
                    m, h = FILL_TILES[k]
                    w0 = ZD + m * P
                    t = slice(h * HALF, (h + 1) * HALF)
                    mm(ps[:, :], wt0a[:, w0:w0 + P], xna[:, t], True, False)
                    ins = mm(ps[:, :], wt0b[:, w0:w0 + P], xnb[0:CB_, t], False, True)
                ins.then_inc(fill_ps.sem, 1)

            def rows(n, c, r):
                ps = bank[ROW_BANKS[r]]
                for k in range(HPB):
                    h = HPB * r + k
                    nc.tensor.matmul(ps[:, k * Q:(k + 1) * Q], bc(csum[:, 0, c, h:h + 1], [P, P]), ident[:, :],
                                     start=(k == 0), stop=False, is_transpose=True, skip_group_check=True)
                mm(ps[:, :].rearrange("p (h q) -> p h q", q=Q), identb[:, :],
                   bc(maskneg[:, :].unsqueeze(1), [P, HPB, Q]), False, True).then_inc(row_ps.sem, 1)

            def transposed_x(n, c):
                t = slice(c * Q, (c + 1) * Q)
                if c >= 2:
                    pe.wait_ge(y0_ready.sem, y0_ready.at(n, c - 1))
                for m in range(XM):
                    nc.tensor.transpose(bank[B_XY][:, m * P:(m + 1) * P], xs[m][:, t], ident[:, :])
                nc.tensor.transpose(bank[B_XY][:, DI:DI + NS], bs[:, t], ident[0:NS, 0:NS]).then_inc(xt_ps.sem, 1)

            def b_by_c(n, c):
                t = slice(c * Q, (c + 1) * Q)
                if c >= 1:
                    pe.wait_ge(cbt_copied.sem, cbt_copied.at(n, c))
                if c >= 3:
                    pe.wait_ge(yt_made.sem, yt_made.at(n, c - 2))
                mm(bank[B_CBT][:, 0:Q], bs[:, t], cs_[:, t], True, True).then_inc(cb_ps.sem, 1)

            def own_state(n, c):
                pe.wait_ge(xw_ready.sem, xw_ready.at(n, c + 1))
                if c >= 1:
                    pe.wait_ge(yint_ready.sem, yint_ready.at(n, c))
                mm(bank[B_STATE][0:NS, 0:DI], xtok[:, c % 2, DI:DI + NS], xw[:, c % 2, :], True, True).then_inc(state_ps.sem, 1)

            def from_state(n, c):
                pe.wait_ge(state_ready.sem, state_ready.at(n, c))
                mm(bank[B_STATE][:, 0:DI], cs_[:, c * Q:(c + 1) * Q], state[:, :], True, True).then_inc(inter_ps.sem, 1)

            def chunk_output(n, c):
                t = slice(c * Q, (c + 1) * Q)
                if c < NCH - 1:
                    pe.wait_ge(xt_copied.sem, xt_copied.at(n, c + 2))
                else:
                    pe.wait_ge(y0_ready.sem, y0_ready.at(n, c))
                for m in range(XM):
                    mm(bank[B_XY][:, m * P:(m + 1) * P], xs[m][:, t], diagd[:, m, :], m == 0, False)
                pe.wait_ge(att_ready.sem, att_ready.at(n, 2 * (c + 1)))
                for h in range(NH):
                    ins = mm(bank[B_XY][:, h * HD:(h + 1) * HD], att[:, c % 2, h, :],
                             xtok[:, c % 2, h * HD:(h + 1) * HD], False, h == NH - 1)
                ins.then_inc(y_ps.sem, 1)

            def transposed_y(n, c):
                pe.wait_ge(ynorm_ready.sem, ynorm_ready.at(n, c + 1))
                if c + 2 < NCH:
                    pe.wait_ge(cbt_copied.sem, cbt_copied.at(n, c + 3))
                else:
                    pe.wait_ge(yt_made.sem, yt_made.at(n, c))
                for m in range(XM):
                    ins = nc.tensor.transpose(bank[B_CBT][:, (m + 1) * Q:(m + 2) * Q],
                                              y0[:, c % 2, m * P:(m + 1) * P], ident[:, :])
                ins.then_inc(yt_ps.sem, 1)

            def gate(n, c):
                t = slice(c * Q, (c + 1) * Q)
                if c >= 1:
                    pe.wait_ge(gated.sem, gated.at(n, c))
                for m in range(XM):
                    o = bank[B_GATE][:, m * Q:(m + 1) * Q]
                    mm(o, wt0a[:, m * P:(m + 1) * P], xna[:, t], True, False)
                    ins = mm(o, wt0b[:, m * P:(m + 1) * P], xnb[0:CB_, t], False, True)
                ins.then_inc(z_ps.sem, 1)

            def projected(n, c):
                pe.wait_ge(gated.sem, gated.at(n, c + 1))
                if c >= 1:
                    pe.wait_ge(x1_ready.sem, x1_ready.at(n, 2 * c))
                for m, w in enumerate((P, CB_)):
                    for j in range(XM):
                        ins = mm(bank[B_OUT][0:w, m * Q:(m + 1) * Q], wo0[:, j, m * P:m * P + w], yzt[:, c % 2, j, :],
                                 j == 0, j == XM - 1)
                ins.then_inc(o0_ps.sem, 1)

            def first_block(n, s, again):
                if s == 1:
                    if again is not None:
                        pe.wait_ge(p1_copied.sem, p1_copied.at(n - 1, EARLY))
                    group_means(n, 0)
                if s == 2:
                    group_variances(n, 0)
                for k, at in enumerate(FILL_AT):
                    if s == at:
                        if k == 0 and again is not None:
                            pe.wait_ge(p1_copied.sem, p1_copied.at(n - 1, 10))
                        fill(n, k)
                if s == 11:
                    pe.wait_ge(da_ready.sem, da_ready.at(n, 1))
                    pe.wait_ge(fill_copied.sem, fill_copied.at(n, FILLS))
                    w = NCH * NH
                    mm(bank[B_CSUM][:, 0:w], upper[:, :], da0[:, :, :].rearrange("p c h -> p (c h)"), True, True)
                    mm(bank[B_CSUM][:, w:2 * w], ones[:, :], da0[:, :, :].rearrange("p c h -> p (c h)"), True, True).then_inc(cs_ps.sem, 1)
                c = chunk_at(s, 0)
                if c >= 0:
                    if c == 0:
                        pe.wait_ge(silu_done.sem, silu_done.at(n, XM + 4))
                        pe.wait_ge(csum_ready.sem, csum_ready.at(n, 1))
                    b_by_c(n, c)
                    if c >= 1:
                        pe.wait_ge(row_exp.sem, row_exp.at(n, NRB * c - 1))
                    rows(n, c, 0)
                for stage, job in ((2, own_state), (6, gate), (8, projected), (0, transposed_x)):
                    c = chunk_at(s, stage)
                    if c >= 0 and (stage != 2 or c < NCH - 1):
                        job(n, c)
                c = chunk_at(s, 1)
                if c >= 0:
                    if c >= 1:
                        from_state(n, c)
                    pe.wait_ge(row_exp.sem, row_exp.at(n, NRB * c + 1))
                    rows(n, c, 1)
                for stage, job in ((3, chunk_output), (5, transposed_y)):
                    if chunk_at(s, stage) >= 0:
                        job(n, chunk_at(s, stage))
                if c >= 0:
                    if c >= 1:
                        pe.wait_ge(row_exp.sem, row_exp.at(n, NRB * c))
                    rows(n, c, 2)
                if s == PRE_AT + 1:
                    group_means(n, 1)
                if s == PRE_AT + 2:
                    group_variances(n, 1)
                for k in range(EARLY):
                    if s == PRE_AT + P1_AT[k]:
                        if k == 0:
                            pe.wait_ge(xn_ready.sem, xn_ready.at(n, 4))
                        project(n, k)

            def project(n, k):
                what, h = P1_TILES[k]
                o = bank[P1_BANKS[k]]
                c0 = {"x": 0, "d": COL_D, "B": COL_B, "C": COL_C}[what[0]]
                if what[1:] == "B":
                    c0 += P
                    jobs1 = [(o[i * CB_:(i + 1) * CB_, :], CB_, i) for i in range(2)]
                else:
                    jobs1 = [(o[:, :], P, h)]
                for out, w, i in jobs1:
                    t = slice(i * HALF, (i + 1) * HALF)
                    mm(out, wt1a[:, c0:c0 + w], xna[:, t], True, False)
                    ins = mm(out, wt1b[:, c0:c0 + w], xnb[:, t], False, True)
                ins.then_inc(p1_ps.sem, 1)

            def second_half(n, s):
                if s == 0:
                    pe.wait_ge(p1_copied.sem, p1_copied.at(n, EARLY))
                    project(n, EARLY)
                    project(n, EARLY + 1)
                if s == 1:
                    project(n, EARLY + 2)
                if s == 2:
                    pe.wait_ge(p1_copied.sem, p1_copied.at(n, EARLY + 1))
                    project(n, EARLY + 3)

            def sum_states(n, i, prev):
                g = i % YG
                if g == 0:
                    q = i // YG
                    if q:
                        pe.wait_ge(y1_copied.sem, y1_copied.at(n, q))
                    elif prev:
                        pe.wait_ge(y1_copied.sem, y1_copied.at(n - 1, 2 * YQ))
                pe.wait_ge(hc_ready.sem, hc_ready.at(n, i + 1))
                for c in range(CPH):
                    o = c * YG * DG + g * DG
                    ins = mm(bank[B_YSUM][:, o:o + DG], hc[:, i % 2, c * Q:(c + 1) * Q], sel[:, :], True, True)
                ins.then_inc(y_sum_ps.sem, 1)

            def run(b, par, scan, end, first):
                for s in range(SLOTS if scan or first else TAIL_AT + NCH + 1):
                    if s < 3:
                        if end:
                            sum_states(b - 1, UNITS - 3 + s, False)
                    elif scan:
                        sum_states(b, s - 3, end)
                    if end:
                        k = s - TAIL_AT
                        if k == 0:
                            pe.wait_ge(y1_copied.sem, y1_copied.at(b - 1, 2 * YQ))
                        if 0 <= k < NCH:
                            h = k // CPH
                            if k >= 1:
                                pe.wait_ge(y1t_made.sem, y1t_made.at(b - 1, k))
                            nc.tensor.transpose(bank[B_YT][:, 0:P], y1[:, k, 0:P], ident[:, :])
                            mm(bank[B_YT][h * CB_:(h + 1) * CB_, Q:2 * Q], y1[:, k, P:C], ident[:, :], True, True).then_inc(y1t_ps.sem, 1)
                        if 1 <= k <= NCH:
                            h = (k - 1) // CPH
                            pe.wait_ge(y1t_made.sem, y1t_made.at(b - 1, k))
                            if k >= 2:
                                pe.wait_ge(out_ready.sem, out_ready.at(b - 1, 2 * (k - 1)))
                            for m, w in enumerate((P, CB_)):
                                o = bank[B_OUT][0:w, m * Q:(m + 1) * Q]
                                mm(o, wo1a[:, m * P:m * P + w], y1ta[:, (k - 1) % 2, :], True, False)
                                ins = mm(o, wo1b[h * CB_:(h + 1) * CB_, m * P:m * P + w],
                                         y1tb[h * CB_:(h + 1) * CB_, (k - 1) % 2, :], False, True)
                            ins.then_inc(o1_ps.sem, 1)
                    if scan:
                        second_half(b, s)
                    if first:
                        first_block(b + 1, s, end if scan else None)

            passes(pe, run)


EXP_LN = "natural_log_exp_and_others"
NLOADS = 54
PREPS = 6
DVE_STEPS = 71
ACT_STEPS = 2
DVE_MID_STEPS = 3
ACT_MID_STEPS = 1

FILL_TILES = {0: (0, 0), 1: (0, 1), 2: (1, 0), 3: (1, 1), 7: (2, 0), 8: (2, 1)}
SILU_AT = (13, 15)
TINY = 1.1754944e-38

_INS = [("x", (B, C, L)), ("L0_conv_in_proj_w", (PROJ0, C)), ("L0_conv_conv_w", (CONVD, 9)),
        ("L0_conv_conv_b", (CONVD,)), ("L0_conv_dt_bias", (NH,)), ("L0_conv_A_log", (NH,)),
        ("L0_conv_D", (NH,)), ("L0_conv_norm_w", (DI,)), ("L0_conv_norm_b", (DI,)),
        ("L0_conv_out_proj_w", (C, DI)), ("L1_conv_W_proj", (PROJ1, C)), ("L1_conv_b_proj", (PROJ1,)),
        ("L1_conv_A_log", (C, S1)), ("L1_conv_D", (C,)), ("L1_conv_dt_bias", (C,)),
        ("L1_conv_W_out", (C, C)), ("L1_conv_b_out", (C,))]


def kernel(**inputs):
    import numpy as _np
    import concourse.bacc as _bacc
    from concourse import mybir as _mybir
    from concourse.bass_utils import run_bass_kernel_spmd as _run

    nc = _bacc.Bacc("TRN2", target_bir_lowering=False, num_devices=1)
    arrays, args = {}, []
    for name, shape in _INS:
        a = _np.ascontiguousarray(inputs[name]).reshape(shape)
        arrays[f"in_{name}_dram"] = a
        args.append(nc.dram_tensor(f"in_{name}_dram", shape, _mybir.dt.from_np(a.dtype), kind="ExternalInput").ap())
    args.append(nc.dram_tensor("out_0_dram", (B, C, L), _mybir.dt.float32, kind="ExternalOutput").ap())
    scratch = nc.dram_tensor("scratch", (2, 2, C, L), _mybir.dt.float32, kind="Internal").ap()
    build(nc, scratch, *args)
    r = _run(nc, [arrays], core_ids=[0])
    return r.results[0]["out_0_dram"].reshape(B, C, H, W)
```

```python
from contextlib import ExitStack

import concourse.bass as bass
from concourse import mybir

ALU = mybir.AluOpType
ACT = mybir.ActivationFunctionType
F32 = mybir.dt.float32
BF16 = mybir.dt.bfloat16
AX_X = mybir.AxisListType.X

P = 128
B, C, H, W = 16, 192, 32, 32
L = H * W
Q = 128
NCH = L // Q
CB_ = C - P
GROUP = 6
GEPS = 1e-5
LEPS = 1e-5
DI = 384
NS = 32
NH = 12
HD = 32
XM = DI // P
CONVD = DI + 2 * NS
PROJ0 = 2 * DI + 2 * NS + NH
ZD = DI + NH
HPB = 4
NRB = NH // HPB
MASKED = -1e30
S1 = 16
PROJ1 = 2 * C + 2 * S1
DG = P // S1
NDG = C // DG
HALF = L // 2
CPH = HALF // Q
UNITS = 2 * NDG


SLOTS = UNITS
FILLS = 9
FILL_AT = (4, 4, 5, 5, 6, 6, 7, 8, 8)
CONV_AT = 6
TAPS = (6, 6, 6, 6, 6, 6, 5, 3, 4, 4, 4, 3, 4)
CONV_GROUPS = ((0, 0), (1, 0), (3, 0), (2, 0), (0, 1), (1, 1), (2, 1))
SSD_AT = 14
SSD_LAST = 9
PRE_AT = SSD_AT + 2 * (NCH - 1) + SSD_LAST
P1_AT = (4, 4, 5, 6, 8, 9, 10)
END_AT = (37, 10)
COL_DB, COL_D, COL_B, COL_C = C, 2 * P, 2 * C, 2 * C + P
WCOLS = 2 * C + 2 * P
PIECE = (0, 2)
MID = 1
P1_TILES = (("dA", 0), ("xA", 0), ("B", 0), ("C", 0), ("xdB", 0), ("xdB", 1), ("dA", 1), ("xA", 1), ("B", 1), ("C", 1))
K_XA, K_B, K_C, K_MID, K_D2, K_X2 = 2, 3, 4, 6, 7, 8
K_ALL = len(P1_TILES)
MID_STORE_AT, LAST_STORE_AT = 6, 8
RING, HRING, CRING, YQ = 4, 3, 3, 2
YG = NDG // YQ


class Signal:

    def __init__(self, sem, per_image):
        self.sem, self.per_image = sem, per_image

    def at(self, n, k):
        return n * self.per_image + k


class Steps:

    def __init__(self, eng, raised, n):
        self.eng, self.raised, self.n, self.done = eng, raised, n, 0

    def __call__(self, ins):
        self.done += 1
        ins.then_inc(self.raised.sem, 1)
        self.eng.wait_ge(self.raised.sem, self.raised.at(self.n, self.done))


def build(nc, scratch, x_d, inw_d, cw_d, cb_d, dtb_d, alog0_d, d0_d, nw_d, nb_d, outw_d,
          wp_d, bp_d, alog1_d, d1_d, dtb1_d, wo_d, bo_d, out_d):
    with ExitStack() as ctx:
        def sb(name, shape, dt=F32):
            return ctx.enter_context(nc.sbuf_tensor(name, shape, dt))

        def sem(name):
            return ctx.enter_context(nc.semaphore(name))

        def sig(name, per_image):
            return Signal(sem(name), per_image)

        bank = [ctx.enter_context(nc.psum_tensor(f"bank{i}", [P, 512], F32)) for i in range(8)]
        B_GATE, B_OUT, B_YSUM = 0, 1, 2
        B_XY, B_CBT, B_STATE = 3, 4, 5
        B_YT, B_LAST = (6, 0), (7, 1)
        FILL_BANKS = (3, 4, 5)
        B_CSUM = 3
        ROW_BANKS = (6, 6, 7)
        P1_BANKS = (3, 4, 5, 6, 7, 0, 5, 6, 7, 5)

        ident = sb("ident", [P, P])
        identb = sb("identb", [P, P], BF16)
        upper = sb("upper", [P, P])
        ones = sb("ones", [P, P])
        maskneg = sb("maskneg", [P, P], BF16)
        sel = sb("sel", [P, DG])
        ga = sb("ga", [P, 43 * GROUP])
        gb = sb("gb", [CB_, 43 * GROUP])
        neghalf = sb("neghalf", [P, 2])
        wt0a = sb("wt0a", [P, PROJ0])
        wt0b = sb("wt0b", [CB_, PROJ0])
        wo0 = sb("wo0", [P, XM, C])
        wt1a = sb("wt1a", [P, WCOLS])
        wt1b = sb("wt1b", [CB_ + 2, WCOLS])
        bbc = sb("bbc", [CB_ + 1, 2 * S1])
        wo1a = sb("wo1a", [P, C])
        wo1b = sb("wo1b", [P, C])
        wod1a = sb("wod1a", [P, C])
        wod1b = sb("wod1b", [P, C])
        cw = sb("cw", [P, XM + 1, 9])
        cb = sb("cb", [P, XM + 1])
        dtb = sb("dtb", [P, NH])
        aneg0 = sb("aneg0", [P, NH])
        dcol = sb("dcol", [P, XM])
        diagd = sb("diagd", [P, XM, P])
        nwc = sb("nwc", [P, XM])
        nbc = sb("nbc", [P, XM])
        aneg1 = sb("aneg1", [P, NDG])
        d1c = sb("d1c", [P, 2])
        boc = sb("boc", [P, 2])

        xa = sb("xa", [P, L])
        xb = sb("xb", [CB_, L])
        xna = sb("xna", [P, L])
        xnb = sb("xnb", [CB_ + 2, L])
        st = sb("st", [P, 2, 2, 6])
        mv = sb("mv", [P, 2, 2])
        spare = sb("spare", [P, 1])
        gm = sb("gm", [P, 2])
        gd = sb("gd", [P, 2])
        gq = sb("gq", [P, 2])
        gv = sb("gv", [P, 2])
        gr = sb("gr", [P, 2])
        cpad = [sb(f"cpad{m}", [P, H + 2, W + 2]) for m in range(XM)]
        bcpad = sb("bcpad", [P, H // 2 + 2, W + 2])
        xs = [sb(f"xs{m}", [P, L]) for m in range(XM)]
        bcacc = sb("bcacc", [P, HALF])
        bs = sb("bs", [NS, L])
        cs_ = sb("cs_", [NS, L])
        dtx = sb("dtx", [P, NCH, NH])
        dte = sb("dte", [P, NCH, NH])
        dtl = sb("dtl", [P, NCH, NH])
        dtu = sb("dtu", [P, NCH, NH])
        dt0 = sb("dt0", [P, NCH, NH])
        da0 = sb("da0", [P, NCH, NH])
        csum = sb("csum", [P, 2, NCH, NH])
        lndt = sb("lndt", [P, NCH, NH])
        ncs = sb("ncs", [P, NCH, NH])
        cexp = sb("cexp", [P, 2, NCH, NH])
        wend = sb("wend", [P, NCH, NH])
        xtok = sb("xtok", [P, 2, DI + NS])
        cbt = sb("cbt", [P, 2, Q])
        att = sb("att", [P, 2, NH, Q])
        xw = sb("xw", [P, 2, DI])
        state = sb("state", [NS, DI])
        yint = sb("yint", [P, 2, DI])
        y0 = sb("y0", [P, 2, DI])
        lst = sb("lst", [P, 2, 6])
        lmv = sb("lmv", [P, 2, 2])
        lve = sb("lve", [P, 2])
        lrs = sb("lrs", [P, 2])
        yzt = sb("yzt", [P, 2, XM, Q])
        x1a = [sb(f"x1a{p}", [P, L]) for p in range(2)]
        x1b = [sb(f"x1b{p}", [CB_, L]) for p in range(2)]
        xcm = [sb(f"xcm{p}", [P, 3, HALF]) for p in range(2)]
        brep = [sb(f"brep{p}", [P, L]) for p in range(2)]
        crep = [sb(f"crep{p}", [P, L]) for p in range(2)]
        delta = sb("delta", [P, 3, HALF])
        u1 = sb("u1", [P, 3, HALF])
        drep = sb("drep", [P, RING, HALF])
        urep = sb("urep", [P, RING, HALF])
        decay = sb("decay", [P, 2, HALF])
        hst = sb("hst", [P, HRING, HALF])
        carry = sb("carry", [P, NDG])
        hc = sb("hc", [P, CRING, HALF])
        y1 = sb("y1", [P, NCH, C])
        y1ta = xw[:, 0, 0:2 * Q].rearrange("p (k q) -> p k q", q=Q)
        y1tb = xw[:, 1, 0:2 * Q].rearrange("p (k q) -> p k q", q=Q)
        attv = att[:, :, :, :].rearrange("p a h q -> p (a h q)")
        sp_e = attv[:, 0:3 * HALF].rearrange("p (c d) -> p c d", d=HALF)
        sp_l = attv[:, 3 * HALF:6 * HALF].rearrange("p (c d) -> p c d", d=HALF)

        s_const = sem("constants_made")
        s_pool = sem("pool_constants")
        s_wload = sem("weights_loaded")
        s_wps = sem("weight_transposed")
        s_wev = sem("weight_copied")
        s_prep = sem("weights_prepared")
        x_loaded = sig("x_loaded", 32)
        stats_ready = sig("stats_ready", 4)
        gmean_ps = sig("gmean_ps", 2)
        gdev_ready = sig("gdev_ready", 2)
        gvar_ps = sig("gvar_ps", 2)
        gve_ready = sig("gve_ready", 2)
        grstd_ready = sig("grstd_ready", 2)
        xn_ready = sig("xn_ready", 4)
        fill_ps = sig("fill_ps", FILLS)
        fill_copied = sig("fill_copied", FILLS)
        conv_done = sig("conv_done", len(CONV_GROUPS))
        silu_done = sig("silu_done", 2 * XM + 4)
        dtx_ready = sig("dtx_ready", 1)
        dte_ready = sig("dte_ready", 1)
        dtl_ready = sig("dtl_ready", 1)
        da_ready = sig("da_ready", 1)
        cs_ps = sig("cs_ps", 1)
        csum_ready = sig("csum_ready", 1)
        lndt_ready = sig("lndt_ready", 1)
        ncs_ready = sig("ncs_ready", 1)
        cexp_ready = sig("cexp_ready", 1)
        wexp_ready = sig("wexp_ready", 1)
        wend_ready = sig("wend_ready", 1)
        xt_ps = sig("xt_ps", NCH)
        xt_copied = sig("xt_copied", NCH)
        cb_ps = sig("cb_ps", NCH)
        cbt_copied = sig("cbt_copied", NCH)
        row_ps = sig("row_ps", NCH * NRB)
        row_exp = sig("row_exp", NCH * NRB)
        att_ready = sig("att_ready", 2 * NCH)
        xw_ready = sig("xw_ready", NCH - 1)
        state_ps = sig("state_ps", NCH - 1)
        inter_ps = sig("inter_ps", NCH - 1)
        state_ready = sig("state_ready", NCH - 1)
        yint_ready = sig("yint_ready", NCH - 1)
        y_ps = sig("y_ps", NCH)
        y0_ready = sig("y0_ready", NCH)
        lve_ready = sig("lve_ready", NCH)
        lrs_ready = sig("lrs_ready", NCH)
        ynorm_ready = sig("ynorm_ready", NCH)
        yt_ps = sig("yt_ps", NCH)
        yt_made = sig("yt_made", NCH)
        z_ps = sig("z_ps", NCH)
        gated = sig("gated", NCH)
        o0_ps = sig("o0_ps", NCH)
        x1_ready = sig("x1_ready", 2 * NCH)
        p1_ps = sig("p1_ps", 10)
        p1_copied = sig("p1_copied", 10)
        spe_ready = sig("spe_ready", 3)
        spl_ready = sig("spl_ready", 3)
        delta_ready = sig("delta_ready", 3)
        u1_first = sig("u1_first", 1)
        u1_later = sig("u1_later", 2)
        kept_first = sig("kept_first", 16 * 2)
        kept_mid = sig("kept_mid", 16 * 4)
        kept_second = sig("kept_second", 16 * 2)
        delta_read = [sig(f"delta_read{k}", 16 * UNITS // RING) for k in range(RING)]
        u_read = [sig(f"u_read{k}", 16 * UNITS // RING) for k in range(RING)]
        w_made = sig("w_made", UNITS)
        decay_ready = sig("decay_ready", UNITS)
        scanned = sig("scanned", UNITS)
        carried = sig("carried", NDG)
        hc_ready = sig("hc_ready", UNITS)
        y_sum_ps = sig("y_sum_ps", UNITS)
        y1_copied = sig("y1_copied", 2 * YQ)
        y1t_ps = sig("y1t_ps", NCH)
        y1t_copied = sig("y1t_copied", NCH)
        x1_ps = sig("x1_ps", NCH)
        o1_ps = sig("o1_ps", NCH)
        out_ready = sig("out_ready", NCH)
        stored = sig("stored", 32)

        dve_steps = sig("dve_steps", DVE_STEPS)
        act_steps = sig("act_steps", ACT_STEPS)
        dve_mid_steps = sig("dve_mid_steps", DVE_MID_STEPS)
        act_mid_steps = sig("act_mid_steps", ACT_MID_STEPS)

        block = ctx.enter_context(nc.Block())

        def bc(ap, shape):
            return ap.to_broadcast(shape)

        def chunk_at(s, stage):
            c, odd = divmod(s - SSD_AT - stage, 2)
            return c if not odd and 0 <= c < NCH else -1

        def passes(eng, run):
            run(-1, 1, False, False, True)
            run(0, 0, True, False, True)
            with eng.Fori(0, (B - 2) // 2) as i:
                run(2 * i + 1, 1, True, True, True)
                run(2 * i + 2, 0, True, True, True)
            run(B - 1, 1, True, True, False)
            run(B, 0, False, True, False)

        nat0 = attv[:, 0:7 * C].rearrange("p (r c) -> p r c", c=C)
        nato = attv[:, 7 * C:11 * C].rearrange("p (r c) -> p r c", c=DI)
        natp = attv[:, 11 * C:15 * C].rearrange("p (r c) -> p r c", c=C)
        natw = y0[:, 0, :].rearrange("p (r c) -> p r c", c=C)
        jobs = []
        for r in range(7):
            n = min(P, PROJ0 - r * P)
            parts = [(0, n, r * P if r < 3 else ZD + (r - 3) * P)]
            if r == 6:
                parts = [(0, 2 * NS, ZD + DI), (2 * NS, NH, DI)]
            for c0, kn, dst in ((0, P, wt0a), (P, CB_, wt0b)):
                jobs.append((nat0[0:n, r, c0:c0 + kn], n, kn, [(dst[0:kn, d:d + w], s, w) for s, w, d in parts]))
        for r in range(2):
            n = P if r == 0 else CB_
            for m in range(XM):
                jobs.append((nato[0:n, r, m * P:(m + 1) * P], n, P, [(wo0[:, m, r * P:r * P + n], 0, n)]))
        for r in range(4):
            n = min(P, PROJ1 - r * P)
            for c0, kn, dst in ((0, P, wt1a), (P, CB_, wt1b)):
                outs = [(dst[0:kn, r * P:r * P + n], 0, n)]
                if r == 1:
                    outs = [(dst[0:kn, P:P + CB_], 0, CB_), (dst[0:kn, COL_D:COL_D + CB_], CB_, CB_)]
                if r == 2:
                    outs = [(dst[0:kn, COL_D + CB_:COL_D + P], 0, CB_), (dst[0:kn, COL_DB:COL_DB + CB_], CB_, CB_)]
                if r == 3:
                    outs = [(dst[0:kn, d:d + P].rearrange("p (n d) -> p n d", d=DG), s0, S1) for s0, d in ((0, COL_B), (S1, COL_C))]
                jobs.append((natp[0:n, r, c0:c0 + kn], n, kn, outs))
        for r in range(2):
            n = P if r == 0 else CB_
            for c0, kn, dst in ((0, P, wo1a), (P, CB_, wo1b)):
                outs = [(dst[k0:k0 + kn, r * P:r * P + n], 0, n) for k0 in ((0,) if kn == P else (0, CB_))]
                jobs.append((natw[0:n, r, c0:c0 + kn], n, kn, outs))
        copies = []
        total = 0
        for j in jobs:
            total += len(j[3])
            copies.append(total)

        @block.sync
        def _(sp):
            n = [0]

            def load(dst, src):
                sp.dma_start(dst, src, allow_slow_non_contiguous=True).then_inc(s_wload, 16)
                n[0] += 1

            def load_x(k):
                sp.dma_start(xa[:, :], x_d[k, 0:P, :]).then_inc(x_loaded.sem, 16)
                sp.dma_start(xb[:, :], x_d[k, P:C, :]).then_inc(x_loaded.sem, 16)

            load_x(0)
            load(nat0[:, 0:6, :], inw_d[0:6 * P, :].rearrange("(r p) c -> p r c", p=P))
            load(nat0[0:PROJ0 - 6 * P, 6, :], inw_d[6 * P:PROJ0, :])
            load(nato[:, 0, :], outw_d[0:P, :])
            load(nato[0:CB_, 1, :], outw_d[P:C, :])
            load(natp[:, 0:3, :], wp_d[0:3 * P, :].rearrange("(r p) c -> p r c", p=P))
            load(natp[0:PROJ1 - 3 * P, 3, :], wp_d[3 * P:PROJ1, :])
            load(natw[:, 0, :], wo_d[0:P, :])
            load(natw[0:CB_, 1, :], wo_d[P:C, :])
            load(cw[:, 0:XM, :], cw_d[0:DI, :].rearrange("(m p) t -> p m t", p=P))
            load(cb[:, 0:XM], cb_d[0:DI].rearrange("(m p) -> p m", p=P))
            for h in range(2):
                load(cw[h * 2 * NS:(h + 1) * 2 * NS, XM, :], cw_d[DI:CONVD, :])
                load(cb[h * 2 * NS:(h + 1) * 2 * NS, XM:XM + 1], cb_d[DI:CONVD].rearrange("(p a) -> p a", a=1))
            load(dtb[:, :], dtb_d.partition_broadcast(P))
            load(aneg0[:, :], alog0_d.partition_broadcast(P))
            for h in range(NH):
                load(dcol[(h % 4) * HD:(h % 4 + 1) * HD, h // 4:h // 4 + 1], d0_d[h:h + 1].partition_broadcast(HD))
            load(nwc[:, :], nw_d.rearrange("(m p) -> p m", p=P))
            load(nbc[:, :], nb_d.rearrange("(m p) -> p m", p=P))
            for s in range(S1):
                load(aneg1[s * DG:(s + 1) * DG, :], alog1_d.rearrange("(g d) n -> n d g", d=DG)[s, :, :])
            load(d1c[:, 0:1], d1_d[0:P].rearrange("(p a) -> p a", a=1))
            for h in range(2):
                load(d1c[h * CB_:(h + 1) * CB_, 1:2], d1_d[P:C].rearrange("(p a) -> p a", a=1))
            sp.wait_ge(s_const, 1)
            load(boc[:, 0:1], bo_d[0:P].rearrange("(p a) -> p a", a=1))
            load(boc[0:CB_, 1:2], bo_d[P:C].rearrange("(p a) -> p a", a=1))
            bp = bp_d.rearrange("(a n) -> a n", a=1)
            for d, s0, w in ((0, 0, C), (COL_D, C, P), (COL_DB, C + P, CB_)):
                load(wt1b[CB_:CB_ + 1, d:d + w], bp[:, s0:s0 + w])
            load(bbc[CB_:CB_ + 1, :], bp[:, 2 * C:2 * C + 2 * S1])
            for d, s0, w in ((COL_D, 0, P), (COL_DB, P, CB_)):
                load(wt1b[CB_ + 1:CB_ + 2, d:d + w], dtb1_d[s0:s0 + w].rearrange("(a n) -> a n", a=1))
            assert n[0] == NLOADS, n

            def keep(par, which, src, piece, done):
                if piece == MID:
                    for h in range(2):
                        sp.dma_start(scratch[par, which, P:C, h * HALF:(h + 1) * HALF],
                                     src[h * CB_:(h + 1) * CB_, MID, :]).then_inc(done.sem, 16)
                else:
                    h = piece // 2
                    sp.dma_start(scratch[par, which, 0:P, h * HALF:(h + 1) * HALF], src[:, piece, :]).then_inc(done.sem, 16)

            def read_repeated(b, i, par, prev):
                hf, g = i // NDG, i % NDG
                if i == 0:
                    sp.wait_ge(kept_first.sem, kept_first.at(b, 16 * 2))
                elif i >= RING or prev:
                    sp.wait_ge(scanned.sem, scanned.at(b, i - RING + 1))
                for which, (dst, read) in enumerate(((drep, delta_read), (urep, u_read))):
                    if which == 1 and i == P // DG - 1:
                        sp.wait_ge(kept_mid.sem, kept_mid.at(b, 16 * 4))
                    if which == 1 and i == NDG - 1:
                        sp.wait_ge(kept_second.sem, kept_second.at(b, 16 * 2))
                    src = scratch[par, which, g * DG:(g + 1) * DG, hf * HALF:(hf + 1) * HALF]
                    sp.dma_start(dst[:, i % RING, :], bc(src.unsqueeze(0), [S1, DG, HALF])).then_inc(read[i % RING].sem, 16)

            def traffic(b, par, scan, end, first, load_next):
                for s in range(SLOTS):
                    if end and s == END_AT[1] + CPH + RING + 1:
                        sp.wait_ge(out_ready.sem, out_ready.at(b - 1, NCH))
                        sp.dma_start(out_d[b - 1, 0:P, :], x1a[1 - par][:, :]).then_inc(stored.sem, 16)
                        sp.dma_start(out_d[b - 1, P:C, :], x1b[1 - par][:, :]).then_inc(stored.sem, 16)
                    if scan:
                        for at, piece, kept in ((MID_STORE_AT, MID, kept_mid), (LAST_STORE_AT, 2, kept_second)):
                            if s == at:
                                sp.wait_ge(delta_ready.sem, delta_ready.at(b, piece + 1))
                                keep(par, 0, delta, piece, kept)
                                sp.wait_ge(u1_later.sem, u1_later.at(b, piece))
                                keep(par, 1, u1, piece, kept)
                        read_repeated(b, s, par, end)
                    if load_next and s == PRE_AT + RING:
                        sp.wait_ge(x1_ready.sem, x1_ready.at(b + 1, 2 * NCH))
                        load_x(b + 2)
                if first:
                    sp.wait_ge(u1_first.sem, u1_first.at(b + 1, 1))
                    keep(1 - par, 1, u1, 0, kept_first)
                    if scan:
                        sp.wait_ge(scanned.sem, scanned.at(b, UNITS - RING + 1))
                    keep(1 - par, 0, delta, 0, kept_first)

            traffic(-1, 1, False, False, True, True)
            traffic(0, 0, True, False, True, True)
            with sp.Fori(0, (B - 4) // 2) as i:
                traffic(2 * i + 1, 1, True, True, True, True)
                traffic(2 * i + 2, 0, True, True, True, True)
            traffic(B - 3, 1, True, True, True, True)
            traffic(B - 2, 0, True, True, True, False)
            traffic(B - 1, 1, True, True, False, False)
            traffic(B, 0, False, True, False, False)
            sp.wait_ge(stored.sem, B * 32)

        @block.gpsimd
        def _(pool):
            done = [0]

            def made_before(ins):
                done[0] += 1
                ins.then_inc(s_pool, 1)
                pool.wait_ge(s_pool, done[0])

            made_before(nc.gpsimd.memset(wt1b[CB_:CB_ + 2, :], 0.0))
            nc.gpsimd.memset(boc[:, :], 0.0).then_inc(s_const, 1)
            pool.wait_ge(s_const, 1)
            made_before(nc.gpsimd.memset(xnb[CB_:CB_ + 2, :], 1.0))
            for t in (ident, identb, maskneg):
                made_before(nc.gpsimd.memset(t[:, :], 0.0))
            for t in (upper, ones, ga, gb):
                made_before(nc.gpsimd.memset(t[:, :], 1.0))
            made_before(nc.gpsimd.memset(neghalf[:, :], -0.5))
            made_before(nc.gpsimd.memset(mv[:, :, :], 0.0))
            for t in cpad + [bcpad]:
                made_before(nc.gpsimd.memset(t[:, :, :], 0.0))
            for t in (ident, identb):
                made_before(nc.gpsimd.affine_select(out=t[:, :], in_=t[:, :], compare_op=ALU.not_equal, fill=1.0,
                                                    base=0, pattern=[[-1, P]], channel_multiplier=1))
            made_before(nc.gpsimd.affine_select(out=upper[:, :], in_=upper[:, :], compare_op=ALU.is_ge, fill=0.0,
                                                base=0, pattern=[[1, P]], channel_multiplier=-1))
            made_before(nc.gpsimd.affine_select(out=maskneg[:, :], in_=maskneg[:, :], compare_op=ALU.is_ge,
                                                fill=MASKED, base=0, pattern=[[1, P]], channel_multiplier=-1))
            for t, off in ((ga, 0), (gb, P)):
                v = t[:, :].rearrange("p (q r) -> p q r", r=GROUP)
                made_before(nc.gpsimd.affine_select(out=v, in_=v, compare_op=ALU.is_ge, fill=0.0, base=off,
                                                    pattern=[[-GROUP, 43], [0, GROUP]], channel_multiplier=1))
                made_before(nc.gpsimd.affine_select(out=v, in_=v, compare_op=ALU.is_ge, fill=0.0,
                                                    base=GROUP - 1 - off,
                                                    pattern=[[GROUP, 43], [0, GROUP]], channel_multiplier=-1))
            nc.gpsimd.memset(carry[:, :], 0.0).then_inc(s_const, 1)
            pool.wait_ge(s_const, 2)
            pool.wait_ge(s_prep, PREPS)

            def group_rstd(n, g):
                pool.wait_ge(gve_ready.sem, gve_ready.at(n, g + 1))
                nc.gpsimd.tensor_tensor(gr[:, :], gv[:, :], neghalf[:, :], ALU.pow).then_inc(grstd_ready.sem, 1)

            def scaled_x(n, c):
                pool.wait_ge(xt_copied.sem, xt_copied.at(n, c + 1))
                if c == 0:
                    pool.wait_ge(wend_ready.sem, wend_ready.at(n, 1))
                if c >= 2:
                    pool.wait_ge(state_ps.sem, state_ps.at(n, c - 1))
                nc.gpsimd.tensor_tensor(xw[:, c % 2, :].rearrange("p (h d) -> p h d", d=HD),
                                        xtok[:, c % 2, 0:DI].rearrange("p (h d) -> p h d", d=HD),
                                        bc(wend[:, c, :].unsqueeze(2), [P, NH, HD]), ALU.mult).then_inc(xw_ready.sem, 1)

            def attention(n, c, h0, h1):
                pool.wait_ge(row_exp.sem, row_exp.at(n, NRB * c + h1 // HPB))
                pool.wait_ge(cbt_copied.sem, cbt_copied.at(n, c + 1))
                a = att[:, c % 2, h0:h1, :]
                nc.gpsimd.tensor_tensor(a, a, bc(cbt[:, c % 2, :].unsqueeze(1), [P, h1 - h0, Q]),
                                        ALU.mult).then_inc(att_ready.sem, 1)

            def layer_rstd(n, c):
                pool.wait_ge(lve_ready.sem, lve_ready.at(n, c + 1))
                nc.gpsimd.tensor_tensor(lrs[:, c % 2:c % 2 + 1], lve[:, c % 2:c % 2 + 1], neghalf[:, 0:1],
                                        ALU.pow).then_inc(lrs_ready.sem, 1)

            def first_block(n, s):
                if s == 3:
                    group_rstd(n, 0)
                c = chunk_at(s, 1)
                if c >= 0:
                    if c < NCH - 1:
                        scaled_x(n, c)
                    attention(n, c, 0, HPB)
                c = chunk_at(s, 2)
                if c >= 0:
                    attention(n, c, HPB, NH)
                c = chunk_at(s, 4)
                if c >= 0:
                    layer_rstd(n, c)
                if s == PRE_AT + 3:
                    group_rstd(n, 1)

            def second_half(n, s, par):
                for piece in (MID, 2):
                    if s == piece + 1:
                        pool.wait_ge(delta_ready.sem, delta_ready.at(n, piece + 1))
                        pool.wait_ge(p1_copied.sem, p1_copied.at(n, (K_MID, K_X2)[piece - 1]))
                        nc.gpsimd.tensor_tensor(u1[:, piece, :], delta[:, piece, :], xcm[par][:, piece, :], ALU.mult).then_inc(u1_later.sem, 1)

            def states_by_c(n, i, par, prev):
                hf = i // NDG
                pool.wait_ge(scanned.sem, scanned.at(n, i + 1))
                if i == 0:
                    pool.wait_ge(p1_copied.sem, p1_copied.at(n, K_C))
                if i == NDG:
                    pool.wait_ge(p1_copied.sem, p1_copied.at(n, 10))
                if i >= CRING or prev:
                    pool.wait_ge(y_sum_ps.sem, y_sum_ps.at(n, i - CRING + 1))
                nc.gpsimd.tensor_tensor(hc[:, i % CRING, :], hst[:, i % HRING, :], crep[par][:, hf * HALF:(hf + 1) * HALF],
                                        ALU.mult).then_inc(hc_ready.sem, 1)

            def run(b, par, scan, end, first):
                for s in range(SLOTS if scan or first else 2):
                    if s < 2:
                        if end:
                            states_by_c(b - 1, UNITS - 2 + s, 1 - par, False)
                    elif scan:
                        states_by_c(b, s - 2, par, end)
                    if scan:
                        second_half(b, s, par)
                    if first:
                        first_block(b + 1, s)

            passes(pool, run)

        @block.scalar
        def _(act):
            nc.scalar.preload_act_table_set(EXP_LN)
            for j, (_, n, kn, outs) in enumerate(jobs):
                act.wait_ge(s_wps, j + 1)
                for dst, s, w in outs:
                    src = bank[j % 8][0:kn, s:s + w]
                    if len(dst.shape) == 3:
                        src = bc(src.unsqueeze(2), [kn, w, DG])
                    nc.scalar.copy(dst, src).then_inc(s_wev, 1)
            act.wait_ge(s_wload, 16 * NLOADS)
            for s0, d in ((0, COL_B), (S1, COL_C)):
                nc.scalar.copy(wt1b[CB_:CB_ + 1, d:d + P].rearrange("p (n d) -> p n d", d=DG),
                               bc(bbc[CB_:CB_ + 1, s0:s0 + S1].unsqueeze(2), [1, S1, DG])).then_inc(s_wev, 1)
            nc.scalar.activation(aneg0[:, :], aneg0[:, :], ACT.Exp).then_inc(s_wev, 1)
            nc.scalar.activation(aneg1[:, :], aneg1[:, :], ACT.Exp).then_inc(s_wev, 1)
            act.wait_ge(s_prep, PREPS)

            def copy_fill(n, k):
                ps = bank[FILL_BANKS[k % 3]]
                act.wait_ge(fill_ps.sem, fill_ps.at(n, k + 1))
                if k == 6:
                    ins = nc.scalar.copy(dtx[:, :, :].rearrange("p c h -> p (c h)"), ps[:, 0:NCH * NH])
                elif k == 4:
                    ins = nc.scalar.copy(bcpad[:, 1:17, 1:W + 1], ps[:, :].rearrange("p (r w) -> p r w", w=W))
                elif k == 5:
                    nc.scalar.copy(bcpad[0:64, 17, 1:W + 1], ps[0:64, 0:W])
                    ins = nc.scalar.copy(bcpad[64:P, 0, 1:W + 1], ps[64:P, 0:W])
                else:
                    m, h = FILL_TILES[k]
                    ins = nc.scalar.copy(cpad[m][:, 1 + 16 * h:17 + 16 * h, 1:W + 1],
                                         ps[:, :].rearrange("p (r w) -> p r w", w=W))
                ins.then_inc(fill_copied.sem, 1)

            def exp_rows(n, c, r):
                act.wait_ge(row_ps.sem, row_ps.at(n, NRB * c + r + 1))
                if r == 0 and c == 0:
                    act.wait_ge(ncs_ready.sem, ncs_ready.at(n, 1))
                if r == 0 and c >= 2:
                    act.wait_ge(y_ps.sem, y_ps.at(n, c - 1))
                for k in range(HPB):
                    h = HPB * r + k
                    ins = nc.scalar.activation(att[:, c % 2, h, :], bank[ROW_BANKS[r]][:, k * Q:(k + 1) * Q], ACT.Exp,
                                               bias=ncs[:, c, h:h + 1])
                ins.then_inc(row_exp.sem, 1)

            def first_block(n, s, step, par, last, again):
                for k, at in enumerate(FILL_AT):
                    if s == at + 1:
                        copy_fill(n, k)
                if s == 10:
                    act.wait_ge(dtx_ready.sem, dtx_ready.at(n, 1))
                    step(nc.scalar.activation(dte[:, :, :], dtx[:, :, :], ACT.Abs))
                    nc.scalar.activation(dte[:, :, :], dte[:, :, :], ACT.Exp, scale=-1.0).then_inc(dte_ready.sem, 1)
                    act.wait_ge(dte_ready.sem, dte_ready.at(n, 1))
                    nc.scalar.activation(dtl[:, :, :], dte[:, :, :], ACT.Ln, bias=1.0).then_inc(dtl_ready.sem, 1)
                if s == 12:
                    act.wait_ge(csum_ready.sem, csum_ready.at(n, 1))
                    nc.scalar.activation(lndt[:, :, :], lndt[:, :, :], ACT.Ln).then_inc(lndt_ready.sem, 1)
                    nc.scalar.activation(cexp[:, :, :, :], csum[:, :, :, :], ACT.Exp).then_inc(cexp_ready.sem, 1)
                    nc.scalar.activation(wend[:, :, :], wend[:, :, :], ACT.Exp).then_inc(wexp_ready.sem, 1)
                c = chunk_at(s, 6)
                if c >= 0:
                    act.wait_ge(yt_ps.sem, yt_ps.at(n, c + 1))
                    if c >= 2:
                        act.wait_ge(o0_ps.sem, o0_ps.at(n, c - 1))
                    for m in range(XM):
                        ins = nc.scalar.activation(yzt[:, c % 2, m, :], bank[B_CBT][:, (m + 1) * Q:(m + 2) * Q],
                                                   ACT.Identity, bias=nbc[:, m:m + 1], scale=nwc[:, m:m + 1])
                    ins.then_inc(yt_made.sem, 1)
                c = chunk_at(s, 2)
                if c >= 0:
                    exp_rows(n, c, 1)
                    exp_rows(n, c, 2)
                c = chunk_at(s, 1)
                if c >= 0:
                    exp_rows(n, c, 0)
                    act.wait_ge(xt_ps.sem, xt_ps.at(n, c + 1))
                    if c >= 2:
                        act.wait_ge(xw_ready.sem, xw_ready.at(n, c - 1))
                        act.wait_ge(state_ps.sem, state_ps.at(n, c - 1))
                    nc.scalar.copy(xtok[:, c % 2, :], bank[B_XY][:, 0:DI + NS]).then_inc(xt_copied.sem, 1)
                    act.wait_ge(cb_ps.sem, cb_ps.at(n, c + 1))
                    if c >= 2:
                        act.wait_ge(att_ready.sem, att_ready.at(n, 2 * (c - 1)))
                    nc.scalar.copy(cbt[:, c % 2, :], bank[B_CBT][:, 0:Q]).then_inc(cbt_copied.sem, 1)
                for k in range(len(P1_AT) - 1):
                    if s == PRE_AT + P1_AT[k] + 1:
                        copy_projected(n, k, par, last, again)
                if s == PRE_AT + 5:
                    softplus_parts(n, 0, step)

            def silu(n, s):
                if s in SILU_AT:
                    half = SILU_AT.index(s)
                    act.wait_ge(conv_done.sem, conv_done.at(n, (4, 7)[half]))
                    for m in range(XM):
                        v = xs[m][:, half * HALF:(half + 1) * HALF]
                        nc.scalar.activation(v, v, ACT.Silu, bias=cb[:, m:m + 1]).then_inc(silu_done.sem, 1)
                    if half == 0:
                        for h in range(2):
                            for k, dst in enumerate((bs, cs_)):
                                r = 64 * h + NS * k
                                nc.scalar.activation(dst[:, h * HALF:(h + 1) * HALF], bcacc[r:r + NS, :], ACT.Silu,
                                                     bias=cb[r:r + NS, XM:XM + 1]).then_inc(silu_done.sem, 1)
                    nc.scalar.preload_act_table_set(EXP_LN)

            def copy_projected(n, k, par, last, again):
                act.wait_ge(p1_ps.sem, p1_ps.at(n, k + 1))
                if k == 0 and last:
                    act.wait_ge(kept_mid.sem, kept_mid.at(n - 1, 16 * 4))
                    act.wait_ge(kept_second.sem, kept_second.at(n - 1, 16 * 2))
                if k == 0 and again:
                    act.wait_ge(y1t_copied.sem, y1t_copied.at(n - 2, NCH))
                    act.wait_ge(hc_ready.sem, hc_ready.at(n - 2, UNITS))
                what, h = P1_TILES[k]
                ps = bank[P1_BANKS[k]]
                if what == "xdB":
                    rows_h = slice(h * CB_, (h + 1) * CB_)
                    nc.scalar.copy(xcm[par][rows_h, MID, :], ps[0:CB_, :])
                    nc.scalar.copy(delta[rows_h, MID, :], ps[CB_:P, :]).then_inc(p1_copied.sem, 1)
                else:
                    dst = {"dA": delta[:, PIECE[h], :], "xA": xcm[par][:, PIECE[h], :],
                           "B": brep[par][:, h * HALF:(h + 1) * HALF], "C": crep[par][:, h * HALF:(h + 1) * HALF]}[what]
                    nc.scalar.copy(dst, ps[:, :]).then_inc(p1_copied.sem, 1)

            def softplus_parts(n, h, step):
                cc = slice(h, h + 1)
                act.wait_ge(p1_copied.sem, p1_copied.at(n, (1, K_MID, K_D2)[h]))
                act.wait_ge(y_ps.sem, y_ps.at(n, NCH))
                step(nc.scalar.activation(sp_e[:, cc, :], delta[:, cc, :], ACT.Abs))
                nc.scalar.activation(sp_e[:, cc, :], sp_e[:, cc, :], ACT.Exp, scale=-1.0).then_inc(spe_ready.sem, 1)
                act.wait_ge(spe_ready.sem, spe_ready.at(n, h + 1))
                nc.scalar.activation(sp_l[:, cc, :], sp_e[:, cc, :], ACT.Ln, bias=1.0).then_inc(spl_ready.sem, 1)

            def second_half(n, s, par, step):
                if s == 0:
                    softplus_parts(n, MID, step)
                for k in range(K_MID, K_ALL):
                    if s == k - K_MID:
                        copy_projected(n, k, par, False, False)
                if s == 1:
                    softplus_parts(n, 2, step)

            def copy_y(n, q, prev):
                hf, k = q // YQ, q % YQ
                act.wait_ge(y_sum_ps.sem, y_sum_ps.at(n, YG * (q + 1)))
                if q == 0 and prev:
                    act.wait_ge(y1t_ps.sem, y1t_ps.at(n - 1, NCH))
                nc.scalar.copy(y1[:, CPH * hf:CPH * (hf + 1), k * YG * DG:(k + 1) * YG * DG],
                               bank[B_YSUM][:, 0:CPH * YG * DG].rearrange("p (c d) -> p c d", d=YG * DG)).then_inc(y1_copied.sem, 1)

            def finish(n, s, h, par):
                j = s - END_AT[h]
                r = slice(h * CB_, (h + 1) * CB_)
                if 0 <= j < CPH:
                    k = CPH * h + j
                    act.wait_ge(y1t_ps.sem, y1t_ps.at(n, k + 1))
                    if k >= 2:
                        act.wait_ge(o1_ps.sem, o1_ps.at(n, k - 1))
                    nc.scalar.copy(y1ta[:, k % 2, :], bank[B_YT[h]][:, 0:Q])
                    nc.scalar.copy(y1tb[r, k % 2, :], bank[B_YT[h]][r, Q:2 * Q]).then_inc(y1t_copied.sem, 1)
                if 1 <= j <= CPH:
                    k = CPH * h + j - 1
                    act.wait_ge(o1_ps.sem, o1_ps.at(n, k + 1))
                    t = slice(k * Q, (k + 1) * Q)
                    nc.scalar.activation(x1a[par][:, t], bank[B_LAST[h]][:, 0:Q], ACT.Identity, bias=boc[:, 0:1])
                    nc.scalar.activation(x1b[par][:, t], bank[B_LAST[h]][0:CB_, Q:2 * Q], ACT.Identity,
                                         bias=boc[0:CB_, 1:2]).then_inc(out_ready.sem, 1)

            def run(b, par, scan, end, first):
                step = Steps(act, act_steps, b + 1)
                mid_step = Steps(act, act_mid_steps, b)
                for s in range(SLOTS if scan or first else END_AT[1] + CPH + 1):
                    if scan:
                        read = delta_read[s % RING]
                        act.wait_ge(read.sem, read.at(b, 16 * (s // RING + 1)))
                        if s >= 2 or end:
                            act.wait_ge(scanned.sem, scanned.at(b, s - 1))
                        g = s % NDG
                        nc.scalar.activation(decay[:, s % 2, :], drep[:, s % RING, :], ACT.Exp,
                                             scale=aneg1[:, g:g + 1]).then_inc(decay_ready.sem, 1)
                    if scan:
                        second_half(b, s, par, mid_step)
                    if first:
                        first_block(b + 1, s, step, 1 - par, scan, end)
                    if scan:
                        if 2 <= s < NDG + 2:
                            act.wait_ge(scanned.sem, scanned.at(b, s - 1))
                            nc.scalar.copy(carry[:, s - 2:s - 1], hst[:, (s - 2) % HRING, HALF - 1:HALF]).then_inc(carried.sem, 1)
                        for q in range(2 * YQ - 1):
                            if s == YG * (q + 1) + 2:
                                copy_y(b, q, end)
                    if end:
                        if s == 2:
                            copy_y(b - 1, 2 * YQ - 1, False)
                        finish(b - 1, s, 1, 1 - par)
                    if scan:
                        finish(b, s, 0, par)
                    if first:
                        silu(b + 1, s)
                assert not first or step.done == ACT_STEPS, step.done

            passes(act, run)

        @block.vector
        def _(dve):
            dve.wait_ge(s_const, 2)
            nc.vector.tensor_reduce(sel[:, :], ident[:, :].rearrange("p (n d) -> p d n", d=DG), AX_X, ALU.add).then_inc(s_prep, 1)
            dve.wait_ge(s_wload, 16 * NLOADS)
            for m in range(XM):
                nc.vector.tensor_scalar(diagd[:, m, :], ident[:, :], dcol[:, m:m + 1], None, ALU.mult).then_inc(s_prep, 1)
            dve.wait_ge(s_wev, copies[-1] + 4)
            nc.vector.tensor_scalar(wod1a[:, :], wo1a[:, :], d1c[:, 0:1], None, ALU.mult).then_inc(s_prep, 1)
            nc.vector.tensor_scalar(wod1b[:, :], wo1b[:, :], d1c[:, 1:2], None, ALU.mult).then_inc(s_prep, 1)
            nc.vector.tensor_scalar(aneg0[:, :], aneg0[:, :], -1.0, None, ALU.mult).then_inc(s_prep, 1)
            nc.vector.tensor_scalar(aneg1[:, :], aneg1[:, :], -1.0, None, ALU.mult).then_inc(s_prep, 1)
            dve.wait_ge(s_prep, PREPS)

            def channel_stats(t, k, n, h):
                return nc.vector.bn_stats(st[0:n, k, h, :], t[:, h * HALF:(h + 1) * HALF])

            def channel_moments():
                nc.vector.memset(spare[:, :], 0.0)
                nc.vector.bn_aggr(mv[:, 0, :], st[:, 0, :, :].rearrange("p a s -> p (a s)")).then_inc(stats_ready.sem, 1)
                nc.vector.bn_aggr(mv[0:CB_, 1, :], st[0:CB_, 1, :, :].rearrange("p a s -> p (a s)")).then_inc(stats_ready.sem, 1)

            def group_deviation(n, g, step):
                dve.wait_ge(gmean_ps.sem, gmean_ps.at(n, g + 1))
                step(nc.vector.tensor_scalar(gm[:, :], bank[3][:, 0:2], 1.0 / GROUP, None, ALU.mult))
                step(nc.vector.tensor_tensor(gd[:, :], mv[:, :, 0], gm[:, :], ALU.subtract))
                step(nc.vector.tensor_tensor(gd[:, :], gd[:, :], gd[:, :], ALU.mult))
                nc.vector.tensor_tensor(gq[:, :], gd[:, :], mv[:, :, 1], ALU.add).then_inc(gdev_ready.sem, 1)

            def group_variance(n, g):
                dve.wait_ge(gvar_ps.sem, gvar_ps.at(n, g + 1))
                nc.vector.tensor_scalar(gv[:, :], bank[4][:, 0:2], 1.0 / GROUP, GEPS, ALU.mult, ALU.add).then_inc(gve_ready.sem, 1)

            def normalise_groups(n, g, ta, tb):
                dve.wait_ge(grstd_ready.sem, grstd_ready.at(n, g + 1))
                nc.vector.tensor_scalar(xna[:, :], ta, gm[:, 0:1], gr[:, 0:1], ALU.subtract, ALU.mult).then_inc(xn_ready.sem, 1)
                nc.vector.tensor_scalar(xnb[0:CB_, :], tb, gm[0:CB_, 1:2], gr[0:CB_, 1:2],
                                        ALU.subtract, ALU.mult).then_inc(xn_ready.sem, 1)

            def conv_tap(n, k, step):
                o, t = k // 9, k % 9
                m, h = CONV_GROUPS[o]
                if t == 0 and h == 0:
                    dve.wait_ge(fill_copied.sem, fill_copied.at(n, (2, 4, 9, 6)[m]))
                image, acc = (cpad[m], xs[m][:, h * HALF:(h + 1) * HALF]) if m < XM else (bcpad, bcacc[:, :])
                r0 = h * H // 2 + t // 3
                accv = acc.rearrange("p (r w) -> p r w", w=W)
                win = image[:, r0:r0 + H // 2, t % 3:t % 3 + W]
                if t == 0:
                    ins = nc.vector.tensor_scalar(accv, win, cw[:, m, 0:1], None, ALU.mult)
                else:
                    ins = nc.vector.scalar_tensor_tensor(accv, win, cw[:, m, t:t + 1], accv, ALU.mult, ALU.add)
                if t < 8:
                    step(ins)
                else:
                    ins.then_inc(conv_done.sem, 1)

            def softplus(v, e, l, u, out, step):
                step(nc.vector.tensor_scalar(u, e, 1.0, None, ALU.add))
                step(nc.vector.scalar_tensor_tensor(u, u, -1.0, e, ALU.add, ALU.subtract))
                step(nc.vector.tensor_tensor(u, l, u, ALU.subtract))
                return nc.vector.scalar_tensor_tensor(out, v, 0.0, u, ALU.max, ALU.add)

            def carry_state(n, c, step):
                sv = state[:, :].rearrange("p (h d) -> p h d", d=HD)
                dve.wait_ge(state_ps.sem, state_ps.at(n, c + 1))
                if c == 0:
                    nc.vector.tensor_copy(state[:, :], bank[B_STATE][0:NS, 0:DI]).then_inc(state_ready.sem, 1)
                    return
                step(nc.vector.tensor_tensor(sv, sv, bc(cexp[0:NS, 1, c, :].unsqueeze(2), [NS, NH, HD]), ALU.mult))
                nc.vector.tensor_tensor(state[:, :], state[:, :], bank[B_STATE][0:NS, 0:DI], ALU.add).then_inc(state_ready.sem, 1)

            def from_state(n, c):
                dve.wait_ge(inter_ps.sem, inter_ps.at(n, c))
                nc.vector.tensor_tensor(yint[:, c % 2, :].rearrange("p (h d) -> p h d", d=HD),
                                        bank[B_STATE][:, 0:DI].rearrange("p (h d) -> p h d", d=HD),
                                        bc(cexp[:, 0, c, :].unsqueeze(2), [P, NH, HD]), ALU.mult).then_inc(yint_ready.sem, 1)

            def chunk_output(n, c, step):
                dve.wait_ge(y_ps.sem, y_ps.at(n, c + 1))
                if c >= 2:
                    dve.wait_ge(yt_ps.sem, yt_ps.at(n, c - 1))
                if c == 0:
                    ins = nc.vector.tensor_copy(y0[:, 0, :], bank[B_XY][:, 0:DI])
                else:
                    dve.wait_ge(yint_ready.sem, yint_ready.at(n, c))
                    ins = nc.vector.tensor_tensor(y0[:, c % 2, :], yint[:, c % 2, :], bank[B_XY][:, 0:DI], ALU.add)
                ins.then_inc(y0_ready.sem, 1)
                dve.wait_ge(y0_ready.sem, y0_ready.at(n, c + 1))
                step(nc.vector.bn_stats(lst[:, c % 2, :], y0[:, c % 2, :]))
                nc.vector.memset(spare[:, :], 0.0)
                step(nc.vector.bn_aggr(lmv[:, c % 2, :], lst[:, c % 2, :]))
                nc.vector.tensor_scalar(lve[:, c % 2:c % 2 + 1], lmv[:, c % 2, 1:2], LEPS, None, ALU.add).then_inc(lve_ready.sem, 1)

            def normalise(n, c):
                dve.wait_ge(lrs_ready.sem, lrs_ready.at(n, c + 1))
                nc.vector.tensor_scalar(y0[:, c % 2, :], y0[:, c % 2, :], lmv[:, c % 2, 0:1], lrs[:, c % 2:c % 2 + 1],
                                        ALU.subtract, ALU.mult).then_inc(ynorm_ready.sem, 1)

            def gate(n, c):
                dve.wait_ge(yt_made.sem, yt_made.at(n, c + 1))
                dve.wait_ge(z_ps.sem, z_ps.at(n, c + 1))
                yz = yzt[:, c % 2, :, :].rearrange("p m q -> p (m q)")
                nc.vector.tensor_tensor(yz, yz, bank[B_GATE][:, 0:DI], ALU.mult).then_inc(gated.sem, 1)

            def residual(n, c, par):
                dve.wait_ge(o0_ps.sem, o0_ps.at(n, c + 1))
                t = slice(c * Q, (c + 1) * Q)
                nc.vector.tensor_tensor(x1a[par][:, t], bank[B_OUT][:, 0:Q], xa[:, t], ALU.add).then_inc(x1_ready.sem, 1)
                nc.vector.tensor_tensor(x1b[par][:, t], bank[B_OUT][0:CB_, Q:2 * Q], xb[:, t], ALU.add).then_inc(x1_ready.sem, 1)

            def first_block_soon(n, s, step, par, last, again):
                if s == 2:
                    group_deviation(n, 0, step)
                if s == 3:
                    group_variance(n, 0)
                if s == 4:
                    if last:
                        dve.wait_ge(p1_ps.sem, p1_ps.at(n - 1, 10))
                    normalise_groups(n, 0, xa[:, :], xb[:, :])
                if s == 9:
                    dve.wait_ge(fill_copied.sem, fill_copied.at(n, 7))
                    nc.vector.tensor_tensor(dtx[:, :, :], dtx[:, :, :], bc(dtb[:, :].unsqueeze(1), [P, NCH, NH]),
                                            ALU.add).then_inc(dtx_ready.sem, 1)
                if s == 11:
                    dve.wait_ge(dtl_ready.sem, dtl_ready.at(n, 1))
                    step(softplus(dtx[:, :, :], dte[:, :, :], dtl[:, :, :], dtu[:, :, :], dt0[:, :, :], step))
                    nc.vector.tensor_tensor(da0[:, :, :], dt0[:, :, :], bc(aneg0[:, :].unsqueeze(1), [P, NCH, NH]),
                                            ALU.mult).then_inc(da_ready.sem, 1)
                if s == 12:
                    step(nc.vector.tensor_scalar(lndt[:, :, :], dt0[:, :, :], TINY, None, ALU.max))
                    dve.wait_ge(cs_ps.sem, cs_ps.at(n, 1))
                    step(nc.vector.tensor_copy(csum[:, :, :, :].rearrange("p a c h -> p (a c h)"),
                                               bank[B_CSUM][:, 0:2 * NCH * NH]))
                    nc.vector.tensor_tensor(wend[:, :, :], csum[:, 1, :, :], csum[:, 0, :, :], ALU.subtract).then_inc(csum_ready.sem, 1)
                if s == 13:
                    dve.wait_ge(lndt_ready.sem, lndt_ready.at(n, 1))
                    nc.vector.tensor_tensor(ncs[:, :, :], lndt[:, :, :], csum[:, 0, :, :], ALU.subtract).then_inc(ncs_ready.sem, 1)
                    dve.wait_ge(wexp_ready.sem, wexp_ready.at(n, 1))
                    nc.vector.tensor_tensor(wend[:, :, :], wend[:, :, :], dt0[:, :, :], ALU.mult).then_inc(wend_ready.sem, 1)
                c = chunk_at(s, 9)
                if c >= 0:
                    if c == 0 and again:
                        dve.wait_ge(stored.sem, stored.at(n - 2, 32))
                    residual(n, c, par)
                c = chunk_at(s, 3)
                if 0 <= c < NCH - 1:
                    carry_state(n, c, step)
                c = chunk_at(s, 5)
                if c >= 0:
                    normalise(n, c)
                c = chunk_at(s, 7)
                if c >= 0:
                    gate(n, c)
                c = chunk_at(s, 2)
                if c >= 1:
                    from_state(n, c)
                c = chunk_at(s, 4)
                if c >= 0:
                    chunk_output(n, c, step)
                if s == PRE_AT + 2:
                    group_deviation(n, 1, step)
                if s == PRE_AT + 3:
                    group_variance(n, 1)
                if s == PRE_AT + 4:
                    normalise_groups(n, 1, x1a[par][:, :], x1b[par][:, :])

            def first_block_later(n, s, step, par, again):
                if s == 0:
                    dve.wait_ge(x_loaded.sem, x_loaded.at(n, 32))
                    for h in range(2):
                        channel_stats(xa, 0, P, h)
                        ins = channel_stats(xb, 1, CB_, h)
                    step(ins)
                    channel_moments()
                if 0 <= s - CONV_AT < len(TAPS):
                    for k in range(sum(TAPS[:s - CONV_AT]), sum(TAPS[:s - CONV_AT + 1])):
                        conv_tap(n, k, step)
                c = chunk_at(s, SSD_LAST)
                if c in (CPH - 1, NCH - 1):
                    h = c // CPH
                    dve.wait_ge(x1_ready.sem, x1_ready.at(n, 2 * (c + 1)))
                    channel_stats(x1a[par], 0, P, h)
                    ins = channel_stats(x1b[par], 1, CB_, h)
                    if h:
                        step(ins)
                        channel_moments()
                if s == PRE_AT + 6:
                    softplus_piece(n, 0, step)
                if s == PRE_AT + 7:
                    dve.wait_ge(delta_ready.sem, delta_ready.at(n, 1))
                    dve.wait_ge(p1_copied.sem, p1_copied.at(n, K_XA))
                    nc.vector.tensor_tensor(u1[:, 0, :], delta[:, 0, :], xcm[par][:, 0, :], ALU.mult).then_inc(u1_first.sem, 1)

            def softplus_piece(n, h, step):
                cc = slice(h, h + 1)
                dve.wait_ge(spl_ready.sem, spl_ready.at(n, h + 1))
                d = delta[:, cc, :]
                softplus(d, sp_e[:, cc, :], sp_l[:, cc, :], u1[:, cc, :], d, step).then_inc(delta_ready.sem, 1)

            def inputs(b, i, par):
                hf = i // NDG
                if i == 0:
                    dve.wait_ge(p1_copied.sem, p1_copied.at(b, K_B))
                if i == NDG:
                    dve.wait_ge(p1_copied.sem, p1_copied.at(b, 10))
                read = u_read[i % RING]
                dve.wait_ge(read.sem, read.at(b, 16 * (i // RING + 1)))
                w = urep[:, i % RING, :]
                nc.vector.tensor_tensor(w, w, brep[par][:, hf * HALF:(hf + 1) * HALF], ALU.mult).then_inc(w_made.sem, 1)

            def scan_unit(n, i, prev):
                hf, g = i // NDG, i % NDG
                dve.wait_ge(decay_ready.sem, decay_ready.at(n, i + 1))
                dve.wait_ge(w_made.sem, w_made.at(n, i + 1))
                if i >= HRING or prev:
                    dve.wait_ge(hc_ready.sem, hc_ready.at(n, i - HRING + 1))
                    if HRING <= i < NDG + HRING:
                        dve.wait_ge(carried.sem, carried.at(n, i - HRING + 1))
                if hf:
                    dve.wait_ge(carried.sem, carried.at(n, g + 1))
                nc.vector.tensor_tensor_scan(hst[:, i % HRING, :], decay[:, i % 2, :], urep[:, i % RING, :],
                                             carry[:, g:g + 1] if hf else 0.0, ALU.mult, ALU.add).then_inc(scanned.sem, 1)

            def run(b, par, scan, end, first):
                step = Steps(dve, dve_steps, b + 1)
                mid_step = Steps(dve, dve_mid_steps, b)
                for s in range(SLOTS if scan or first else END_AT[1] + CPH + 1):
                    if first:
                        first_block_soon(b + 1, s, step, 1 - par, scan, end)
                    if s == 0:
                        if end:
                            scan_unit(b - 1, UNITS - 1, False)
                    elif scan:
                        scan_unit(b, s - 1, end)
                    if scan:
                        inputs(b, s, par)
                        for piece in (MID, 2):
                            if s == piece:
                                softplus_piece(b, piece, mid_step)
                    if first:
                        first_block_later(b + 1, s, step, 1 - par, end)
                assert not first or step.done == DVE_STEPS, step.done

            passes(dve, run)

        @block.tensor
        def _(pe):
            pe.wait_ge(s_const, 2)
            pe.wait_ge(s_wload, 16 * NLOADS)
            for j, (src, n, kn, outs) in enumerate(jobs):
                if j >= 8:
                    pe.wait_ge(s_wev, copies[j - 8])
                nc.tensor.transpose(bank[j % 8][0:kn, 0:n], src, ident[0:n, 0:n]).then_inc(s_wps, 1)
            pe.wait_ge(s_prep, PREPS)
            pe.wait_ge(s_wev, copies[-1] + 2)

            def mm(out, lhsT, rhs, start, stop):
                return nc.tensor.matmul(out, lhsT, rhs, start=start, stop=stop, skip_group_check=True)

            def group_sum(out, stats):
                for m in range(2):
                    mm(out[:, m:m + 1], ga[:, m * P:(m + 1) * P], stats[0], True, False)
                    ins = mm(out[:, m:m + 1], gb[:, m * P:(m + 1) * P], stats[1], False, True)
                return ins

            def group_means(n, g):
                pe.wait_ge(stats_ready.sem, stats_ready.at(n, 2 * g + 2))
                group_sum(bank[3], (mv[:, 0, 0:1], mv[0:CB_, 1, 0:1])).then_inc(gmean_ps.sem, 1)

            def group_variances(n, g):
                pe.wait_ge(gdev_ready.sem, gdev_ready.at(n, g + 1))
                group_sum(bank[4], (gq[:, 0:1], gq[0:CB_, 1:2])).then_inc(gvar_ps.sem, 1)

            def fill(n, k):
                ps = bank[FILL_BANKS[k % 3]]
                if k == 0:
                    pe.wait_ge(xn_ready.sem, xn_ready.at(n, 2))
                if k >= 3:
                    pe.wait_ge(fill_copied.sem, fill_copied.at(n, k - 2))
                if k == 6:
                    for c in range(NCH):
                        t = slice(c * Q, (c + 1) * Q)
                        o = ps[:, c * NH:(c + 1) * NH]
                        mm(o, xna[:, t], wt0a[:, DI:ZD], True, False)
                        ins = mm(o, xnb[0:CB_, t], wt0b[:, DI:ZD], False, True)
                elif k in (4, 5):
                    w0 = ZD + DI
                    for h, (t0, w) in enumerate(((0, HALF), (HALF, HALF)) if k == 4 else ((HALF, W), (HALF - W, W))):
                        o = ps[64 * h:64 * (h + 1), 0:w]
                        mm(o, wt0a[:, w0:w0 + 2 * NS], xna[:, t0:t0 + w], True, False)
                        ins = mm(o, wt0b[:, w0:w0 + 2 * NS], xnb[0:CB_, t0:t0 + w], False, True)
                else:
                    m, h = FILL_TILES[k]
                    w0 = ZD + m * P
                    t = slice(h * HALF, (h + 1) * HALF)
                    mm(ps[:, :], wt0a[:, w0:w0 + P], xna[:, t], True, False)
                    ins = mm(ps[:, :], wt0b[:, w0:w0 + P], xnb[0:CB_, t], False, True)
                ins.then_inc(fill_ps.sem, 1)

            def rows(n, c, r):
                ps = bank[ROW_BANKS[r]]
                for k in range(HPB):
                    h = HPB * r + k
                    nc.tensor.matmul(ps[:, k * Q:(k + 1) * Q], bc(csum[:, 0, c, h:h + 1], [P, P]), ident[:, :],
                                     start=(k == 0), stop=False, is_transpose=True, skip_group_check=True)
                mm(ps[:, :].rearrange("p (h q) -> p h q", q=Q), identb[:, :],
                   bc(maskneg[:, :].unsqueeze(1), [P, HPB, Q]), False, True).then_inc(row_ps.sem, 1)

            def transposed_x(n, c):
                t = slice(c * Q, (c + 1) * Q)
                if c == CPH:
                    pe.wait_ge(silu_done.sem, silu_done.at(n, 2 * XM + 4))
                if c >= 2:
                    pe.wait_ge(y0_ready.sem, y0_ready.at(n, c - 1))
                for m in range(XM):
                    nc.tensor.transpose(bank[B_XY][:, m * P:(m + 1) * P], xs[m][:, t], ident[:, :])
                nc.tensor.transpose(bank[B_XY][:, DI:DI + NS], bs[:, t], ident[0:NS, 0:NS]).then_inc(xt_ps.sem, 1)

            def b_by_c(n, c):
                t = slice(c * Q, (c + 1) * Q)
                if c >= 1:
                    pe.wait_ge(cbt_copied.sem, cbt_copied.at(n, c))
                if c >= 3:
                    pe.wait_ge(yt_made.sem, yt_made.at(n, c - 2))
                mm(bank[B_CBT][:, 0:Q], bs[:, t], cs_[:, t], True, True).then_inc(cb_ps.sem, 1)

            def own_state(n, c):
                pe.wait_ge(xw_ready.sem, xw_ready.at(n, c + 1))
                if c >= 1:
                    pe.wait_ge(yint_ready.sem, yint_ready.at(n, c))
                mm(bank[B_STATE][0:NS, 0:DI], xtok[:, c % 2, DI:DI + NS], xw[:, c % 2, :], True, True).then_inc(state_ps.sem, 1)

            def from_state(n, c):
                pe.wait_ge(state_ready.sem, state_ready.at(n, c))
                mm(bank[B_STATE][:, 0:DI], cs_[:, c * Q:(c + 1) * Q], state[:, :], True, True).then_inc(inter_ps.sem, 1)

            def chunk_output(n, c):
                t = slice(c * Q, (c + 1) * Q)
                if c < NCH - 1:
                    pe.wait_ge(xt_copied.sem, xt_copied.at(n, c + 2))
                else:
                    pe.wait_ge(y0_ready.sem, y0_ready.at(n, c))
                for m in range(XM):
                    mm(bank[B_XY][:, m * P:(m + 1) * P], xs[m][:, t], diagd[:, m, :], m == 0, False)
                pe.wait_ge(att_ready.sem, att_ready.at(n, 2 * (c + 1)))
                for h in range(NH):
                    ins = mm(bank[B_XY][:, h * HD:(h + 1) * HD], att[:, c % 2, h, :],
                             xtok[:, c % 2, h * HD:(h + 1) * HD], False, h == NH - 1)
                ins.then_inc(y_ps.sem, 1)

            def transposed_y(n, c):
                pe.wait_ge(ynorm_ready.sem, ynorm_ready.at(n, c + 1))
                if c + 2 < NCH:
                    pe.wait_ge(cbt_copied.sem, cbt_copied.at(n, c + 3))
                else:
                    pe.wait_ge(yt_made.sem, yt_made.at(n, c))
                for m in range(XM):
                    ins = nc.tensor.transpose(bank[B_CBT][:, (m + 1) * Q:(m + 2) * Q],
                                              y0[:, c % 2, m * P:(m + 1) * P], ident[:, :])
                ins.then_inc(yt_ps.sem, 1)

            def gate(n, c):
                t = slice(c * Q, (c + 1) * Q)
                if c >= 1:
                    pe.wait_ge(gated.sem, gated.at(n, c))
                for m in range(XM):
                    o = bank[B_GATE][:, m * Q:(m + 1) * Q]
                    mm(o, wt0a[:, m * P:(m + 1) * P], xna[:, t], True, False)
                    ins = mm(o, wt0b[:, m * P:(m + 1) * P], xnb[0:CB_, t], False, True)
                ins.then_inc(z_ps.sem, 1)

            def projected(n, c):
                pe.wait_ge(gated.sem, gated.at(n, c + 1))
                if c >= 1:
                    pe.wait_ge(x1_ready.sem, x1_ready.at(n, 2 * c))
                for m, w in enumerate((P, CB_)):
                    for j in range(XM):
                        ins = mm(bank[B_OUT][0:w, m * Q:(m + 1) * Q], wo0[:, j, m * P:m * P + w], yzt[:, c % 2, j, :],
                                 j == 0, j == XM - 1)
                ins.then_inc(o0_ps.sem, 1)

            def first_block(n, s, again):
                if s == 1:
                    if again is not None:
                        pe.wait_ge(p1_copied.sem, p1_copied.at(n - 1, K_MID))
                    group_means(n, 0)
                if s == 2:
                    group_variances(n, 0)
                for k, at in enumerate(FILL_AT):
                    if s == at:
                        if k == 0 and again is not None:
                            pe.wait_ge(p1_copied.sem, p1_copied.at(n - 1, 10))
                        fill(n, k)
                if s == 11:
                    pe.wait_ge(da_ready.sem, da_ready.at(n, 1))
                    pe.wait_ge(fill_copied.sem, fill_copied.at(n, FILLS))
                    w = NCH * NH
                    mm(bank[B_CSUM][:, 0:w], upper[:, :], da0[:, :, :].rearrange("p c h -> p (c h)"), True, True)
                    mm(bank[B_CSUM][:, w:2 * w], ones[:, :], da0[:, :, :].rearrange("p c h -> p (c h)"), True, True).then_inc(cs_ps.sem, 1)
                c = chunk_at(s, 0)
                if c >= 0:
                    if c == 0:
                        pe.wait_ge(silu_done.sem, silu_done.at(n, XM + 4))
                        pe.wait_ge(csum_ready.sem, csum_ready.at(n, 1))
                    b_by_c(n, c)
                    if c >= 1:
                        pe.wait_ge(row_exp.sem, row_exp.at(n, NRB * c - 1))
                    rows(n, c, 0)
                for stage, job in ((2, own_state), (6, gate), (8, projected), (0, transposed_x)):
                    c = chunk_at(s, stage)
                    if c >= 0 and (stage != 2 or c < NCH - 1):
                        job(n, c)
                c = chunk_at(s, 1)
                if c >= 0:
                    if c >= 1:
                        from_state(n, c)
                    pe.wait_ge(row_exp.sem, row_exp.at(n, NRB * c + 1))
                    rows(n, c, 1)
                for stage, job in ((3, chunk_output), (5, transposed_y)):
                    if chunk_at(s, stage) >= 0:
                        job(n, chunk_at(s, stage))
                if c >= 0:
                    if c >= 1:
                        pe.wait_ge(row_exp.sem, row_exp.at(n, NRB * c))
                    rows(n, c, 2)
                if s == PRE_AT + 1:
                    group_means(n, 1)
                if s == PRE_AT + 2:
                    group_variances(n, 1)
                for k in range(len(P1_AT)):
                    if s == PRE_AT + P1_AT[k]:
                        if k == 0:
                            pe.wait_ge(xn_ready.sem, xn_ready.at(n, 4))
                        if k == K_MID:
                            pe.wait_ge(p1_copied.sem, p1_copied.at(n, K_B))
                        if k == 3 and again is not None:
                            pe.wait_ge(out_ready.sem, out_ready.at(n - 1, CPH))
                        project(n, k)

            def project(n, k):
                what, h = P1_TILES[k]
                o = bank[P1_BANKS[k]]
                c0 = {"xA": 0, "xdB": P, "dA": COL_D, "B": COL_B, "C": COL_C}[what]
                t = slice(h * HALF, (h + 1) * HALF)
                mm(o[:, :], wt1a[:, c0:c0 + P], xna[:, t], True, False)
                mm(o[:, :], wt1b[:, c0:c0 + P], xnb[:, t], False, True).then_inc(p1_ps.sem, 1)

            def second_half(n, s):
                if s == 0:
                    pe.wait_ge(p1_copied.sem, p1_copied.at(n, K_C))
                    project(n, K_D2)
                if s == 1:
                    pe.wait_ge(p1_copied.sem, p1_copied.at(n, K_MID))
                    project(n, K_X2)
                if s == 2:
                    pe.wait_ge(p1_copied.sem, p1_copied.at(n, K_D2))
                    project(n, K_X2 + 1)

            def sum_states(n, i, prev):
                g = i % YG
                if g == 0:
                    q = i // YG
                    if q:
                        pe.wait_ge(y1_copied.sem, y1_copied.at(n, q))
                    elif prev:
                        pe.wait_ge(y1_copied.sem, y1_copied.at(n - 1, 2 * YQ))
                pe.wait_ge(hc_ready.sem, hc_ready.at(n, i + 1))
                for c in range(CPH):
                    o = c * YG * DG + g * DG
                    ins = mm(bank[B_YSUM][:, o:o + DG], hc[:, i % CRING, c * Q:(c + 1) * Q], sel[:, :], True, True)
                ins.then_inc(y_sum_ps.sem, 1)

            def finish(n, s, h, par):
                j = s - END_AT[h]
                r = slice(h * CB_, (h + 1) * CB_)
                if 0 <= j < CPH:
                    k = CPH * h + j
                    if j == 0:
                        pe.wait_ge(y1_copied.sem, y1_copied.at(n, YQ * (h + 1)))
                    if k >= 1:
                        pe.wait_ge(y1t_copied.sem, y1t_copied.at(n, k))
                    nc.tensor.transpose(bank[B_YT[h]][:, 0:P], y1[:, k, 0:P], ident[:, :])
                    mm(bank[B_YT[h]][r, Q:2 * Q], y1[:, k, P:C], ident[:, :], True, True).then_inc(y1t_ps.sem, 1)
                if 1 <= j <= CPH:
                    k = CPH * h + j - 1
                    pe.wait_ge(y1t_copied.sem, y1t_copied.at(n, k + 1))
                    if k >= 1:
                        pe.wait_ge(out_ready.sem, out_ready.at(n, k))
                    t = slice((j - 1) * Q, j * Q)
                    tt = slice(k * Q, (k + 1) * Q)
                    tiles = [(bank[B_LAST[h]][0:w, m * Q:(m + 1) * Q], slice(m * P, m * P + w)) for m, w in enumerate((P, CB_))]
                    for (o, c), x1 in zip(tiles, (x1a, x1b)):
                        w = c.stop - c.start
                        ins = mm(o, ident[0:w, 0:w], x1[par][:, tt], w == P, False)
                    ins.then_inc(x1_ps.sem, 1)
                    for o, c in tiles:
                        mm(o, wod1a[:, c], xcm[par][:, PIECE[h], t], False, False)
                        mm(o, wo1a[:, c], y1ta[:, k % 2, :], False, False)
                    pe.wait_ge(x1_ps.sem, x1_ps.at(n, k + 1))
                    for o, c in tiles:
                        mm(o, wod1b[r, c], xcm[par][r, MID, t], False, False)
                        ins = mm(o, wo1b[r, c], y1tb[r, k % 2, :], False, True)
                    ins.then_inc(o1_ps.sem, 1)

            def run(b, par, scan, end, first):
                for s in range(SLOTS if scan or first else END_AT[1] + CPH + 1):
                    if s < 3:
                        if end:
                            sum_states(b - 1, UNITS - 3 + s, False)
                    elif scan:
                        sum_states(b, s - 3, end)
                    if end:
                        if scan and s == END_AT[1]:
                            pe.wait_ge(p1_copied.sem, p1_copied.at(b, 10))
                        finish(b - 1, s, 1, 1 - par)
                        if s == SSD_AT + 5:
                            pe.wait_ge(out_ready.sem, out_ready.at(b - 1, NCH))
                    if scan:
                        if first and s == END_AT[0]:
                            pe.wait_ge(row_exp.sem, row_exp.at(b + 1, NRB * NCH))
                        finish(b, s, 0, par)
                        second_half(b, s)
                    if first:
                        first_block(b + 1, s, end if scan else None)

            passes(pe, run)


EXP_LN = "natural_log_exp_and_others"
NLOADS = 57
PREPS = 8
DVE_STEPS = 95
ACT_STEPS = 2
DVE_MID_STEPS = 6
ACT_MID_STEPS = 2

FILL_TILES = {0: (0, 0), 1: (0, 1), 2: (1, 0), 3: (1, 1), 7: (2, 0), 8: (2, 1)}
SILU_AT = (12, 19)
TINY = 1.1754944e-38

_INS = [("x", (B, C, L)), ("L0_conv_in_proj_w", (PROJ0, C)), ("L0_conv_conv_w", (CONVD, 9)),
        ("L0_conv_conv_b", (CONVD,)), ("L0_conv_dt_bias", (NH,)), ("L0_conv_A_log", (NH,)),
        ("L0_conv_D", (NH,)), ("L0_conv_norm_w", (DI,)), ("L0_conv_norm_b", (DI,)),
        ("L0_conv_out_proj_w", (C, DI)), ("L1_conv_W_proj", (PROJ1, C)), ("L1_conv_b_proj", (PROJ1,)),
        ("L1_conv_A_log", (C, S1)), ("L1_conv_D", (C,)), ("L1_conv_dt_bias", (C,)),
        ("L1_conv_W_out", (C, C)), ("L1_conv_b_out", (C,))]


def kernel(**inputs):
    import numpy as _np
    import concourse.bacc as _bacc
    from concourse import mybir as _mybir
    from concourse.bass_utils import run_bass_kernel_spmd as _run

    nc = _bacc.Bacc("TRN2", target_bir_lowering=False, num_devices=1)
    arrays, args = {}, []
    for name, shape in _INS:
        a = _np.ascontiguousarray(inputs[name]).reshape(shape)
        arrays[f"in_{name}_dram"] = a
        args.append(nc.dram_tensor(f"in_{name}_dram", shape, _mybir.dt.from_np(a.dtype), kind="ExternalInput").ap())
    args.append(nc.dram_tensor("out_0_dram", (B, C, L), _mybir.dt.float32, kind="ExternalOutput").ap())
    scratch = nc.dram_tensor("scratch", (2, 2, C, L), _mybir.dt.float32, kind="Internal").ap()
    build(nc, scratch, *args)
    r = _run(nc, [arrays], core_ids=[0])
    return r.results[0]["out_0_dram"].reshape(B, C, H, W)
```
